# Optimizing a Trainium2 kernel written in Bass

```python
import numpy as np
import jax
import jax.numpy as jnp

def _softmax(x, axis=-1):
    return jax.nn.softmax(x, axis=axis)

def _gelu(x):
    return jax.nn.gelu(x, approximate=True)

def _silu(x):
    return jax.nn.silu(x)

def _sigmoid(x):
    return jax.nn.sigmoid(x)

def _layernorm(x, axis=-1, eps=1e-05):
    m = jnp.mean(x, axis=axis, keepdims=True)
    v = jnp.var(x, axis=axis, keepdims=True)
    return (x - m) / jnp.sqrt(v + eps)

def _scatter_add(tgt, idx, src, axis=0):
    return tgt.at[idx].add(src)

def _segment_sum(src, seg, n):
    return jax.ops.segment_sum(src, seg, n)
kernel_name = 'mk_xattn_ffn_d4_seqx_r8_9234ed'

def setup_inputs(seed: int=0):
    np.random.seed(seed)
    _w = jnp.asarray

    def _rec_inputs():
        import jax
        import jax.numpy as jnp
        _rk = jax.random.key(seed)
        x = -0.0003929 + 0.9999 * jax.random.normal(jax.random.fold_in(_rk, 1), (32, 56, 128), jnp.float32)
        _lenS = 56 - jax.random.randint(jax.random.fold_in(_rk, 7), (32,), 0, max(1, 56 // 4) + 1, jnp.int32)
        _lenS2 = 1500 - jax.random.randint(jax.random.fold_in(_rk, 8), (32,), 0, max(1, 1500 // 4) + 1, jnp.int32)
        _ctx_1024P = jax.random.normal(jax.random.fold_in(_rk, 11), (32, 16, 128), jnp.float32)
        _ctx_1024c = jax.random.dirichlet(jax.random.fold_in(_rk, 511), 0.3 * jnp.ones((16,), jnp.float32), (32, 1500))
        _ctx_1024t = jnp.einsum('bsk,bkd->bsd', _ctx_1024c, _ctx_1024P)
        _ctx_1024t = _ctx_1024t * jax.lax.rsqrt(jnp.mean(jnp.square(_ctx_1024t)) + 1e-12) * 0.953939
        ctx_1024 = 2.81802e-05 + 1.00001 * (_ctx_1024t + 0.3 * jax.random.normal(jax.random.fold_in(_rk, 611), (32, 1500, 128), jnp.float32))
        _validS = jnp.arange(56)[None, :] < _lenS[:, None]
        _validS2 = jnp.arange(1500)[None, :] < _lenS2[:, None]
        _causal = jnp.tril(jnp.ones((56, 56), dtype=bool))
        mask_BxS2_ik1 = jnp.where(jnp.broadcast_to(_validS2[:, :], (32, 1500)), 1, 0).astype(jnp.int32)
        return (x, ctx_1024, mask_BxS2_ik1)
    x, ctx_1024, mask_BxS2_ik1 = _rec_inputs()

    def _L0_xattn_setup():
        import jax, jax.numpy as jnp
        import numpy as np
        import math
        INPUT_SIZE = 128
        DK = INPUT_SIZE // 2
        key = jax.random.key(seed)
        ks = jax.random.split(key, 8)
        B, LQ, LK, D = (4, 512, 512, INPUT_SIZE)
        Q = jax.random.normal(ks[0], (B, LQ, D), dtype=jnp.float32)
        K = jax.random.normal(ks[1], (B, LK, D), dtype=jnp.float32)
        V = jax.random.normal(ks[2], (B, LK, D), dtype=jnp.float32)
        K_mask = jax.random.randint(ks[3], (B, LK), 0, 2, dtype=jnp.int32)
        lim = 1.0 / math.sqrt(D)
        Wq = jax.random.uniform(ks[4], (DK, D), minval=-lim, maxval=lim, dtype=jnp.float32)
        bq = jax.random.uniform(ks[5], (DK,), minval=-lim, maxval=lim, dtype=jnp.float32)
        Wk = jax.random.uniform(ks[6], (DK, D), minval=-lim, maxval=lim, dtype=jnp.float32)
        bk = jax.random.uniform(ks[7], (DK,), minval=-lim, maxval=lim, dtype=jnp.float32)
        return {'Q': Q, 'K': K, 'V': V, 'K_mask': K_mask, 'Wq': Wq, 'bq': bq, 'Wk': Wk, 'bk': bk}
    _L0_xattn_all = _L0_xattn_setup()
    _L0_xattn_in = {k: v for k, v in _L0_xattn_all.items() if k in ('Wq', 'bq', 'Wk', 'bk')}
    del _L0_xattn_all

    def _L0_ffn_setup():
        import jax, jax.numpy as jnp
        import numpy as np
        TOP_K = 2
        NUM_EXPERTS = 8
        DIM = 128
        HIDDEN = 352
        BS, SLEN = (2, 128)

        def _grouped_ffn(x, w1, w2, w3, counts):
            num_experts = w1.shape[0]
            ends = jnp.cumsum(counts)
            starts = ends - counts
            t = jnp.arange(x.shape[0])
            out = jnp.zeros((x.shape[0], w2.shape[-1]), x.dtype)
            for e in range(num_experts):
                m = ((t >= starts[e]) & (t < ends[e])).astype(x.dtype)[:, None]
                xe = x * m
                h = jax.nn.silu(xe @ w1[e]) * (xe @ w3[e])
                out = out + h @ w2[e] * m
            return out
        key = jax.random.key(seed)
        k = jax.random.split(key, 5)
        std = 0.02
        return {'x': jax.random.normal(k[0], (BS, SLEN, DIM), jnp.float32), 'gate_w': jax.random.normal(k[1], (NUM_EXPERTS, DIM), jnp.float32) * std, 'expert_bias': jnp.zeros((NUM_EXPERTS,), jnp.float32), 'w1': jax.random.normal(k[2], (NUM_EXPERTS, DIM, HIDDEN), jnp.float32) * std, 'w2': jax.random.normal(k[3], (NUM_EXPERTS, HIDDEN, DIM), jnp.float32) * std, 'w3': jax.random.normal(k[4], (NUM_EXPERTS, DIM, HIDDEN), jnp.float32) * std}
    _L0_ffn_all = _L0_ffn_setup()
    _L0_ffn_in = {k: v for k, v in _L0_ffn_all.items() if k in ('gate_w', 'expert_bias', 'w1', 'w2', 'w3')}
    del _L0_ffn_all

    def _L1_xattn_setup():
        import jax, jax.numpy as jnp
        import numpy as np
        import math
        D_MODEL = 128
        N_HEADS = 16
        D_HEAD = D_MODEL // N_HEADS
        key = jax.random.key(seed)
        ks = jax.random.split(key, 11)
        N, L, S = (2, 256, 256)
        inp = {'queries': jax.random.normal(ks[0], (N, L, D_MODEL), dtype=jnp.float32), 'keys': jax.random.normal(ks[1], (N, S, D_MODEL), dtype=jnp.float32), 'values': jax.random.normal(ks[2], (N, S, D_MODEL), dtype=jnp.float32), 'Wq': jax.random.normal(ks[3], (D_MODEL, N_HEADS * D_HEAD), dtype=jnp.float32) / math.sqrt(D_MODEL), 'bq': jnp.zeros((N_HEADS * D_HEAD,), dtype=jnp.float32), 'Wk': jax.random.normal(ks[4], (D_MODEL, N_HEADS * D_HEAD), dtype=jnp.float32) / math.sqrt(D_MODEL), 'bk': jnp.zeros((N_HEADS * D_HEAD,), dtype=jnp.float32), 'Wv': jax.random.normal(ks[5], (D_MODEL, N_HEADS * D_HEAD), dtype=jnp.float32) / math.sqrt(D_MODEL), 'bv': jnp.zeros((N_HEADS * D_HEAD,), dtype=jnp.float32), 'Wo': jax.random.normal(ks[6], (N_HEADS * D_HEAD, D_MODEL), dtype=jnp.float32) / math.sqrt(N_HEADS * D_HEAD), 'bo': jnp.zeros((D_MODEL,), dtype=jnp.float32)}
        return inp
    _L1_xattn_all = _L1_xattn_setup()
    _L1_xattn_in = {k: v for k, v in _L1_xattn_all.items() if k in ('Wq', 'bq', 'Wk', 'bk', 'Wv', 'bv', 'Wo', 'bo')}
    del _L1_xattn_all

    def _L1_ffn_setup():
        import jax, jax.numpy as jnp
        import numpy as np
        from jax import lax
        B, S, D = (4, 256, 128)
        E = 8
        K = 2
        F = 408
        NORM_TOPK = True
        key = jax.random.key(seed)
        ks = jax.random.split(key, 8)
        sd = 0.02
        return {'x': jax.random.normal(ks[0], (B, S, D), jnp.float32), 'gate_w': jax.random.normal(ks[1], (E, D), jnp.float32) * sd, 'gate_b': jnp.zeros((E,), jnp.float32), 'up_w': jax.random.normal(ks[2], (E, F, D), jnp.float32) * sd, 'up_b': jnp.zeros((E, F), jnp.float32), 'gp_w': jax.random.normal(ks[3], (E, F, D), jnp.float32) * sd, 'gp_b': jnp.zeros((E, F), jnp.float32), 'down_w': jax.random.normal(ks[4], (E, D, F), jnp.float32) * sd, 'down_b': jnp.zeros((E, D), jnp.float32)}
    _L1_ffn_all = _L1_ffn_setup()
    _L1_ffn_in = {k: v for k, v in _L1_ffn_all.items() if k in ('gate_w', 'gate_b', 'up_w', 'up_b', 'gp_w', 'gp_b', 'down_w', 'down_b')}
    del _L1_ffn_all

    def _L2_xattn_setup():
        import jax, jax.numpy as jnp
        import numpy as np
        DIM = 128
        NUM_HEADS = 16
        DIM_HEAD = 64
        INNER = NUM_HEADS * DIM_HEAD
        SCALE = DIM_HEAD ** (-0.5)

        def _layernorm(x, gamma, beta, eps=1e-05):
            mu = jnp.mean(x, axis=-1, keepdims=True)
            var = jnp.mean(jnp.square(x - mu), axis=-1, keepdims=True)
            return (x - mu) * jax.lax.rsqrt(var + eps) * gamma + beta
        key = jax.random.key(seed)
        ks = jax.random.split(key, 8)
        B, SQ, SK = (2, 256, 512)
        x = jax.random.normal(ks[0], (B, SQ, DIM), dtype=jnp.float32)
        context = jax.random.normal(ks[1], (B, SK, DIM), dtype=jnp.float32)
        ln_gamma = jnp.ones((DIM,), jnp.float32)
        ln_beta = jnp.zeros((DIM,), jnp.float32)
        w_q = jax.random.normal(ks[2], (DIM, INNER), dtype=jnp.float32) / np.sqrt(DIM)
        w_kv = jax.random.normal(ks[3], (DIM, 2 * INNER), dtype=jnp.float32) / np.sqrt(DIM)
        w_out = jax.random.normal(ks[4], (INNER, DIM), dtype=jnp.float32) / np.sqrt(INNER)
        b_out = jnp.zeros((DIM,), jnp.float32)
        gate = jnp.array([0.5], jnp.float32)
        return {'x': x, 'context': context, 'ln_gamma': ln_gamma, 'ln_beta': ln_beta, 'w_q': w_q, 'w_kv': w_kv, 'w_out': w_out, 'b_out': b_out, 'gate': gate}
    _L2_xattn_all = _L2_xattn_setup()
    _L2_xattn_in = {k: v for k, v in _L2_xattn_all.items() if k in ('ln_gamma', 'ln_beta', 'w_q', 'w_kv', 'w_out', 'b_out', 'gate')}
    del _L2_xattn_all

    def _L2_ffn_setup():
        import jax, jax.numpy as jnp
        import numpy as np
        DIM = 128
        HIDDEN = 384
        SCALE = 1.0 / 127.0

        def _dequant(w_int, dtype):
            return w_int.astype(dtype) * jnp.asarray(SCALE, dtype)
        key = jax.random.key(seed)
        k_x, k_g, k_u, k_d = jax.random.split(key, 4)
        x = jax.random.normal(k_x, (4, 256, DIM), dtype=jnp.float32)
        w_gate = jax.random.randint(k_g, (HIDDEN, DIM), -127, 128, dtype=jnp.int32)
        w_up = jax.random.randint(k_u, (HIDDEN, DIM), -127, 128, dtype=jnp.int32)
        w_down = jax.random.randint(k_d, (DIM, HIDDEN), -127, 128, dtype=jnp.int32)
        return {'x': x, 'w_gate': w_gate, 'w_up': w_up, 'w_down': w_down}
    _L2_ffn_all = _L2_ffn_setup()
    _L2_ffn_in = {k: v for k, v in _L2_ffn_all.items() if k in ('w_gate', 'w_up', 'w_down')}
    del _L2_ffn_all

    def _L3_xattn_setup():
        import jax, jax.numpy as jnp
        import numpy as np
        D_MODEL = 128
        NUM_HEADS = 16
        HEAD_DIM = D_MODEL // NUM_HEADS
        B, T = (4, 256)
        key = jax.random.key(seed)
        ks = jax.random.split(key, 11)
        s = 0.02
        return {'q': jax.random.normal(ks[0], (B, T, D_MODEL), jnp.float32), 'k': jax.random.normal(ks[1], (B, T, D_MODEL), jnp.float32), 'v': jax.random.normal(ks[2], (B, T, D_MODEL), jnp.float32), 'Wq': jax.random.normal(ks[3], (D_MODEL, D_MODEL), jnp.float32) * s, 'bq': jnp.zeros((D_MODEL,), jnp.float32), 'Wk': jax.random.normal(ks[4], (D_MODEL, D_MODEL), jnp.float32) * s, 'bk': jnp.zeros((D_MODEL,), jnp.float32), 'Wv': jax.random.normal(ks[5], (D_MODEL, D_MODEL), jnp.float32) * s, 'bv': jnp.zeros((D_MODEL,), jnp.float32), 'Wo': jax.random.normal(ks[6], (D_MODEL, D_MODEL), jnp.float32) * s, 'bo': jnp.zeros((D_MODEL,), jnp.float32)}
    _L3_xattn_all = _L3_xattn_setup()
    _L3_xattn_in = {k: v for k, v in _L3_xattn_all.items() if k in ('Wq', 'bq', 'Wk', 'bk', 'Wv', 'bv', 'Wo', 'bo')}
    del _L3_xattn_all

    def _L3_ffn_setup():
        import jax, jax.numpy as jnp
        import numpy as np
        TOP_K = 2
        key = jax.random.key(seed)
        k1, k2, k3, k4 = jax.random.split(key, 4)
        B, S, H, I, E = (2, 256, 128, 512, 8)
        return {'hidden_states': jax.random.normal(k1, (B, S, H), jnp.float32), 'gate_w': jax.random.normal(k2, (E, H), jnp.float32) * 0.02, 'gate_up_proj': jax.random.normal(k3, (E, 2 * I, H), jnp.float32) * 0.02, 'down_proj': jax.random.normal(k4, (E, H, I), jnp.float32) * 0.02}
    _L3_ffn_all = _L3_ffn_setup()
    _L3_ffn_in = {k: v for k, v in _L3_ffn_all.items() if k in ('gate_w', 'gate_up_proj', 'down_proj')}
    del _L3_ffn_all
    return {'x': x, 'ctx_1024': ctx_1024, 'mask_BxS2_ik1': mask_BxS2_ik1, 'L0_xattn_Wq': _L0_xattn_in['Wq'], 'L0_xattn_bq': _L0_xattn_in['bq'], 'L0_xattn_Wk': _L0_xattn_in['Wk'], 'L0_xattn_bk': _L0_xattn_in['bk'], 'L0_ffn_gate_w': _L0_ffn_in['gate_w'], 'L0_ffn_expert_bias': _L0_ffn_in['expert_bias'], 'L0_ffn_w1': _L0_ffn_in['w1'], 'L0_ffn_w2': _L0_ffn_in['w2'], 'L0_ffn_w3': _L0_ffn_in['w3'], 'L1_xattn_Wq': _L1_xattn_in['Wq'], 'L1_xattn_bq': _L1_xattn_in['bq'], 'L1_xattn_Wk': _L1_xattn_in['Wk'], 'L1_xattn_bk': _L1_xattn_in['bk'], 'L1_xattn_Wv': _L1_xattn_in['Wv'], 'L1_xattn_bv': _L1_xattn_in['bv'], 'L1_xattn_Wo': _L1_xattn_in['Wo'], 'L1_xattn_bo': _L1_xattn_in['bo'], 'L1_ffn_gate_w': _L1_ffn_in['gate_w'], 'L1_ffn_gate_b': _L1_ffn_in['gate_b'], 'L1_ffn_up_w': _L1_ffn_in['up_w'], 'L1_ffn_up_b': _L1_ffn_in['up_b'], 'L1_ffn_gp_w': _L1_ffn_in['gp_w'], 'L1_ffn_gp_b': _L1_ffn_in['gp_b'], 'L1_ffn_down_w': _L1_ffn_in['down_w'], 'L1_ffn_down_b': _L1_ffn_in['down_b'], 'L2_xattn_ln_gamma': _L2_xattn_in['ln_gamma'], 'L2_xattn_ln_beta': _L2_xattn_in['ln_beta'], 'L2_xattn_w_q': _L2_xattn_in['w_q'], 'L2_xattn_w_kv': _L2_xattn_in['w_kv'], 'L2_xattn_w_out': _L2_xattn_in['w_out'], 'L2_xattn_b_out': _L2_xattn_in['b_out'], 'L2_xattn_gate': _L2_xattn_in['gate'], 'L2_ffn_w_gate': _L2_ffn_in['w_gate'], 'L2_ffn_w_up': _L2_ffn_in['w_up'], 'L2_ffn_w_down': _L2_ffn_in['w_down'], 'L3_xattn_Wq': _L3_xattn_in['Wq'], 'L3_xattn_bq': _L3_xattn_in['bq'], 'L3_xattn_Wk': _L3_xattn_in['Wk'], 'L3_xattn_bk': _L3_xattn_in['bk'], 'L3_xattn_Wv': _L3_xattn_in['Wv'], 'L3_xattn_bv': _L3_xattn_in['bv'], 'L3_xattn_Wo': _L3_xattn_in['Wo'], 'L3_xattn_bo': _L3_xattn_in['bo'], 'L3_ffn_gate_w': _L3_ffn_in['gate_w'], 'L3_ffn_gate_up_proj': _L3_ffn_in['gate_up_proj'], 'L3_ffn_down_proj': _L3_ffn_in['down_proj']}

def reference(x, ctx_1024, mask_BxS2_ik1, L0_xattn_Wq, L0_xattn_bq, L0_xattn_Wk, L0_xattn_bk, L0_ffn_gate_w, L0_ffn_expert_bias, L0_ffn_w1, L0_ffn_w2, L0_ffn_w3, L1_xattn_Wq, L1_xattn_bq, L1_xattn_Wk, L1_xattn_bk, L1_xattn_Wv, L1_xattn_bv, L1_xattn_Wo, L1_xattn_bo, L1_ffn_gate_w, L1_ffn_gate_b, L1_ffn_up_w, L1_ffn_up_b, L1_ffn_gp_w, L1_ffn_gp_b, L1_ffn_down_w, L1_ffn_down_b, L2_xattn_ln_gamma, L2_xattn_ln_beta, L2_xattn_w_q, L2_xattn_w_kv, L2_xattn_w_out, L2_xattn_b_out, L2_xattn_gate, L2_ffn_w_gate, L2_ffn_w_up, L2_ffn_w_down, L3_xattn_Wq, L3_xattn_bq, L3_xattn_Wk, L3_xattn_bk, L3_xattn_Wv, L3_xattn_bv, L3_xattn_Wo, L3_xattn_bo, L3_ffn_gate_w, L3_ffn_gate_up_proj, L3_ffn_down_proj):
    import jax
    import jax.numpy as jnp

    def _L0_xattn_ref(Q, K, V, K_mask, Wq, bq, Wk, bk):
        import jax, jax.numpy as jnp
        import numpy as np
        import math
        INPUT_SIZE = 128
        DK = INPUT_SIZE // 2
        Qp = jnp.einsum('bqd,ed->bqe', Q, Wq) + bq
        Kp = jnp.einsum('bkd,ed->bke', K, Wk) + bk
        scores = jnp.einsum('bqe,bke->bqk', Qp, Kp) / math.sqrt(INPUT_SIZE)
        scores = jnp.where((K_mask == 1)[:, None, :], -jnp.inf, scores)
        alpha = jax.nn.sigmoid(scores)
        matched_seq = jnp.einsum('bqk,bkv->bqv', alpha, V)
        return matched_seq

    def _L0_ffn_ref(x, gate_w, expert_bias, w1, w2, w3):
        import jax, jax.numpy as jnp
        import numpy as np
        TOP_K = 2
        NUM_EXPERTS = 8
        DIM = 128
        HIDDEN = 352
        BS, SLEN = (2, 128)

        def _grouped_ffn(x, w1, w2, w3, counts):
            num_experts = w1.shape[0]
            ends = jnp.cumsum(counts)
            starts = ends - counts
            t = jnp.arange(x.shape[0])
            out = jnp.zeros((x.shape[0], w2.shape[-1]), x.dtype)
            for e in range(num_experts):
                m = ((t >= starts[e]) & (t < ends[e])).astype(x.dtype)[:, None]
                xe = x * m
                h = jax.nn.silu(xe @ w1[e]) * (xe @ w3[e])
                out = out + h @ w2[e] * m
            return out
        bs, slen, dim = x.shape
        num_experts = gate_w.shape[0]
        xf = x.reshape(bs * slen, dim)
        scores = jax.nn.softmax((xf @ gate_w.T).astype(jnp.float32), axis=-1)
        _, sel = jax.lax.top_k(scores + expert_bias, TOP_K)
        top_scores = jnp.take_along_axis(scores, sel, axis=1).reshape(-1)
        sel_flat = sel.reshape(-1)
        counts = jnp.zeros((num_experts,), jnp.int32).at[sel_flat].add(1)
        order = jnp.argsort(sel_flat, stable=True)
        top_scores_sorted = top_scores[order]
        token_idx = order // TOP_K
        routed = xf[token_idx] * top_scores_sorted[:, None].astype(xf.dtype)
        routed_out = _grouped_ffn(routed, w1, w2, w3, counts)
        out = jnp.zeros_like(xf).at[token_idx].add(routed_out)
        return out.reshape(bs, slen, dim)

    def _L1_xattn_ref(queries, keys, values, Wq, bq, Wk, bk, Wv, bv, Wo, bo):
        import jax, jax.numpy as jnp
        import numpy as np
        import math
        D_MODEL = 128
        N_HEADS = 16
        D_HEAD = D_MODEL // N_HEADS
        N, L, _ = queries.shape
        S = keys.shape[1]
        H, D = (N_HEADS, D_HEAD)
        q = (queries @ Wq + bq).reshape(N, L, H, D)
        k = (keys @ Wk + bk).reshape(N, S, H, D)
        v = (values @ Wv + bv).reshape(N, S, H, D)
        sm = jnp.einsum('nlhd,nshd->nlhs', q, k) / math.sqrt(D)
        sm = jax.nn.softmax(sm, axis=1)
        attn = jnp.einsum('nlhs,nshd->nlhd', sm, v).reshape(N, L, H * D)
        return attn @ Wo + bo

    def _L1_ffn_ref(x, gate_w, gate_b, up_w, up_b, gp_w, gp_b, down_w, down_b):
        import jax, jax.numpy as jnp
        import numpy as np
        from jax import lax
        B, S, D = (4, 256, 128)
        E = 8
        K = 2
        F = 408
        NORM_TOPK = True
        bs, slen, dim = x.shape
        xf = x.reshape(-1, dim)
        N = xf.shape[0]
        scores = jax.nn.softmax(xf @ gate_w.T + gate_b, axis=-1)
        top_w, top_idx = lax.top_k(scores, K)
        if NORM_TOPK:
            top_w = top_w / (top_w.sum(-1, keepdims=True) + 1e-20)
        comb = jnp.zeros((N, E), xf.dtype).at[jnp.arange(N)[:, None], top_idx].add(top_w)

        def step(acc, p):
            uw, ub, gw, gb, dw, db, w = p
            h = jax.nn.silu((xf @ gw.T + gb) * (xf @ uw.T + ub))
            return (acc + w[:, None] * (h @ dw.T + db), None)
        y0 = jnp.zeros_like(xf)
        y, _ = lax.scan(step, y0, (up_w, up_b, gp_w, gp_b, down_w, down_b, comb.T))
        return y.reshape(bs, slen, dim)

    def _L2_xattn_ref(x, context, ln_gamma, ln_beta, w_q, w_kv, w_out, b_out, gate):
        import jax, jax.numpy as jnp
        import numpy as np
        DIM = 128
        NUM_HEADS = 16
        DIM_HEAD = 64
        INNER = NUM_HEADS * DIM_HEAD
        SCALE = DIM_HEAD ** (-0.5)

        def _layernorm(x, gamma, beta, eps=1e-05):
            mu = jnp.mean(x, axis=-1, keepdims=True)
            var = jnp.mean(jnp.square(x - mu), axis=-1, keepdims=True)
            return (x - mu) * jax.lax.rsqrt(var + eps) * gamma + beta
        B, SQ, _ = x.shape
        SK = context.shape[1]
        xn = _layernorm(x, ln_gamma, ln_beta)
        q = (xn @ w_q).reshape(B, SQ, NUM_HEADS, DIM_HEAD)
        kv = context @ w_kv
        k, v = jnp.split(kv, 2, axis=-1)
        k = k.reshape(B, SK, NUM_HEADS, DIM_HEAD)
        v = v.reshape(B, SK, NUM_HEADS, DIM_HEAD)
        scores = jnp.einsum('bqhd,bkhd->bhqk', q * SCALE, k)
        attn = jax.nn.softmax(scores, axis=-1)
        out = jnp.einsum('bhqk,bkhd->bqhd', attn, v).reshape(B, SQ, INNER)
        out = out @ w_out + b_out
        return out * jnp.tanh(gate[0])

    def _L2_ffn_ref(x, w_gate, w_up, w_down):
        import jax, jax.numpy as jnp
        import numpy as np
        DIM = 128
        HIDDEN = 384
        SCALE = 1.0 / 127.0

        def _dequant(w_int, dtype):
            return w_int.astype(dtype) * jnp.asarray(SCALE, dtype)
        wg = _dequant(w_gate, x.dtype)
        wu = _dequant(w_up, x.dtype)
        wd = _dequant(w_down, x.dtype)
        gate = jnp.einsum('bsd,hd->bsh', x, wg)
        up = jnp.einsum('bsd,hd->bsh', x, wu)
        h = jax.nn.silu(gate) * up
        return jnp.einsum('bsh,dh->bsd', h, wd)

    def _L3_xattn_ref(q, k, v, Wq, bq, Wk, bk, Wv, bv, Wo, bo):
        import jax, jax.numpy as jnp
        import numpy as np
        D_MODEL = 128
        NUM_HEADS = 16
        HEAD_DIM = D_MODEL // NUM_HEADS
        B, T = (4, 256)
        Bq, Tq, _ = q.shape
        Tk = k.shape[1]
        qh = (q @ Wq + bq).reshape(Bq, Tq, NUM_HEADS, HEAD_DIM).transpose(0, 2, 1, 3)
        kh = (k @ Wk + bk).reshape(Bq, Tk, NUM_HEADS, HEAD_DIM).transpose(0, 2, 1, 3)
        vh = (v @ Wv + bv).reshape(Bq, Tk, NUM_HEADS, HEAD_DIM).transpose(0, 2, 1, 3)
        scale = 1.0 / jnp.sqrt(jnp.asarray(HEAD_DIM, qh.dtype))
        scores = jnp.einsum('bhqd,bhkd->bhqk', qh, kh) * scale
        attn = jax.nn.softmax(scores, axis=-1)
        out = jnp.einsum('bhqk,bhkd->bhqd', attn, vh)
        out = out.transpose(0, 2, 1, 3).reshape(Bq, Tq, D_MODEL)
        return out @ Wo + bo

    def _L3_ffn_ref(hidden_states, gate_w, gate_up_proj, down_proj):
        import jax, jax.numpy as jnp
        import numpy as np
        TOP_K = 2
        B, S, H = hidden_states.shape
        E = gate_w.shape[0]
        x = hidden_states.reshape(-1, H)
        T = x.shape[0]
        probs = jax.nn.softmax(x @ gate_w.T, axis=-1)
        w, idx = jax.lax.top_k(probs, TOP_K)
        w = w / jnp.sum(w, axis=-1, keepdims=True)
        combine = jnp.zeros((T, E), x.dtype).at[jnp.arange(T)[:, None], idx].add(w)

        def step(acc, inputs):
            gup, dn, ce = inputs
            g, u = jnp.split(x @ gup.T, 2, axis=-1)
            acc = acc + ce[:, None] * (jax.nn.silu(g) * u @ dn.T)
            return (acc, None)
        out, _ = jax.lax.scan(step, jnp.zeros_like(x), (gate_up_proj, down_proj, combine.T))
        return out.reshape(B, S, H)
    x = x + _L0_xattn_ref(_layernorm(x, axis=-1), ctx_1024, ctx_1024, mask_BxS2_ik1, L0_xattn_Wq, L0_xattn_bq, L0_xattn_Wk, L0_xattn_bk)
    x = x + _L0_ffn_ref(_layernorm(x, axis=-1), L0_ffn_gate_w, L0_ffn_expert_bias, L0_ffn_w1, L0_ffn_w2, L0_ffn_w3)
    x = x + _L1_xattn_ref(_layernorm(x, axis=-1), ctx_1024, ctx_1024, L1_xattn_Wq, L1_xattn_bq, L1_xattn_Wk, L1_xattn_bk, L1_xattn_Wv, L1_xattn_bv, L1_xattn_Wo, L1_xattn_bo)
    x = x + _L1_ffn_ref(_layernorm(x, axis=-1), L1_ffn_gate_w, L1_ffn_gate_b, L1_ffn_up_w, L1_ffn_up_b, L1_ffn_gp_w, L1_ffn_gp_b, L1_ffn_down_w, L1_ffn_down_b)
    x = x + _L2_xattn_ref(_layernorm(x, axis=-1), ctx_1024, L2_xattn_ln_gamma, L2_xattn_ln_beta, L2_xattn_w_q, L2_xattn_w_kv, L2_xattn_w_out, L2_xattn_b_out, L2_xattn_gate)
    x = x + _L2_ffn_ref(_layernorm(x, axis=-1), L2_ffn_w_gate, L2_ffn_w_up, L2_ffn_w_down)
    x = x + _L3_xattn_ref(_layernorm(x, axis=-1), ctx_1024, ctx_1024, L3_xattn_Wq, L3_xattn_bq, L3_xattn_Wk, L3_xattn_bk, L3_xattn_Wv, L3_xattn_bv, L3_xattn_Wo, L3_xattn_bo)
    x = x + _L3_ffn_ref(_layernorm(x, axis=-1), L3_ffn_gate_w, L3_ffn_gate_up_proj, L3_ffn_down_proj)
    return x

_drawn_inputs = setup_inputs


def setup_inputs(seed=0):
    import zlib

    import numpy as np

    out = dict(_drawn_inputs(seed))
    spreads = {'L0_ffn_expert_bias': (0.0, 0.8),
     'L1_xattn_bq': (0.0, 2.0),
     'L1_xattn_bk': (0.0, 0.8),
     'L1_xattn_bv': (0.0, 0.1),
     'L1_xattn_bo': (0.0, 0.8),
     'L1_ffn_gate_b': (0.0, 0.8),
     'L1_ffn_up_b': (0.0, 0.8),
     'L1_ffn_gp_b': (0.0, 0.8),
     'L1_ffn_down_b': (0.0, 0.8),
     'L2_xattn_ln_gamma': (1.0, 0.6),
     'L2_xattn_ln_beta': (0.0, 0.8),
     'L2_xattn_b_out': (0.0, 2.0),
     'L3_xattn_bq': (0.0, 2.0),
     'L3_xattn_bk': (0.0, 0.8),
     'L3_xattn_bv': (0.0, 2.0),
     'L3_xattn_bo': (0.0, 2.0)}
    factors = {'L0_xattn_bq': 8.0,
     'L0_xattn_bk': 8.0,
     'L0_ffn_gate_w': 8.0,
     'L0_ffn_w1': 8.0,
     'L0_ffn_w2': 8.0,
     'L0_ffn_w3': 8.0,
     'L1_ffn_gate_w': 8.0,
     'L1_ffn_up_w': 8.0,
     'L1_ffn_gp_w': 8.0,
     'L1_ffn_down_w': 8.0,
     'L2_xattn_w_q': 8.0,
     'L2_xattn_w_kv': 5.924,
     'L2_xattn_w_out': 5.599,
     'L3_xattn_Wq': 62.028,
     'L3_xattn_Wk': 61.113,
     'L3_xattn_Wv': 51.348,
     'L3_xattn_Wo': 47.175,
     'L3_ffn_gate_w': 29.27,
     'L3_ffn_gate_up_proj': 26.018,
     'L3_ffn_down_proj': 25.837}
    for name, (base, spread) in spreads.items():
        noise = np.random.default_rng([zlib.crc32(name.encode()), seed]).standard_normal(out[name].shape)
        drawn = base * np.exp(spread * noise) if base else spread * noise
        out[name] = jnp.asarray(drawn.astype(out[name].dtype))
    for name, factor in factors.items():
        out[name] = (out[name] * factor).astype(out[name].dtype)
    return out
```

```python
from contextlib import ExitStack, contextmanager

import concourse.bass as bass
from concourse import mybir

F32 = mybir.dt.float32
I32 = mybir.dt.int32
U32 = mybir.dt.uint32
ALU = mybir.AluOpType
ACT = mybir.ActivationFunctionType
AX = mybir.AxisListType

D = 128
B, LQ, LK = 32, 56, 1500
T = B * LQ
CH = 448
NCH = T // CH
CB = CH // LQ
KT = 125
NT = LK // KT
H = 16
HQ = H * LQ
HALF = HQ // 2
RT = HQ // 128
NPAIR = B // 2
E = 8
RTOK = 112
NR = T // RTOK
EPS = 1e-5


def reach(eng, sem, k, per, off):
    if isinstance(k, int):
        if per * k + off > 0:
            eng.wait_ge(sem, per * k + off)
    else:
        assert per + off >= 0
        eng.wait_ge(sem, k * per + off)


def over_pairs(eng, step):
    step(0)
    with eng.Fori(1, NPAIR - 1) as k:
        step(k)
    step(NPAIR - 1)


def samples(k):
    for j in range(2):
        yield j, isinstance(k, int) and k == 0 and j == 0, isinstance(k, int) and k == NPAIR - 1 and j == 1


class Phases:

    def __init__(self, nc):
        self.nc, self.own, self.before = nc, [], []
        self.own_held, self.before_held = ExitStack(), ExitStack()

    def semaphore(self, name):
        self.own.append(self.own_held.enter_context(self.nc.semaphore(name)))
        return self.own[-1]

    @contextmanager
    def block(self):
        with self.nc.Block() as block:
            @block.gpsimd
            def _(pool):
                for s in self.before:
                    pool.sem_clear(s)
            yield block
        self.before_held.close()
        self.before, self.before_held = self.own, self.own_held
        self.own, self.own_held = [], ExitStack()


def layer_norm(ph, name, src, dst, ones_mean, psum, affine=None):
    nc = ph.nc
    with ExitStack() as ctx:
        cen = ctx.enter_context(nc.sbuf_tensor(f"{name}_cen", [D, NCH, CH], F32))
        sq = ctx.enter_context(nc.sbuf_tensor(f"{name}_sq", [D, NCH, CH], F32))
        sem = lambda n: ph.semaphore(f"{name}_{n}")
        mean_ready, centred, squared, var_ready, rooted, inverted, scaled, done = map(
            sem, ("mean_ready", "centred", "squared", "var_ready", "rooted", "inverted", "scaled", "done"))
        block = ctx.enter_context(ph.block())

        @block.tensor
        def _(pe):
            for c in range(NCH):
                nc.tensor.matmul(psum[:, c, 0:CH], ones_mean[:], src[:, c * CH:(c + 1) * CH],
                                 start=True, stop=True).then_inc(mean_ready, 1)
            for c in range(NCH):
                pe.wait_ge(squared, c + 1)
                nc.tensor.matmul(psum[:, 4 + c, 0:CH], ones_mean[:], sq[:, c, :],
                                 start=True, stop=True).then_inc(var_ready, 1)

        @block.scalar
        def _(act):
            for c in range(NCH):
                act.wait_ge(centred, c + 1)
                nc.scalar.activation(sq[:, c, :], cen[:, c, :], ACT.Square).then_inc(squared, 1)
            for c in range(NCH):
                act.wait_ge(inverted, c + 1)
                nc.scalar.activation(sq[:, c, :], sq[:, c, :], ACT.Sqrt).then_inc(rooted, 1)

        @block.vector
        def _(dve):
            for c in range(NCH):
                dve.wait_ge(mean_ready, c + 1)
                nc.vector.tensor_tensor(cen[:, c, :], src[:, c * CH:(c + 1) * CH], psum[:, c, 0:CH],
                                        ALU.subtract).then_inc(centred, 1)
            for c in range(NCH):
                dve.wait_ge(var_ready, c + 1)
                nc.vector.tensor_scalar(sq[:, c, :], psum[:, 4 + c, 0:CH], EPS, None,
                                        ALU.add).then_inc(scaled, 1)
                dve.wait_ge(scaled, c + 1)
                nc.vector.reciprocal(sq[:, c, :], sq[:, c, :]).then_inc(inverted, 1)
            for c in range(NCH):
                dve.wait_ge(rooted, c + 1)
                nc.vector.tensor_tensor(dst[:, c * CH:(c + 1) * CH], cen[:, c, :], sq[:, c, :],
                                        ALU.mult).then_inc(done, 1)
            if affine is not None:
                gamma, beta = affine
                dve.wait_ge(done, NCH)
                nc.vector.tensor_scalar(dst[:], dst[:], gamma, beta, ALU.mult, ALU.add).then_inc(done, 1)


def sigmoid_attention(ph, xT, xnT, ctxT_d, ctx_d, mask_d, wqT_d, bq_d, wk_d, bk_d, psum):
    SCALE = float(D) ** -0.5
    DK = 64
    nc = ph.nc
    with ExitStack() as ctx:
        sb = lambda n, s, dt=F32: ctx.enter_context(nc.sbuf_tensor(f"sa_{n}", s, dt))
        sem = lambda n: ph.semaphore(f"sa_{n}")
        wqT, wk, bq, bk = sb("wqT", [D, DK]), sb("wk", [DK, D]), sb("bq", [DK, 1]), sb("bk", [DK, 1])
        masked = sb("masked", [KT, B, NT], I32)
        keep = sb("keep", [KT, B, NT])
        ones_row = sb("ones_row", [1, KT])
        qT, qkT, qb = sb("qT", [DK, T]), sb("qkT", [D, T]), sb("qb", [1, T])
        ctxT = [sb(f"ctxT{i}", [D, LK]) for i in range(2)]
        cx = [sb(f"cx{i}", [KT, NT, D]) for i in range(2)]
        alpha = [sb(f"alpha{i}", [KT, NT, LQ]) for i in range(2)]
        weights_in, mask_in, keep_done, ones_done = sem("weights_in"), sem("mask_in"), sem("keep_done"), sem("ones_done")
        q_ready, q_done, qk_ready, qk_done, qb_ready, qb_done = map(
            sem, ("q_ready", "q_done", "qk_ready", "qk_done", "qb_ready", "qb_done"))
        ctxT_in = [sem(f"ctxT_in{i}") for i in range(2)]
        cx_in = [sem(f"cx_in{i}") for i in range(2)]
        s_ready, sig_done, alpha_done, y_ready, x_done = map(
            sem, ("s_ready", "sig_done", "alpha_done", "y_ready", "x_done"))
        block = ctx.enter_context(ph.block())

        @block.sync
        def _(sp):
            sp.dma_start(wqT[:], wqT_d).then_inc(weights_in, 16)
            sp.dma_start(wk[:], wk_d).then_inc(weights_in, 16)
            sp.dma_start(bq[:], bq_d).then_inc(weights_in, 16)
            sp.dma_start(bk[:], bk_d).then_inc(weights_in, 16)
            sp.dma_start(masked[:], mask_d).then_inc(mask_in, 16)

            def step(k):
                for j, _, _ in samples(k):
                    reach(sp, s_ready, k, 2, j - 1)
                    sp.dma_start(ctxT[j][:], ctxT_d[2 * k + j]).then_inc(ctxT_in[j], 16)
                    reach(sp, y_ready, k, 2, j - 1)
                    sp.dma_start(cx[j][:], ctx_d[2 * k + j]).then_inc(cx_in[j], 16)
            over_pairs(sp, step)

        @block.tensor
        def _(pe):
            pe.wait_ge(weights_in, 64)
            for c in range(NCH):
                nc.tensor.matmul(psum[0:DK, c, 0:CH], wqT[:], xnT[:, c * CH:(c + 1) * CH],
                                 start=True, stop=True).then_inc(q_ready, 1)
            for c in range(NCH):
                pe.wait_ge(q_done, c + 1)
                nc.tensor.matmul(psum[:, 4 + c, 0:CH], wk[:], qT[:, c * CH:(c + 1) * CH],
                                 start=True, stop=True).then_inc(qk_ready, 1)
            for c in range(NCH):
                nc.tensor.matmul(psum[0:1, c, 0:CH], bk[:], qT[:, c * CH:(c + 1) * CH],
                                 start=True, stop=True).then_inc(qb_ready, 1)
            pe.wait_ge(ones_done, 1)
            pe.wait_ge(qk_done, NCH)
            pe.wait_ge(qb_done, NCH)

            def scores(k, j):
                pe.wait_ge(ctxT_in[j], 16 * (k + 1))
                reach(pe, sig_done, k, 2, j - 1)
                q = bass.ds((2 * k + j) * LQ, LQ)
                for t in range(NT):
                    out = psum[0:KT, 2 * j + t // 6, (t % 6) * LQ:(t % 6 + 1) * LQ]
                    nc.tensor.matmul(out, ctxT[j][:, t * KT:(t + 1) * KT], qkT[:, q], start=True, stop=False)
                    last = nc.tensor.matmul(out, ones_row[:], qb[:, q], start=False, stop=True)
                last.then_inc(s_ready, 1)

            def output(k, j):
                i = 1 - j
                reach(pe, alpha_done, k, 2, j)
                pe.wait_ge(cx_in[i], 16 * (k + j) if isinstance(k, int) else (k + j) * 16)
                reach(pe, x_done, k, 2, j - 2)
                for t in range(NT):
                    last = nc.tensor.matmul(psum[:, 4 + i, 0:LQ], cx[i][:, t, :], alpha[i][:, t, :],
                                            start=t == 0, stop=t == NT - 1)
                last.then_inc(y_ready, 1)

            def step(k):
                for j, first, _ in samples(k):
                    scores(k, j)
                    if not first:
                        output(k, j)
            over_pairs(pe, step)
            output(NPAIR, 0)

        @block.scalar
        def _(act):
            for c in range(NCH):
                act.wait_ge(q_ready, c + 1)
                nc.scalar.activation(qT[:, c * CH:(c + 1) * CH], psum[0:DK, c, 0:CH], ACT.Identity,
                                     bias=bq[:]).then_inc(q_done, 1)

            def step(k):
                for j, _, _ in samples(k):
                    reach(act, s_ready, k, 2, j + 1)
                    reach(act, y_ready, k, 2, j - 1)
                    nc.scalar.activation(
                        alpha[j][:].rearrange("p (a t) q -> p a (t q)", a=2),
                        psum[0:KT, 2 * j:2 * j + 2, 0:6 * LQ], ACT.Sigmoid, scale=SCALE).then_inc(sig_done, 1)
            over_pairs(act, step)

        @block.vector
        def _(dve):
            nc.vector.memset(ones_row[:], 1.0).then_inc(ones_done, 1)
            dve.wait_ge(mask_in, 16)
            nc.vector.tensor_scalar(keep[:], masked[:], 1.0, None, ALU.not_equal).then_inc(keep_done, 1)
            for c in range(NCH):
                dve.wait_ge(qk_ready, c + 1)
                nc.vector.tensor_copy(qkT[:, c * CH:(c + 1) * CH], psum[:, 4 + c, 0:CH]).then_inc(qk_done, 1)
            for c in range(NCH):
                dve.wait_ge(qb_ready, c + 1)
                nc.vector.tensor_copy(qb[:, c * CH:(c + 1) * CH], psum[0:1, c, 0:CH]).then_inc(qb_done, 1)
            dve.wait_ge(keep_done, 1)

            def add(k, j):
                reach(dve, y_ready, k, 2, j)
                q = bass.ds((2 * k + j - 1) * LQ, LQ)
                nc.vector.tensor_tensor(xT[:, q], xT[:, q], psum[:, 5 - j, 0:LQ], ALU.add).then_inc(x_done, 1)

            def step(k):
                for j, first, _ in samples(k):
                    reach(dve, sig_done, k, 2, j + 1)
                    nc.vector.tensor_tensor(
                        alpha[j][:], alpha[j][:],
                        keep[:, 2 * k + j, :].unsqueeze(2).broadcast_to([KT, NT, LQ]),
                        ALU.mult).then_inc(alpha_done, 1)
                    if not first:
                        add(k, j)
            over_pairs(dve, step)
            add(NPAIR, 0)


def head_queries(ph, name, xnT, wq_d, bq_d, heads, qx_d, psum):
    nc = ph.nc
    with ExitStack() as ctx:
        sb = lambda n, s: ctx.enter_context(nc.sbuf_tensor(f"{name}_{n}", s, F32))
        sem = lambda n: ph.semaphore(f"{name}_{n}")
        wq, bq, qT = sb("wq", [D, D]), sb("bq", [D, 1]), sb("qT", [D, T])
        stage = [sb(f"stage{i}", [D, CB, H, LQ]) for i in range(2)]
        weights_in, q_ready, q_done, staged = sem("weights_in"), sem("q_ready"), sem("q_done"), sem("staged")
        stored = [sem(f"stored{i}") for i in range(2)]
        block = ctx.enter_context(ph.block())

        @block.sync
        def _(sp):
            sp.dma_start(wq[:], wq_d).then_inc(weights_in, 16)
            sp.dma_start(bq[:], bq_d).then_inc(weights_in, 16)
            for c in range(NCH):
                sp.wait_ge(staged, H * (c + 1))
                sp.dma_start(qx_d[c * CB:(c + 1) * CB].rearrange("b p n -> p b n"),
                             stage[c % 2][:].rearrange("p b h q -> p b (h q)")).then_inc(stored[c % 2], 16)
            for i in range(2):
                sp.wait_ge(stored[i], 16 * (NCH // 2))

        @block.tensor
        def _(pe):
            pe.wait_ge(weights_in, 32)
            for c in range(NCH):
                nc.tensor.matmul(psum[:, c, 0:CH], wq[:], xnT[:, c * CH:(c + 1) * CH],
                                 start=True, stop=True).then_inc(q_ready, 1)

        @block.scalar
        def _(act):
            for c in range(NCH):
                act.wait_ge(q_ready, c + 1)
                nc.scalar.activation(qT[:, c * CH:(c + 1) * CH], psum[:, c, 0:CH], ACT.Identity,
                                     bias=bq[:]).then_inc(q_done, 1)

        @block.vector
        def _(dve):
            for c in range(NCH):
                dve.wait_ge(q_done, c + 1)
                if c >= 2:
                    dve.wait_ge(stored[c % 2], 16 * (c // 2))
                for h in range(H):
                    nc.vector.tensor_scalar(
                        stage[c % 2][:, :, h, :], qT[:, c * CH:(c + 1) * CH].rearrange("p (b q) -> p b q", b=CB),
                        heads[:, h:h + 1], None, ALU.mult).then_inc(staged, 1)


def folded_weights(ph, wqT_d, wkT_d, wvT_d, wo_d, gate_d, bo, w_in, w_out, psum):
    DH = 64
    nc = ph.nc
    with ExitStack() as ctx:
        sb = lambda n, s: ctx.enter_context(nc.sbuf_tensor(f"fw_{n}", s, F32))
        sem = lambda n: ph.semaphore(f"fw_{n}")
        wqT, wkT, wvT, wo = (sb(n, [DH, H, D]) for n in ("wqT", "wkT", "wvT", "wo"))
        gate, tanh = sb("gate", [D, 1]), sb("tanh", [D, 1])
        weights_in, gate_in, tanh_done, m_ready, m_done = map(
            sem, ("weights_in", "gate_in", "tanh_done", "m_ready", "m_done"))
        block = ctx.enter_context(ph.block())
        NG = 2 * H // 4

        @block.sync
        def _(sp):
            sp.dma_start(gate[:], gate_d.broadcast_to([D, 1])).then_inc(gate_in, 16)
            for dst, src in ((wqT, wqT_d), (wkT, wkT_d), (wvT, wvT_d), (wo, wo_d)):
                sp.dma_start(dst[:], src.rearrange("(h e) d -> e h d", h=H)).then_inc(weights_in, 16)

        @block.tensor
        def _(pe):
            pe.wait_ge(weights_in, 64)
            for g in range(NG):
                left, right = (wqT, wkT) if g < NG // 2 else (wvT, wo)
                for i in range(4):
                    h = (4 * g + i) % H
                    last = nc.tensor.matmul(psum[:, g, i * D:(i + 1) * D], left[:, h, :], right[:, h, :],
                                            start=True, stop=True)
                last.then_inc(m_ready, 1)

        @block.scalar
        def _(act):
            act.wait_ge(gate_in, 16)
            nc.scalar.activation(tanh[:], gate[:], ACT.Tanh).then_inc(tanh_done, 1)

        @block.vector
        def _(dve):
            for g in range(NG // 2):
                dve.wait_ge(m_ready, g + 1)
                nc.vector.tensor_copy(w_in[:, 4 * g:4 * g + 4, :],
                                      psum[:, g, :].rearrange("p (h d) -> p h d", h=4)).then_inc(m_done, 1)
            dve.wait_ge(tanh_done, 1)
            nc.vector.tensor_scalar(bo[:], bo[:], tanh[:], None, ALU.mult).then_inc(m_done, 1)
            for g in range(NG // 2):
                dve.wait_ge(m_ready, NG // 2 + g + 1)
                nc.vector.tensor_scalar(w_out[:, 4 * g:4 * g + 4, :],
                                        psum[:, NG // 2 + g, :].rearrange("p (h d) -> p h d", h=4),
                                        tanh[:], None, ALU.mult).then_inc(m_done, 1)


def folded_queries(ph, xnT, w_in, qx_d, psum):
    nc = ph.nc
    with ExitStack() as ctx:
        stage = [ctx.enter_context(nc.sbuf_tensor(f"fq_stage{i}", [D, CB, H, LQ], F32)) for i in range(2)]
        sem = lambda n: ph.semaphore(f"fq_{n}")
        ready = sem("ready")
        staged = [sem("staged_act"), sem("staged_dve")]
        stored = [sem(f"stored{i}") for i in range(2)]
        block = ctx.enter_context(ph.block())

        @block.sync
        def _(sp):
            for c in range(NCH):
                for s in staged:
                    sp.wait_ge(s, H // 2 * (c + 1))
                sp.dma_start(qx_d[c * CB:(c + 1) * CB].rearrange("b p n -> p b n"),
                             stage[c % 2][:].rearrange("p b h q -> p b (h q)")).then_inc(stored[c % 2], 16)
            for i in range(2):
                sp.wait_ge(stored[i], 16 * (NCH // 2))

        @block.tensor
        def _(pe):
            for c in range(NCH):
                for h in range(H):
                    n = c * H + h
                    if n >= 8:
                        pe.wait_ge(staged[n % 2], (n - 8) // 2 + 1)
                    nc.tensor.matmul(psum[:, n % 8, 0:CH], w_in[:, h, :], xnT[:, c * CH:(c + 1) * CH],
                                     start=True, stop=True).then_inc(ready, 1)

        @block.scalar
        def _(act):
            for c in range(NCH):
                if c >= 2:
                    act.wait_ge(stored[c % 2], 16 * (c // 2))
                for h in range(0, H, 2):
                    act.wait_ge(ready, c * H + h + 1)
                    nc.scalar.activation(
                        stage[c % 2][:, :, h, :],
                        psum[:, h % 8, 0:CH].rearrange("p (b q) -> p b q", b=CB),
                        ACT.Copy).then_inc(staged[0], 1)

        @block.vector
        def _(dve):
            for c in range(NCH):
                if c >= 2:
                    dve.wait_ge(stored[c % 2], 16 * (c // 2))
                for h in range(1, H, 2):
                    dve.wait_ge(ready, c * H + h + 1)
                    nc.vector.tensor_copy(
                        stage[c % 2][:, :, h, :],
                        psum[:, h % 8, 0:CH].rearrange("p (b q) -> p b q", b=CB)).then_inc(staged[1], 1)


class Front:

    ITEMS = 6

    def __init__(self, nc, ctxT, ctxT_in, wk, wv, bk, bv, kT, v, bank, side_ready, side_free):
        self.nc, self.ctxT, self.ctxT_in, self.wk, self.wv, self.bk, self.bv = nc, ctxT, ctxT_in, wk, wv, bk, bv
        self.kT, self.v, self.bank, self.side_ready, self.side_free = kT, v, bank, side_ready, side_free

    def product(self, pe, k, j, i):
        nc = self.nc
        if i == 0:
            pe.wait_ge(self.ctxT_in[j], 16 * (k + 1))
        reach(pe, self.side_free, k, 2 * self.ITEMS, self.ITEMS * j + i)
        if i < 3:
            nc.tensor.matmul(self.bank[:, 0:500], self.wk[:], self.ctxT[j][:, i * 500:(i + 1) * 500],
                             start=True, stop=True).then_inc(self.side_ready, 1)
        else:
            for n in range(4):
                t = 4 * (i - 3) + n
                last = nc.tensor.matmul(self.bank[0:KT, n * D:(n + 1) * D],
                                        self.ctxT[j][:, t * KT:(t + 1) * KT], self.wv[:], start=True, stop=True)
            last.then_inc(self.side_ready, 1)

    def key_out(self, act, k, j, i):
        reach(act, self.side_ready, k, 2 * self.ITEMS, self.ITEMS * j + i + 1)
        self.nc.scalar.activation(self.kT[j][:, i * 500:(i + 1) * 500], self.bank[:, 0:500], ACT.Identity,
                                  bias=self.bk[:]).then_inc(self.side_free, 1)

    def value_out(self, dve, k, j, i):
        reach(dve, self.side_ready, k, 2 * self.ITEMS, self.ITEMS * j + i + 1)
        t = 4 * (i - 3)
        self.nc.vector.tensor_tensor(
            self.v[j][:, t:t + 4, :], self.bank[0:KT, :].rearrange("p (t n) -> p t n", t=4),
            self.bv[0:KT, :].unsqueeze(1).broadcast_to([KT, 4, D]), ALU.add).then_inc(self.side_free, 1)


def after(k, j):
    return (k, 1) if j == 0 else (k + 1, 0)


def query_softmax_attention(ph, name, ctxT_d, qx_d, ox_d, wk_d, bk_d, wv_d, bv_d, scale, psum):
    nc = ph.nc
    with ExitStack() as ctx:
        sb = lambda n, s: ctx.enter_context(nc.sbuf_tensor(f"{name}_{n}", s, F32))
        sem = lambda n: ph.semaphore(f"{name}_{n}")
        wk, wv, bk, bv = sb("wk", [D, D]), sb("wv", [D, D]), sb("bk", [D, 1]), sb("bv", [D, D])
        ctxT = [sb(f"ctxT{i}", [D, LK]) for i in range(2)]
        kT = [sb(f"kT{i}", [D, LK]) for i in range(2)]
        v = [sb(f"v{i}", [KT, NT, D]) for i in range(2)]
        qx = [sb(f"qx{i}", [D, HQ]) for i in range(2)]
        ox = [sb(f"ox{i}", [D, HQ]) for i in range(2)]
        p = [sb(f"p{i}", [KT, H, LQ]) for i in range(4)]
        vz = [sb(f"vz{i}", [KT, H, D // H]) for i in range(4)]
        top = [sb(f"top{i}", [KT, H]) for i in range(2)]
        f28 = [sb(f"f28{i}", [KT, H, 28]) for i in range(2)]
        f14 = [sb(f"f14{i}", [KT, H, 14]) for i in range(2)]
        f7 = [sb(f"f7{i}", [KT, H, 7]) for i in range(2)]
        z = [sb(f"z{i}", [KT, H]) for i in range(2)]
        rz = [sb(f"rz{i}", [KT, H]) for i in range(2)]
        weights_in = sem("weights_in")
        ctxT_in = [sem(f"ctxT_in{i}") for i in range(2)]
        qx_in = [sem(f"qx_in{i}") for i in range(2)]
        ox_out = [sem(f"ox_out{i}") for i in range(2)]
        (side_ready, side_free, s_ready, top_done, sub_done, exp_done, half_done, quarter_done, tree_done,
         z_done, rz_done, vz_done, o_ready, o_done) = map(sem, (
             "side_ready", "side_free", "s_ready", "top_done", "sub_done", "exp_done", "half_done",
             "quarter_done", "tree_done", "z_done", "rz_done", "vz_done", "o_ready", "o_done"))
        front = Front(nc, ctxT, ctxT_in, wk, wv, bk, bv, kT, v, psum[:, 6, :], side_ready, side_free)
        ITEM_AT = {1: 0, 2: 1, 4: 2, 6: 3, 8: 4, 10: 5}
        LAG = 3
        block = ctx.enter_context(ph.block())

        def score(j):
            return psum[0:KT, 2 * j:2 * j + 2, 0:HALF].rearrange("p a (h q) -> p a h q", h=H // 2)

        @block.sync
        def _(sp):
            sp.dma_start(wk[:], wk_d).then_inc(weights_in, 16)
            sp.dma_start(wv[:], wv_d).then_inc(weights_in, 16)
            sp.dma_start(bk[:], bk_d).then_inc(weights_in, 16)
            sp.dma_start(bv[:], bv_d.broadcast_to([D, D])).then_inc(weights_in, 16)
            for j in range(2):
                sp.dma_start(ctxT[j][:], ctxT_d[j]).then_inc(ctxT_in[j], 16)
            sp.dma_start(qx[0][:], qx_d[0]).then_inc(qx_in[0], 16)

            def store(k, j):
                reach(sp, o_done, k, 2, j + 1)
                sp.dma_start(ox_d[2 * k + j], ox[j][:]).then_inc(ox_out[j], 16)

            def step(k):
                end = isinstance(k, int) and k == NPAIR - 1
                for j, first, last in samples(k):
                    if not last:
                        kn, jn = after(k, j)
                        reach(sp, s_ready, k, 2 * NT, NT * j)
                        sp.dma_start(qx[jn][:], qx_d[2 * k + j + 1]).then_inc(qx_in[jn], 16)
                    if not end:
                        reach(sp, side_ready, k, 12, 6 * j + 6)
                        sp.dma_start(ctxT[j][:], ctxT_d[2 * k + j + 2]).then_inc(ctxT_in[j], 16)
                    if not first:
                        store(*((k, 0) if j else (k - 1, 1)))
            over_pairs(sp, step)
            store(NPAIR - 1, 1)
            for i in range(2):
                sp.wait_ge(ox_out[i], 16 * NPAIR)

        @block.tensor
        def _(pe):
            pe.wait_ge(weights_in, 64)
            for i in range(6):
                front.product(pe, 0, 0, i)

            def output(k, s):
                s -= LAG
                j, t = s // NT % 2, s % NT
                reach(pe, vz_done, k, 2 * NT, s + 1)
                if t == 0:
                    reach(pe, o_done, k, 2, s // NT)
                for a in range(2):
                    last = nc.tensor.matmul(
                        psum[:, 4 + a, 0:HALF], vz[s % 4][:].rearrange("p h d -> p (h d)"),
                        p[s % 4][:, 8 * a:8 * a + 8, :].rearrange("p h q -> p (h q)"),
                        start=t == 0, stop=t == NT - 1)
                last.then_inc(o_ready, 1)

            def step(k):
                for j, first, last_sample in samples(k):
                    for t in range(NT):
                        s = NT * j + t
                        if t == 0:
                            reach(pe, side_free, k, 12, 6 * j + 6)
                            pe.wait_ge(qx_in[j], (k + 1) * 16)
                        reach(pe, sub_done, k, 2 * NT, s - 1)
                        for a in range(2):
                            last = nc.tensor.matmul(psum[0:KT, 2 * (s % 2) + a, 0:HALF],
                                                    kT[j][:, t * KT:(t + 1) * KT],
                                                    qx[j][:, a * HALF:(a + 1) * HALF], start=True, stop=True)
                        last.then_inc(s_ready, 1)
                        if not (first and t < LAG):
                            output(k, s)
                        if t in ITEM_AT and not last_sample:
                            front.product(pe, *after(k, j), ITEM_AT[t])
            over_pairs(pe, step)
            for s in range(LAG):
                output(NPAIR, s)

        @block.scalar
        def _(act):
            act.wait_ge(weights_in, 64)
            for i in range(3):
                front.key_out(act, 0, 0, i)

            def output(k, j):
                i = 1 - j
                reach(act, o_ready, k, 2 * NT, NT * j)
                reach(act, ox_out[i], k, 16, 16 * (j - 1))
                nc.scalar.activation(ox[i][:].rearrange("p (a n) -> p a n", a=2), psum[:, 4:6, 0:HALF],
                                     ACT.Copy).then_inc(o_done, 1)

            def step(k):
                for j, first, last_sample in samples(k):
                    for t in range(NT):
                        s = NT * j + t
                        reach(act, sub_done, k, 2 * NT, s + 1)
                        nc.scalar.activation(p[s % 4][:], p[s % 4][:], ACT.Exp, scale=scale).then_inc(exp_done, 1)
                        if t == LAG - 1 and not first:
                            output(k, j)
                        if t in ITEM_AT and ITEM_AT[t] < 3 and not last_sample:
                            front.key_out(act, *after(k, j), ITEM_AT[t])
            over_pairs(act, step)
            output(NPAIR, 0)

        @block.gpsimd
        def _(pool):
            def step(k):
                for j, _, _ in samples(k):
                    for t in range(NT):
                        s = NT * j + t
                        reach(pool, exp_done, k, 2 * NT, s + 1)
                        pt = p[s % 4]
                        nc.gpsimd.tensor_tensor(f28[s % 2][:], pt[:, :, 0:28], pt[:, :, 28:56],
                                                ALU.add).then_inc(half_done, 1)
                        reach(pool, half_done, k, 2 * NT, s + 1)
                        nc.gpsimd.tensor_tensor(f14[s % 2][:], f28[s % 2][:, :, 0:14], f28[s % 2][:, :, 14:28],
                                                ALU.add).then_inc(quarter_done, 1)
                        reach(pool, quarter_done, k, 2 * NT, s + 1)
                        reach(pool, z_done, k, 2 * NT, s - 1)
                        nc.gpsimd.tensor_tensor(f7[s % 2][:], f14[s % 2][:, :, 0:7], f14[s % 2][:, :, 7:14],
                                                ALU.add).then_inc(tree_done, 1)
            over_pairs(pool, step)

        @block.vector
        def _(dve):
            dve.wait_ge(weights_in, 64)
            for i in range(3, 6):
                front.value_out(dve, 0, 0, i)

            def normalise(k, s):
                s -= 2
                j, t = s // NT % 2, s % NT
                reach(dve, tree_done, k, 2 * NT, s + 1)
                nc.vector.tensor_reduce(z[s % 2][:], f7[s % 2][:], AX.X, ALU.add).then_inc(z_done, 1)
                reach(dve, z_done, k, 2 * NT, s + 1)
                nc.vector.reciprocal(rz[s % 2][:], z[s % 2][:]).then_inc(rz_done, 1)
                reach(dve, rz_done, k, 2 * NT, s + 1)
                reach(dve, o_ready, k, 2 * NT, s - 3)
                nc.vector.tensor_tensor(
                    vz[s % 4][:], v[j][:, t, :].rearrange("p (h d) -> p h d", h=H),
                    rz[s % 2][:].unsqueeze(2).broadcast_to([KT, H, D // H]), ALU.mult).then_inc(vz_done, 1)

            def step(k):
                for j, first, last_sample in samples(k):
                    for t in range(NT):
                        s = NT * j + t
                        reach(dve, s_ready, k, 2 * NT, s + 1)
                        nc.vector.tensor_reduce(top[s % 2][:].rearrange("p (a h) -> p a h", a=2), score(s % 2),
                                                AX.X, ALU.max).then_inc(top_done, 1)
                        reach(dve, top_done, k, 2 * NT, s + 1)
                        reach(dve, o_ready, k, 2 * NT, s - 3)
                        nc.vector.tensor_tensor(
                            p[s % 4][:].rearrange("p (a h) q -> p a h q", a=2), score(s % 2),
                            top[s % 2][:].rearrange("p (a h) -> p a h", a=2).unsqueeze(3)
                            .broadcast_to([KT, 2, H // 2, LQ]), ALU.subtract).then_inc(sub_done, 1)
                        if not (first and t < 2):
                            normalise(k, s)
                        if t in ITEM_AT and ITEM_AT[t] >= 3 and not last_sample:
                            front.value_out(dve, *after(k, j), ITEM_AT[t])
            over_pairs(dve, step)
            for s in range(2):
                normalise(NPAIR, s)


def key_softmax_attention(ph, name, ctxT_d, ctx_d, qx_d, ox_d, proj, scale, ident, psum):
    nc = ph.nc
    with ExitStack() as ctx:
        sb = lambda n, s: ctx.enter_context(nc.sbuf_tensor(f"{name}_{n}", s, F32))
        sem = lambda n: ph.semaphore(f"{name}_{n}")
        ctxT = [sb(f"ctxT{i}", [D, LK]) for i in range(2)]
        v = [sb(f"v{i}", [KT, NT, D]) for i in range(2)]
        qx = [sb(f"qx{i}", [D, HQ]) for i in range(2)]
        ox = [sb(f"ox{i}", [D, HQ]) for i in range(2)]
        p = [sb(f"p{i}", [D, LK]) for i in range(2)]
        pT = [sb(f"pT{i}", [KT, NT, D]) for i in range(2)]
        stats = sb("stats", [D, 4, 2])
        top, shift, z, rz = (stats[:, i, :] for i in range(4))
        ctxT_in = [sem(f"ctxT_in{i}") for i in range(2)]
        qx_in = [sem(f"qx_in{i}") for i in range(2)]
        v_in = [sem(f"v_in{i}") for i in range(2)]
        ox_out = [sem(f"ox_out{i}") for i in range(2)]
        pT_done = [sem(f"pT_done{i}") for i in range(3)]
        (stats_clear, weights_in, side_ready, side_free, s_ready, top_done, shift_done, exp_done, rz_done,
         norm_done, t_ready, o_ready, o_done) = map(sem, (
             "stats_clear", "weights_in", "side_ready", "side_free", "s_ready", "top_done", "shift_done", "exp_done",
             "rz_done", "norm_done", "t_ready", "o_ready", "o_done"))
        S_BANKS, T_BANK, O_BANK, SIDE = slice(0, 3), 3, 5, 7
        if proj:
            kT = [sb(f"kT{i}", [D, LK]) for i in range(2)]
            wk, wv, bk, bv = sb("wk", [D, D]), sb("wv", [D, D]), sb("bk", [D, 1]), sb("bv", [D, D])
            front = Front(nc, ctxT, ctxT_in, wk, wv, bk, bv, kT, v, psum[:, SIDE, :], side_ready, side_free)
        else:
            kT = ctxT
        ITEM_AT = {(0, 0): 0, (0, 1): 1, (1, 0): 2, (3, 0): 3, (4, 0): 4, (5, 0): 5} if proj else {}
        block = ctx.enter_context(ph.block())

        @block.sync
        def _(sp):
            if proj:
                wk_d, bk_d, wv_d, bv_d = proj
                sp.dma_start(wk[:], wk_d).then_inc(weights_in, 16)
                sp.dma_start(wv[:], wv_d).then_inc(weights_in, 16)
                sp.dma_start(bk[:], bk_d).then_inc(weights_in, 16)
                sp.dma_start(bv[:], bv_d.broadcast_to([D, D])).then_inc(weights_in, 16)
            sp.dma_start(ctxT[0][:], ctxT_d[0]).then_inc(ctxT_in[0], 16)
            sp.dma_start(qx[0][:], qx_d[0]).then_inc(qx_in[0], 16)
            if proj:
                sp.dma_start(ctxT[1][:], ctxT_d[1]).then_inc(ctxT_in[1], 16)
            else:
                sp.dma_start(v[0][:], ctx_d[0]).then_inc(v_in[0], 16)

            def store(k, j):
                reach(sp, o_done, k, 2 * RT, RT * (j + 1))
                sp.dma_start(ox_d[2 * k + j], ox[j][:]).then_inc(ox_out[j], 16)

            def step(k):
                end = isinstance(k, int) and k == NPAIR - 1
                for j, first, last in samples(k):
                    jn = 1 - j
                    if not last:
                        reach(sp, s_ready, k, 2 * RT, RT * j)
                        sp.dma_start(qx[jn][:], qx_d[2 * k + j + 1]).then_inc(qx_in[jn], 16)
                    if not proj and not last:
                        sp.dma_start(ctxT[jn][:], ctxT_d[2 * k + j + 1]).then_inc(ctxT_in[jn], 16)
                        reach(sp, o_ready, k, 2 * RT, RT * j)
                        sp.dma_start(v[jn][:], ctx_d[2 * k + j + 1]).then_inc(v_in[jn], 16)
                    if proj and not end:
                        reach(sp, side_ready, k, 12, 6 * j + 6)
                        sp.dma_start(ctxT[j][:], ctxT_d[2 * k + j + 2]).then_inc(ctxT_in[j], 16)
                    if not first:
                        store(*((k, 0) if j else (k - 1, 1)))
            over_pairs(sp, step)
            store(NPAIR - 1, 1)
            for i in range(2):
                sp.wait_ge(ox_out[i], 16 * NPAIR)

        @block.tensor
        def _(pe):
            if proj:
                pe.wait_ge(weights_in, 64)
                for i in range(6):
                    front.product(pe, 0, 0, i)

            def transposes(k, s, i):
                s -= 1
                n = 3 * s + i
                if i == 0:
                    reach(pe, norm_done, k, 2 * RT, s + 1)
                    reach(pe, pT_done[1], k, 2 * RT, s)
                elif i == 1:
                    reach(pe, pT_done[2], k, 2 * RT, s)
                else:
                    reach(pe, pT_done[0], k, 2 * RT, s + 1)
                for m in range(4):
                    t = 4 * i + m
                    last = nc.tensor.transpose(psum[0:KT, T_BANK + n % 2, m * D:(m + 1) * D],
                                               p[s % 2][:, t * KT:(t + 1) * KT], ident[:])
                last.then_inc(t_ready, 1)

            def output(k, s, i):
                s -= 2
                j = s // RT % 2
                reach(pe, pT_done[i], k, 2 * RT, s + 1)
                if i == 0:
                    reach(pe, o_done, k, 2 * RT, s - 1)
                    if not proj and s % RT == 0:
                        pe.wait_ge(v_in[j], (k + (1 if s >= 0 else 0)) * 16)
                for m in range(4):
                    t = 4 * i + m
                    last = nc.tensor.matmul(psum[:, O_BANK + s % 2, 0:D], v[j][:, t, :], pT[s % 2][:, t, :],
                                            start=t == 0, stop=t == NT - 1)
                if i == 2:
                    last.then_inc(o_ready, 1)

            def thirds(k, s, t_on, o_on, item):
                for i in range(3):
                    if i == 2 and item is not None:
                        front.product(pe, *item)
                    if t_on:
                        transposes(k, s, i)
                    if o_on:
                        output(k, s, i)

            def step(k):
                for j, first, last_sample in samples(k):
                    for r in range(RT):
                        s = RT * j + r
                        if r == 0:
                            pe.wait_ge(qx_in[j], (k + 1) * 16)
                            if proj:
                                reach(pe, side_free, k, 12, 6 * j + 6)
                            else:
                                pe.wait_ge(ctxT_in[j], (k + 1) * 16)
                        reach(pe, exp_done, k, 2 * RT, s)
                        for a in range(3):
                            last = nc.tensor.matmul(psum[:, a, 0:500], qx[j][:, r * 128:(r + 1) * 128],
                                                    kT[j][:, a * 500:(a + 1) * 500], start=True, stop=True)
                        last.then_inc(s_ready, 1)
                        items = {} if last_sample else ITEM_AT
                        if (r, 0) in items:
                            front.product(pe, *after(k, j), items[r, 0])
                        thirds(k, s, not (first and r < 1), not (first and r < 2),
                               (*after(k, j), items[r, 1]) if (r, 1) in items else None)
            over_pairs(pe, step)
            thirds(NPAIR, 0, True, True, None)
            thirds(NPAIR, 1, False, True, None)

        @block.scalar
        def _(act):
            if proj:
                act.wait_ge(weights_in, 64)
                for i in range(3):
                    front.key_out(act, 0, 0, i)

            def transposed(k, s):
                s -= 1
                reach(act, t_ready, k, 6 * RT, 3 * s + 2)
                reach(act, o_ready, k, 2 * RT, s - 1)
                nc.scalar.activation(pT[s % 2][:, 4:8, :].rearrange("p t n -> p (t n)"),
                                     psum[0:KT, T_BANK + (3 * s + 1) % 2, :], ACT.Copy).then_inc(pT_done[1], 1)

            def output(k, s):
                s -= 2
                j, r = s // RT % 2, s % RT
                reach(act, o_ready, k, 2 * RT, s + 1)
                if r == 0:
                    reach(act, ox_out[j], k, 16, 0 if s >= 0 else -16)
                nc.scalar.activation(ox[j][:, r * 128:(r + 1) * 128], psum[:, O_BANK + s % 2, 0:D],
                                     ACT.Copy).then_inc(o_done, 1)

            def step(k):
                for j, first, last_sample in samples(k):
                    for r in range(RT):
                        s = RT * j + r
                        reach(act, shift_done, k, 2 * RT, s + 1)
                        reach(act, t_ready, k, 6 * RT, 3 * (s - 1))
                        nc.scalar.activation(
                            p[s % 2][:].rearrange("p (a n) -> p a n", a=3), psum[:, S_BANKS, 0:500], ACT.Exp,
                            bias=shift[:, s % 2:s % 2 + 1], scale=scale,
                            accum_out=z[:, s % 2:s % 2 + 1]).then_inc(exp_done, 1)
                        for slot in range(2):
                            if ITEM_AT.get((r, slot), 9) < 3 and not last_sample:
                                front.key_out(act, *after(k, j), ITEM_AT[r, slot])
                            if slot == 0 and not (first and r < 1):
                                transposed(k, s)
                        if not (first and r < 2):
                            output(k, s)
            over_pairs(act, step)
            transposed(NPAIR, 0)
            output(NPAIR, 0)
            output(NPAIR, 1)

        @block.vector
        def _(dve):
            nc.vector.memset(stats[:], 0.0).then_inc(stats_clear, 1)
            dve.wait_ge(stats_clear, 1)
            if proj:
                dve.wait_ge(weights_in, 64)
                for i in range(3, 6):
                    front.value_out(dve, 0, 0, i)

            def transposed(k, s, i):
                s -= 1
                reach(dve, t_ready, k, 6 * RT, 3 * s + i + 1)
                reach(dve, o_ready, k, 2 * RT, s - 1)
                nc.vector.tensor_copy(pT[s % 2][:, 4 * i:4 * i + 4, :].rearrange("p t n -> p (t n)"),
                                      psum[0:KT, T_BANK + (3 * s + i) % 2, :]).then_inc(pT_done[i], 1)

            def step(k):
                for j, first, last_sample in samples(k):
                    for r in range(RT):
                        s = RT * j + r
                        c = slice(s % 2, s % 2 + 1)
                        reach(dve, s_ready, k, 2 * RT, s + 1)
                        nc.vector.tensor_reduce(top[:, c], psum[:, S_BANKS, 0:500], AX.XY,
                                                ALU.max).then_inc(top_done, 1)
                        reach(dve, top_done, k, 2 * RT, s + 1)
                        nc.vector.tensor_scalar(shift[:, c], top[:, c], -scale, None,
                                                ALU.mult).then_inc(shift_done, 1)
                        if ITEM_AT.get((r, 0), 0) >= 3 and not last_sample:
                            front.value_out(dve, *after(k, j), ITEM_AT[r, 0])
                        if not (first and r < 1):
                            transposed(k, s, 0)
                        reach(dve, exp_done, k, 2 * RT, s + 1)
                        nc.vector.reciprocal(rz[:, c], z[:, c]).then_inc(rz_done, 1)
                        reach(dve, rz_done, k, 2 * RT, s + 1)
                        nc.vector.tensor_scalar(p[s % 2][:], p[s % 2][:], rz[:, c], None,
                                                ALU.mult).then_inc(norm_done, 1)
                        if not (first and r < 1):
                            transposed(k, s, 2)
            over_pairs(dve, step)
            for i in (0, 2):
                transposed(NPAIR, 0, i)


def output_projection(ph, name, xT, ox_d, w_out, bo, psum):
    nc = ph.nc
    with ExitStack() as ctx:
        ox = [ctx.enter_context(nc.sbuf_tensor(f"{name}_ox{i}", [D, CB, HQ], F32)) for i in range(2)]
        sem = lambda n: ph.semaphore(f"{name}_{n}")
        ox_in = [sem(f"ox_in{i}") for i in range(2)]
        y_ready, x_done = sem("y_ready"), sem("x_done")
        block = ctx.enter_context(ph.block())

        @block.sync
        def _(sp):
            for c in range(NCH):
                if c >= 2:
                    sp.wait_ge(y_ready, c - 1)
                sp.dma_start(ox[c % 2][:], ox_d[c * CB:(c + 1) * CB].rearrange("b p n -> p b n")).then_inc(ox_in[c % 2], 16)

        @block.tensor
        def _(pe):
            for c in range(NCH):
                pe.wait_ge(ox_in[c % 2], 16 * (c // 2 + 1))
                for h in range(H):
                    last = nc.tensor.matmul(psum[:, c, 0:CH], w_out[:, h, :], ox[c % 2][:, :, h * LQ:(h + 1) * LQ],
                                            start=h == 0, stop=h == H - 1)
                last.then_inc(y_ready, 1)

        @block.vector
        def _(dve):
            for c in range(NCH):
                dve.wait_ge(y_ready, c + 1)
                x = xT[:, c * CH:(c + 1) * CH]
                nc.vector.scalar_tensor_tensor(x, psum[:, c, 0:CH], bo[:], x, ALU.add, ALU.add).then_inc(x_done, 1)


def masked_output_weights(ph, name, wo_d, heads, w_out):
    nc = ph.nc
    with ExitStack() as ctx:
        wo = ctx.enter_context(nc.sbuf_tensor(f"{name}_wo", [D, D], F32))
        wo_in = ph.semaphore(f"{name}_wo_in")
        done = ph.semaphore(f"{name}_done")
        block = ctx.enter_context(ph.block())

        @block.sync
        def _(sp):
            sp.dma_start(wo[:], wo_d).then_inc(wo_in, 16)

        @block.vector
        def _(dve):
            dve.wait_ge(wo_in, 16)
            for h in range(H):
                nc.vector.tensor_scalar(w_out[:, h, :], wo[:], heads[:, h:h + 1], None, ALU.mult).then_inc(done, 1)


def router(ph, name, xnT, gate_d, gate_bias_d, select_bias_d, norm_eps, iota, comb, psum):
    nc = ph.nc
    with ExitStack() as ctx:
        sb = lambda n, s, dt=F32: ctx.enter_context(nc.sbuf_tensor(f"{name}_{n}", s, dt))
        sem = lambda n: ph.semaphore(f"{name}_{n}")
        gate, bias = sb("gate", [D, E]), sb("bias", [D, 1, E])
        logit, prob, sel = (sb(n, [RTOK, NR, E]) for n in ("logit", "prob", "sel"))
        best, index, indexf = sb("best", [RTOK, NR, 8]), sb("index", [RTOK, NR, 8], U32), sb("indexf", [RTOK, NR, 8])
        first, second = sb("first", [RTOK, NR, E]), sb("second", [RTOK, NR, E])
        one = sb("one", [RTOK, NR])
        weights_in, logit_ready, exp_ready, exp_done, step_done, best_done, index_done = map(
            sem, ("weights_in", "logit_ready", "exp_ready", "exp_done", "step_done", "best_done", "index_done"))
        block = ctx.enter_context(ph.block())
        bias_d = gate_bias_d if gate_bias_d is not None else select_bias_d

        def wide(a):
            return a.unsqueeze(2).broadcast_to([RTOK, NR, E])

        @block.sync
        def _(sp):
            sp.dma_start(gate[:], gate_d).then_inc(weights_in, 16)
            if bias_d is not None:
                sp.dma_start(bias[:, 0, :], bias_d.broadcast_to([D, E])).then_inc(weights_in, 16)

        @block.tensor
        def _(pe):
            pe.wait_ge(weights_in, 32 if bias_d is not None else 16)
            for i in range(NR):
                last = nc.tensor.matmul(psum[0:RTOK, 0, i * E:(i + 1) * E], xnT[:, i * RTOK:(i + 1) * RTOK],
                                        gate[:], start=True, stop=True)
            last.then_inc(logit_ready, 1)

        @block.scalar
        def _(act):
            act.wait_ge(exp_ready, 1)
            nc.scalar.activation(prob[:], logit[:], ACT.Exp).then_inc(exp_done, 1)

        @block.vector
        def _(dve):
            done = 0

            def then(ins):
                nonlocal done
                done += 1
                ins.then_inc(step_done, 1)
                dve.wait_ge(step_done, done)

            dve.wait_ge(logit_ready, 1)
            wide_bias = bias[0:RTOK, :, :].broadcast_to([RTOK, NR, E])
            raw = psum[0:RTOK, 0, 0:NR * E].rearrange("p (i e) -> p i e", i=NR)
            if gate_bias_d is not None:
                then(nc.vector.tensor_tensor(logit[:], raw, wide_bias, ALU.add))
            else:
                then(nc.vector.tensor_copy(logit[:], raw))
            then(nc.vector.tensor_reduce(one[:], logit[:], AX.X, ALU.max))
            nc.vector.tensor_tensor(logit[:], logit[:], wide(one[:]), ALU.subtract).then_inc(exp_ready, 1)
            dve.wait_ge(exp_done, 1)
            then(nc.vector.tensor_reduce(one[:], prob[:], AX.X, ALU.add))
            then(nc.vector.reciprocal(one[:], one[:]))
            then(nc.vector.tensor_tensor(prob[:], prob[:], wide(one[:]), ALU.mult))
            key = prob
            if select_bias_d is not None:
                then(nc.vector.tensor_tensor(sel[:], prob[:], wide_bias, ALU.add))
                key = sel
            for i in range(NR):
                nc.vector.max(best[:, i, :], key[:, i, :]).then_inc(best_done, 1)
            for i in range(NR):
                dve.wait_ge(best_done, i + 1)
                nc.vector.max_index(index[:, i, :], best[:, i, :], key[:, i, :]).then_inc(index_done, 1)
            dve.wait_ge(index_done, NR)
            then(nc.vector.tensor_copy(indexf[:], index[:]))
            wide_iota = iota[0:RTOK, :].unsqueeze(1).broadcast_to([RTOK, NR, E])
            then(nc.vector.tensor_tensor(first[:], wide_iota, wide(indexf[:, :, 0]), ALU.is_equal))
            then(nc.vector.tensor_tensor(second[:], wide_iota, wide(indexf[:, :, 1]), ALU.is_equal))
            then(nc.vector.tensor_tensor(first[:], first[:], second[:], ALU.add))
            then(nc.vector.tensor_tensor(comb[:], first[:], prob[:], ALU.mult))
            if norm_eps is not None:
                then(nc.vector.tensor_reduce(one[:], comb[:], AX.X, ALU.add))
                then(nc.vector.tensor_scalar(one[:], one[:], norm_eps, None, ALU.add))
                then(nc.vector.reciprocal(one[:], one[:]))
                then(nc.vector.tensor_tensor(comb[:], comb[:], wide(one[:]), ALU.mult))


def experts(ph, name, xT, xnT, comb, gate_d, up_d, down_d, biases, pieces, mode, n_exp, ident, ones, psum, int_scale=None):
    NF = len(pieces)
    F = sum(n for _, n in pieces)
    PMAX = max(n for _, n in pieces)
    weighted = mode != "plain"
    NS = 2 if n_exp > 1 else 1
    nc = ph.nc
    with ExitStack() as ctx:
        sb = lambda n, s, dt=F32: ctx.enter_context(nc.sbuf_tensor(f"{name}_{n}", s, dt))
        sem = lambda n: ph.semaphore(f"{name}_{n}")
        wg = [sb(f"wg{i}", [D, F]) for i in range(NS)]
        wu = [sb(f"wu{i}", [D, F]) for i in range(NS)]
        wd = [sb(f"wd{i}", [PMAX, NF, D]) for i in range(NS)]
        hid = [sb(f"hid{i}", [PMAX, NF, CH]) for i in range(2)]
        act_out = [sb(f"act_out{i}", [PMAX, CH]) for i in range(2)]
        prod = [sb(f"prod{i}", [PMAX, CH]) for i in range(2)]
        y = [sb(f"y{i}", [D, CH]) for i in range(2)]
        if weighted:
            diag = [sb(f"diag{i}", [RTOK, NR, RTOK]) for i in range(2)]
            wide = [sb(f"wide{i}", [D, T]) for i in range(2)]
        xs = [sb(f"xs{i}", [D, T]) for i in range(2)] if mode == "in" else None
        if mode == "bias":
            gb, ub = ([sb(f"{n}{i}", [PMAX, NF]) for i in range(2)] for n in ("gb", "ub"))
            db = [sb(f"db{i}", [D, 1]) for i in range(2)]
        if int_scale is not None:
            raw = [sb(f"raw{i}", [D, F], I32) for i in range(2)] + [sb("raw2", [PMAX, NF, D], I32)]
        loads = (2 + (1 if all(n == PMAX for _, n in pieces) else 2)) + (3 if mode == "bias" else 0)
        w_in = [sem(f"w_in{i}") for i in range(NS)]
        (w_cast, diag_done, wide_ready, wide_done, xs_done, g_ready, u_ready, act_done, mid_done, h_done,
         y_ready, y_done, x_done) = map(sem, (
             "w_cast", "diag_done", "wide_ready", "wide_done", "xs_done", "g_ready", "u_ready", "act_done",
             "mid_done", "h_done", "y_ready", "y_done", "x_done"))
        G_BANK, U_BANK, Y_BANK, W_BANK = 0, 2, 4, 6
        block = ctx.enter_context(ph.block())
        UNITS = NCH * NS

        def over(eng, step):
            step(0)
            if n_exp > 2:
                with eng.Fori(1, n_exp // 2) as k:
                    step(k)

        @block.sync
        def _(sp):
            def load(e, i):
                sp.dma_start(wg[i][:], gate_d[:, e, :]).then_inc(w_in[i], 16)
                sp.dma_start(wu[i][:], up_d[:, e, :]).then_inc(w_in[i], 16)
                full = [n for _, n in pieces if n == PMAX]
                sp.dma_start(wd[i][:, 0:len(full), :],
                             down_d[e, 0:PMAX * len(full), :].rearrange("(f p) d -> p f d", p=PMAX)).then_inc(w_in[i], 16)
                if len(full) < NF:
                    at, n = pieces[-1]
                    sp.dma_start(wd[i][0:n, NF - 1, :], down_d[e, at:at + n, :]).then_inc(w_in[i], 16)
                if mode == "bias":
                    gb_d, ub_d, db_d = biases
                    sp.dma_start(gb[i][:], gb_d[e]).then_inc(w_in[i], 16)
                    sp.dma_start(ub[i][:], ub_d[e]).then_inc(w_in[i], 16)
                    sp.dma_start(db[i][:], db_d[e]).then_inc(w_in[i], 16)

            if int_scale is not None:
                sp.dma_start(raw[0][:], gate_d[:, 0, :]).then_inc(w_in[0], 16)
                sp.dma_start(raw[1][:], up_d[:, 0, :]).then_inc(w_in[0], 16)
                sp.dma_start(raw[2][:], down_d[0].rearrange("(f p) d -> p f d", p=PMAX)).then_inc(w_in[0], 16)
            else:
                def step(k):
                    for i in range(NS):
                        reach(sp, x_done, k, UNITS, NCH * (i - 1))
                        load(NS * k + i, i)
                over(sp, step)

        @block.tensor
        def _(pe):
            def weights(k, i):
                reach(pe, diag_done, k, NS, i + 1)
                for c in range(NCH):
                    reach(pe, wide_done, k, UNITS, NCH * i + c)
                    nc.tensor.matmul(psum[:, W_BANK, 0:CH], ones[0:RTOK, :],
                                     diag[i][:, 4 * c:4 * c + 4, :].rearrange("p i n -> p (i n)"),
                                     start=True, stop=True).then_inc(wide_ready, 1)

            def down(k, u, f):
                u -= 1
                i = u // NCH % NS
                n = pieces[f][1]
                reach(pe, h_done if mode == "bias" else mid_done, k, UNITS * NF, NF * u + f + 1)
                if f == 0:
                    reach(pe, y_done, k, UNITS, u - 1)
                last = nc.tensor.matmul(psum[:, Y_BANK + u % 2, 0:CH], wd[i][0:n, f, :], hid[u % 2][0:n, f, :],
                                        start=f == 0, stop=f == NF - 1)
                if f == NF - 1:
                    last.then_inc(y_ready, 1)

            def step(k):
                if weighted:
                    weights(k, 0)
                for u in range(UNITS):
                    i, c = u // NCH, u % NCH
                    if c == 0:
                        if int_scale is not None:
                            pe.wait_ge(w_cast, 3)
                        else:
                            pe.wait_ge(w_in[i], (k + 1) * 16 * loads)
                        if mode == "in":
                            reach(pe, xs_done, k, NS, i + 1)
                    if weighted and NS == 2 and u == 2:
                        weights(k, 1)
                    src = xs[i] if mode == "in" else xnT
                    for f, (at, n) in enumerate(pieces):
                        m = NF * u + f
                        reach(pe, act_done, k, UNITS * NF, m - 1)
                        nc.tensor.matmul(psum[0:n, G_BANK + m % 2, 0:CH], wg[i][:, at:at + n],
                                         src[:, c * CH:(c + 1) * CH], start=True, stop=True).then_inc(g_ready, 1)
                        reach(pe, mid_done, k, UNITS * NF, m - 1)
                        nc.tensor.matmul(psum[0:n, U_BANK + m % 2, 0:CH], wu[i][:, at:at + n],
                                         src[:, c * CH:(c + 1) * CH], start=True, stop=True).then_inc(u_ready, 1)
                        if not (isinstance(k, int) and k == 0 and u == 0):
                            down(k, u, f)
            over(pe, step)
            for f in range(NF):
                down(max(n_exp // 2, 1), 0, f)

        @block.scalar
        def _(act):
            def weights(k, i):
                for c in range(NCH):
                    reach(act, wide_ready, k, UNITS, NCH * i + c + 1)
                    if mode == "in":
                        reach(act, xs_done, k, NS, i - 1)
                    else:
                        reach(act, y_done, k, UNITS, NCH * (i - 1))
                    nc.scalar.activation(wide[i][:, c * CH:(c + 1) * CH], psum[:, W_BANK, 0:CH],
                                         ACT.Copy).then_inc(wide_done, 1)

            def step(k):
                if weighted:
                    weights(k, 0)
                for u in range(UNITS):
                    i = u // NCH
                    if weighted and NS == 2 and u == 2:
                        weights(k, 1)
                    for f, (at, n) in enumerate(pieces):
                        m = NF * u + f
                        if mode == "bias":
                            reach(act, g_ready, k, UNITS * NF, m + 1)
                            if u % NCH == 0 and f == 0:
                                act.wait_ge(w_in[i], (k + 1) * 16 * loads)
                            reach(act, mid_done, k, UNITS * NF, m - 1)
                            nc.scalar.activation(act_out[m % 2][0:n, :], psum[0:n, G_BANK + m % 2, 0:CH],
                                                 ACT.Identity, bias=gb[i][0:n, f:f + 1]).then_inc(act_done, 1)
                            reach(act, mid_done, k, UNITS * NF, m + 1)
                            reach(act, y_ready, k, UNITS, u - 1)
                            nc.scalar.activation(hid[u % 2][0:n, f, :], prod[m % 2][0:n, :],
                                                 ACT.Silu).then_inc(h_done, 1)
                        else:
                            reach(act, g_ready, k, UNITS * NF, m + 1)
                            reach(act, mid_done, k, UNITS * NF, m - 1)
                            nc.scalar.activation(act_out[m % 2][0:n, :], psum[0:n, G_BANK + m % 2, 0:CH],
                                                 ACT.Silu).then_inc(act_done, 1)
            over(act, step)

        @block.gpsimd
        def _(pool):
            def step(k):
                for u in range(UNITS):
                    c = u % NCH
                    reach(pool, y_done, k, UNITS, u + 1)
                    reach(pool, x_done, k, UNITS, u)
                    x = xT[:, c * CH:(c + 1) * CH]
                    nc.gpsimd.tensor_tensor(x, x, y[u % 2][:], ALU.add).then_inc(x_done, 1)
            over(pool, step)

        @block.vector
        def _(dve):
            def diagonals(k, i):
                reach(dve, wide_ready, k, UNITS, NCH * (i - 1))
                e = NS * k + i
                c = comb[:, :, e:e + 1] if isinstance(k, int) else comb[:, :, bass.ds(e, 1)]
                nc.vector.tensor_tensor(diag[i][:], ident[0:RTOK, 0:RTOK].unsqueeze(1).broadcast_to([RTOK, NR, RTOK]),
                                        c.broadcast_to([RTOK, NR, RTOK]), ALU.mult).then_inc(diag_done, 1)

            def inputs(k, i):
                reach(dve, wide_done, k, UNITS, NCH * (i + 1))
                reach(dve, u_ready, k, UNITS * NF, NCH * NF * (i - 1))
                nc.vector.tensor_tensor(xs[i][:], xnT[:], wide[i][:], ALU.mult).then_inc(xs_done, 1)

            def outputs(k, u):
                u -= 1
                i, c = u // NCH % NS, u % NCH
                reach(dve, y_ready, k, UNITS, u + 1)
                reach(dve, x_done, k, UNITS, u - 1)
                out, got = y[u % 2][:], psum[:, Y_BANK + u % 2, 0:CH]
                if mode in ("in", "plain"):
                    nc.vector.tensor_copy(out, got).then_inc(y_done, 1)
                else:
                    if c == 0:
                        reach(dve, wide_done, k, UNITS, NCH * (u // NCH + 1))
                    w = wide[i][:, c * CH:(c + 1) * CH]
                    if mode == "bias":
                        nc.vector.scalar_tensor_tensor(out, got, db[i][:], w, ALU.add, ALU.mult).then_inc(y_done, 1)
                    else:
                        nc.vector.tensor_tensor(out, got, w, ALU.mult).then_inc(y_done, 1)

            if int_scale is not None:
                dve.wait_ge(w_in[0], 48)
                for dst, src in ((wg[0], raw[0]), (wu[0], raw[1]), (wd[0], raw[2])):
                    nc.vector.tensor_scalar(dst[:], src[:], int_scale, None, ALU.mult).then_inc(w_cast, 1)

            def step(k):
                if weighted:
                    diagonals(k, 0)
                    if mode == "in":
                        inputs(k, 0)
                for u in range(UNITS):
                    i = u // NCH
                    if weighted and NS == 2 and u == 1:
                        diagonals(k, 1)
                    if mode == "in" and u == 3:
                        inputs(k, 1)
                    for f, (at, n) in enumerate(pieces):
                        m = NF * u + f
                        reach(dve, act_done, k, UNITS * NF, m + 1)
                        reach(dve, u_ready, k, UNITS * NF, m + 1)
                        up = psum[0:n, U_BANK + m % 2, 0:CH]
                        if mode == "bias":
                            if u % NCH == 0 and f == 0:
                                dve.wait_ge(w_in[i], (k + 1) * 16 * loads)
                            reach(dve, h_done, k, UNITS * NF, m - 1)
                            nc.vector.scalar_tensor_tensor(prod[m % 2][0:n, :], up, ub[i][0:n, f:f + 1],
                                                           act_out[m % 2][0:n, :], ALU.add,
                                                           ALU.mult).then_inc(mid_done, 1)
                        else:
                            reach(dve, y_ready, k, UNITS, u - 1)
                            nc.vector.tensor_tensor(hid[u % 2][0:n, f, :], act_out[m % 2][0:n, :], up,
                                                    ALU.mult).then_inc(mid_done, 1)
                    if not (isinstance(k, int) and k == 0 and u == 0):
                        outputs(k, u)
            over(dve, step)
            outputs(max(n_exp // 2, 1), 0)


def build(nc, a, out):
    with ExitStack() as ctx:
        sb = lambda n, s, dt=F32: ctx.enter_context(nc.sbuf_tensor(n, s, dt))
        xT, xnT = sb("xT", [D, T]), sb("xnT", [D, T])
        ident, ones, ones_mean = sb("ident", [D, D]), sb("ones", [D, D]), sb("ones_mean", [D, D])
        heads, iota = sb("heads", [D, H]), sb("iota", [D, E])
        gamma, beta, bo = sb("gamma", [D, 1]), sb("beta", [D, 1]), [sb(f"bo{i}", [D, 1]) for i in range(3)]
        comb = sb("comb", [RTOK, NR, E])
        psum = ctx.enter_context(nc.psum_tensor("psum", [D, 8, 512], F32))
        qx_d = nc.dram_tensor("qx_scratch", (B, D, HQ), F32, kind="Internal").ap()
        ox_d = nc.dram_tensor("ox_scratch", (B, D, HQ), F32, kind="Internal").ap()
        ph = Phases(nc)
        start_in, const_done = ph.semaphore("start_in"), ph.semaphore("const_done")
        col = lambda n: a[n].rearrange("(d o) -> d o", o=1)
        row = lambda n: a[n].rearrange("(o d) -> o d", o=1)

        with ph.block() as block:
            @block.sync
            def _(sp):
                moves = [(xT[:], a["xT"]), (ident[:], a["ident"]), (heads[:], a["heads"]), (iota[:], a["iota"]),
                         (gamma[:], col("L2_xattn_ln_gamma")), (beta[:], col("L2_xattn_ln_beta")),
                         (bo[0][:], col("L1_xattn_bo")), (bo[1][:], col("L2_xattn_b_out")), (bo[2][:], col("L3_xattn_bo"))]
                for dst, src in moves:
                    sp.dma_start(dst, src).then_inc(start_in, 16)
                sp.wait_ge(start_in, 16 * len(moves))

            @block.vector
            def _(dve):
                nc.vector.memset(ones[:], 1.0).then_inc(const_done, 1)
                nc.vector.memset(ones_mean[:], 1.0 / D).then_inc(const_done, 1)

        norm = lambda name: layer_norm(ph, name, xT, xnT, ones_mean, psum)

        norm("n0")
        sigmoid_attention(ph, xT, xnT, a["ctxT"], a["ctx"].rearrange("b (t p) d -> b p t d", p=KT),
                          a["mask"], a["L0_xattn_WqT"], col("L0_xattn_bq"), a["L0_xattn_Wk"], col("L0_xattn_bk"), psum)
        norm("n1")
        router(ph, "r0", xnT, a["L0_ffn_gate_wT"], None, row("L0_ffn_expert_bias"), None, iota, comb, psum)
        experts(ph, "e0", xT, xnT, comb, a["L0_ffn_w1"], a["L0_ffn_w3"], a["L0_ffn_w2"], None,
                [(0, 128), (128, 128), (256, 96)], "in", E, ident, ones, psum)

        norm("n2")
        with nc.sbuf_tensor("w_out1", [D, H, D], F32) as w_out:
            masked_output_weights(ph, "w1", a["L1_xattn_Wo"], heads, w_out)
            head_queries(ph, "q1", xnT, a["L1_xattn_Wq"], col("L1_xattn_bq"), heads, qx_d, psum)
            query_softmax_attention(ph, "a1", a["ctxT"], qx_d, ox_d, a["L1_xattn_Wk"], col("L1_xattn_bk"),
                                    a["L1_xattn_Wv"], row("L1_xattn_bv"), float(D // H) ** -0.5, psum)
            output_projection(ph, "o1", xT, ox_d, w_out, bo[0], psum)
        norm("n3")
        router(ph, "r1", xnT, a["L1_ffn_gate_wT"], row("L1_ffn_gate_b"), None, 1e-20, iota, comb, psum)
        experts(ph, "e1", xT, xnT, comb, a["L1_ffn_gp_wT"], a["L1_ffn_up_wT"], a["L1_ffn_down_wT"],
                (a["L1_ffn_gp_bT"], a["L1_ffn_up_bT"],
                 a["L1_ffn_down_b"].rearrange("e (d o) -> e d o", o=1)),
                [(102 * f, 102) for f in range(4)], "bias", E, ident, ones, psum)

        norm("n4")
        layer_norm(ph, "n4b", xnT, xnT, ones_mean, psum, (gamma[:], beta[:]))
        with nc.sbuf_tensor("w_out2", [D, H, D], F32) as w_out:
            with nc.sbuf_tensor("w_in2", [D, H, D], F32) as w_in:
                folded_weights(ph, a["L2_xattn_w_qT"], a["L2_xattn_w_kT"], a["L2_xattn_w_vT"], a["L2_xattn_w_out"],
                               a["L2_xattn_gate"].rearrange("(o d) -> o d", o=1), bo[1], w_in, w_out, psum)
                folded_queries(ph, xnT, w_in, qx_d, psum)
            key_softmax_attention(ph, "a2", a["ctxT"], a["ctx"].rearrange("b (t p) d -> b p t d", p=KT), qx_d, ox_d,
                                  None, 64.0 ** -0.5, ident, psum)
            output_projection(ph, "o2", xT, ox_d, w_out, bo[1], psum)
        norm("n5")
        experts(ph, "e2", xT, xnT, None, a["L2_ffn_w_gateT"], a["L2_ffn_w_upT"], a["L2_ffn_w_downT"], None,
                [(128 * f, 128) for f in range(3)], "plain", 1, ident, ones, psum, int_scale=1.0 / 127.0)

        norm("n6")
        with nc.sbuf_tensor("w_out3", [D, H, D], F32) as w_out:
            masked_output_weights(ph, "w3", a["L3_xattn_Wo"], heads, w_out)
            head_queries(ph, "q3", xnT, a["L3_xattn_Wq"], col("L3_xattn_bq"), heads, qx_d, psum)
            key_softmax_attention(ph, "a3", a["ctxT"], None, qx_d, ox_d,
                                  (a["L3_xattn_Wk"], col("L3_xattn_bk"), a["L3_xattn_Wv"], row("L3_xattn_bv")),
                                  float(D // H) ** -0.5, ident, psum)
            output_projection(ph, "o3", xT, ox_d, w_out, bo[2], psum)
        norm("n7")
        router(ph, "r3", xnT, a["L3_ffn_gate_wT"], None, None, 0.0, iota, comb, psum)
        experts(ph, "e3", xT, xnT, comb, a["L3_ffn_gateT"], a["L3_ffn_upT"], a["L3_ffn_down_projT"], None,
                [(128 * f, 128) for f in range(4)], "out", E, ident, ones, psum)

        out_done = ph.semaphore("out_done")
        with ph.block() as block:
            @block.sync
            def _(sp):
                sp.dma_start(out, xT[:]).then_inc(out_done, 16)
                sp.wait_ge(out_done, 16)


def kernel(**inputs):
    import numpy as np
    import concourse.bacc as bacc
    from concourse.bass_utils import run_bass_kernel_spmd

    i = {n: np.asarray(x) for n, x in inputs.items()}
    a = {
        "xT": i["x"].reshape(T, D).T, "ctx": i["ctx_1024"], "ctxT": i["ctx_1024"].transpose(0, 2, 1),
        "mask": i["mask_BxS2_ik1"].reshape(B, NT, KT).transpose(2, 0, 1),
        "ident": np.eye(D, dtype=np.float32),
        "heads": np.repeat(np.eye(H, dtype=np.float32), D // H, axis=0),
        "iota": np.tile(np.arange(E, dtype=np.float32), (D, 1)),
        "L0_xattn_WqT": i["L0_xattn_Wq"].T, "L0_ffn_gate_wT": i["L0_ffn_gate_w"].T,
        "L0_ffn_w1": i["L0_ffn_w1"].transpose(1, 0, 2), "L0_ffn_w3": i["L0_ffn_w3"].transpose(1, 0, 2),
        "L0_ffn_w2": i["L0_ffn_w2"],
        "L1_ffn_gate_wT": i["L1_ffn_gate_w"].T,
        "L1_ffn_gp_wT": i["L1_ffn_gp_w"].transpose(2, 0, 1), "L1_ffn_up_wT": i["L1_ffn_up_w"].transpose(2, 0, 1),
        "L1_ffn_down_wT": i["L1_ffn_down_w"].transpose(0, 2, 1),
        "L1_ffn_gp_bT": i["L1_ffn_gp_b"].reshape(E, 4, 102).transpose(0, 2, 1),
        "L1_ffn_up_bT": i["L1_ffn_up_b"].reshape(E, 4, 102).transpose(0, 2, 1),
        "L2_xattn_w_qT": i["L2_xattn_w_q"].T, "L2_xattn_w_kT": i["L2_xattn_w_kv"][:, :1024].T,
        "L2_xattn_w_vT": i["L2_xattn_w_kv"][:, 1024:].T,
        "L2_ffn_w_gateT": i["L2_ffn_w_gate"].T[:, None], "L2_ffn_w_upT": i["L2_ffn_w_up"].T[:, None],
        "L2_ffn_w_downT": i["L2_ffn_w_down"].T[None],
        "L3_ffn_gate_wT": i["L3_ffn_gate_w"].T,
        "L3_ffn_gateT": i["L3_ffn_gate_up_proj"][:, :512].transpose(2, 0, 1),
        "L3_ffn_upT": i["L3_ffn_gate_up_proj"][:, 512:].transpose(2, 0, 1),
        "L3_ffn_down_projT": i["L3_ffn_down_proj"].transpose(0, 2, 1),
    }
    for n in ("L0_xattn_bq", "L0_xattn_Wk", "L0_xattn_bk", "L0_ffn_expert_bias", "L1_xattn_Wq", "L1_xattn_bq",
              "L1_xattn_Wk", "L1_xattn_bk", "L1_xattn_Wv", "L1_xattn_bv", "L1_xattn_Wo", "L1_xattn_bo",
              "L1_ffn_gate_b", "L1_ffn_down_b", "L2_xattn_ln_gamma",
              "L2_xattn_ln_beta", "L2_xattn_w_out", "L2_xattn_b_out", "L2_xattn_gate", "L3_xattn_Wq", "L3_xattn_bq",
              "L3_xattn_Wk", "L3_xattn_bk", "L3_xattn_Wv", "L3_xattn_bv", "L3_xattn_Wo", "L3_xattn_bo"):
        a[n] = i[n]
    nc = bacc.Bacc("TRN2", target_bir_lowering=False, num_devices=1)
    arrays, aps = {}, {}
    for n, x in a.items():
        arrays[f"in_{n}"] = np.ascontiguousarray(x)
        aps[n] = nc.dram_tensor(f"in_{n}", x.shape, mybir.dt.from_np(x.dtype), kind="ExternalInput").ap()
    out = nc.dram_tensor("out_xT", (D, T), F32, kind="ExternalOutput").ap()
    build(nc, aps, out)
    r = run_bass_kernel_spmd(nc, [arrays], core_ids=[0])
    return np.ascontiguousarray(r.results[0]["out_xT"].T).reshape(B, LQ, D)
```

```python
import math
from contextlib import ExitStack, contextmanager

import concourse.bass as bass
from concourse import mybir

F32 = mybir.dt.float32
F16 = mybir.dt.float16
BF16 = mybir.dt.bfloat16
I32 = mybir.dt.int32
U32 = mybir.dt.uint32
ALU = mybir.AluOpType
ACT = mybir.ActivationFunctionType
AX = mybir.AxisListType

D = 128
B, LQ, LK = 32, 56, 1500
T = B * LQ
CH = 448
NCH = T // CH
CB = CH // LQ
KT = 125
NT = LK // KT
H = 16
HQ = H * LQ
HALF = HQ // 2
RT = HQ // 128
NPAIR = B // 2
E = 8
RTOK = 112
NR = T // RTOK
EPS = 1e-5


def reach(eng, sem, k, per, off):
    if isinstance(k, int):
        if per * k + off > 0:
            eng.wait_ge(sem, per * k + off)
    else:
        assert per + off >= 0
        eng.wait_ge(sem, k * per + off)


def over_pairs(eng, step):
    step(0)
    with eng.Fori(1, NPAIR - 1) as k:
        step(k)
    step(NPAIR - 1)


def samples(k):
    for j in range(2):
        yield j, isinstance(k, int) and k == 0 and j == 0, isinstance(k, int) and k == NPAIR - 1 and j == 1


class Phases:

    def __init__(self, nc):
        self.nc, self.own, self.before = nc, [], []
        self.own_held, self.before_held = ExitStack(), ExitStack()

    def semaphore(self, name):
        self.own.append(self.own_held.enter_context(self.nc.semaphore(name)))
        return self.own[-1]

    @contextmanager
    def block(self):
        with self.nc.Block() as block:
            @block.gpsimd
            def _(pool):
                for s in self.before:
                    pool.sem_clear(s)
            yield block
        self.before_held.close()
        self.before, self.before_held = self.own, self.own_held
        self.own, self.own_held = [], ExitStack()


def layer_norm(ph, name, src, dst, ones_mean, psum, affine=None):
    nc = ph.nc
    with ExitStack() as ctx:
        cen = ctx.enter_context(nc.sbuf_tensor(f"{name}_cen", [D, NCH, CH], F32))
        sq = ctx.enter_context(nc.sbuf_tensor(f"{name}_sq", [D, NCH, CH], F32))
        sem = lambda n: ph.semaphore(f"{name}_{n}")
        mean_ready, centred, squared, var_ready, rooted, inverted, scaled, done = map(
            sem, ("mean_ready", "centred", "squared", "var_ready", "rooted", "inverted", "scaled", "done"))
        block = ctx.enter_context(ph.block())

        @block.tensor
        def _(pe):
            for c in range(NCH):
                nc.tensor.matmul(psum[:, c, 0:CH], ones_mean[:], src[:, c * CH:(c + 1) * CH],
                                 start=True, stop=True).then_inc(mean_ready, 1)
            for c in range(NCH):
                pe.wait_ge(squared, c + 1)
                nc.tensor.matmul(psum[:, 4 + c, 0:CH], ones_mean[:], sq[:, c, :],
                                 start=True, stop=True).then_inc(var_ready, 1)

        @block.scalar
        def _(act):
            for c in range(NCH):
                act.wait_ge(centred, c + 1)
                nc.scalar.activation(sq[:, c, :], cen[:, c, :], ACT.Square).then_inc(squared, 1)
            for c in range(NCH):
                act.wait_ge(inverted, c + 1)
                nc.scalar.activation(sq[:, c, :], sq[:, c, :], ACT.Sqrt).then_inc(rooted, 1)

        @block.vector
        def _(dve):
            for c in range(NCH):
                dve.wait_ge(mean_ready, c + 1)
                nc.vector.tensor_tensor(cen[:, c, :], src[:, c * CH:(c + 1) * CH], psum[:, c, 0:CH],
                                        ALU.subtract).then_inc(centred, 1)
            for c in range(NCH):
                dve.wait_ge(var_ready, c + 1)
                nc.vector.tensor_scalar(sq[:, c, :], psum[:, 4 + c, 0:CH], EPS, None,
                                        ALU.add).then_inc(scaled, 1)
                dve.wait_ge(scaled, c + 1)
                nc.vector.reciprocal(sq[:, c, :], sq[:, c, :]).then_inc(inverted, 1)
            for c in range(NCH):
                dve.wait_ge(rooted, c + 1)
                nc.vector.tensor_tensor(dst[:, c * CH:(c + 1) * CH], cen[:, c, :], sq[:, c, :],
                                        ALU.mult).then_inc(done, 1)
            if affine is not None:
                gamma, beta = affine
                dve.wait_ge(done, NCH)
                nc.vector.tensor_scalar(dst[:], dst[:], gamma, beta, ALU.mult, ALU.add).then_inc(done, 1)


def sigmoid_attention(ph, xT, xnT, ctxT_d, ctx_d, mask_d, wqT_d, bq_d, wk_d, bk_d, ident, psum):
    SCALE = float(D) ** -0.5
    DK = 64
    nc = ph.nc
    with ExitStack() as ctx:
        sb = lambda n, s, dt=F32: ctx.enter_context(nc.sbuf_tensor(f"sa_{n}", s, dt))
        sem = lambda n: ph.semaphore(f"sa_{n}")
        wqT, wk, bq, bk = sb("wqT", [D, DK]), sb("wk", [DK, D]), sb("bq", [DK, 1]), sb("bk", [DK, 1])
        masked = sb("masked", [KT, B, NT], I32)
        keep = sb("keep", [KT, B, NT])
        qT, qkT, qb = sb("qT", [DK, T]), sb("qkT", [D, T]), sb("qb", [LQ, B])
        qk, bias = [sb(f"qk{i}", [D, LQ]) for i in range(2)], [sb(f"bias{i}", [LQ, 1]) for i in range(2)]
        ctxT = [sb(f"ctxT{i}", [D, LK]) for i in range(2)]
        cx = [sb(f"cx{i}", [KT, NT, D]) for i in range(2)]
        sig = [sb(f"sig{i}", [D, LK]) for i in range(2)]
        alpha = [sb(f"alpha{i}", [KT, NT, LQ]) for i in range(2)]
        y = [sb(f"y{i}", [D, D]) for i in range(2)]
        weights_in, mask_in, keep_done, cleared = sem("weights_in"), sem("mask_in"), sem("keep_done"), sem("cleared")
        q_ready, q_done, qk_ready, qk_done, qb_ready, qb_done = map(
            sem, ("q_ready", "q_done", "qk_ready", "qk_done", "qb_ready", "qb_done"))
        ctxT_in = [sem(f"ctxT_in{i}") for i in range(2)]
        cx_in = [sem(f"cx_in{i}") for i in range(2)]
        picked, s_ready, sig_done, sigT_ready, alpha_done, o_ready, y_done, yT_ready, x_done = map(
            sem, ("picked", "s_ready", "sig_done", "sigT_ready", "alpha_done", "o_ready", "y_done", "yT_ready",
                  "x_done"))
        S_BANKS, T_BANKS, O_BANK, Y_BANK = slice(0, 3), slice(3, 6), 6, 7
        block = ctx.enter_context(ph.block())

        @block.sync
        def _(sp):
            sp.dma_start(wqT[:], wqT_d).then_inc(weights_in, 16)
            sp.dma_start(wk[:], wk_d).then_inc(weights_in, 16)
            sp.dma_start(bq[:], bq_d).then_inc(weights_in, 16)
            sp.dma_start(bk[:], bk_d).then_inc(weights_in, 16)
            sp.dma_start(ctxT[0][:], ctxT_d[0]).then_inc(ctxT_in[0], 16)
            sp.dma_start(masked[:], mask_d).then_inc(mask_in, 16)
            sp.dma_start(ctxT[1][:], ctxT_d[1]).then_inc(ctxT_in[1], 16)
            sp.dma_start(cx[0][:], ctx_d[0]).then_inc(cx_in[0], 16)

            def step(k):
                for j, _, last in samples(k):
                    if not (isinstance(k, int) and k == NPAIR - 1):
                        reach(sp, s_ready, k, 2, j + 1)
                        sp.dma_start(ctxT[j][:], ctxT_d[2 * k + j + 2]).then_inc(ctxT_in[j], 16)
                    if not last:
                        reach(sp, o_ready, k, 2, j)
                        sp.dma_start(cx[1 - j][:], ctx_d[2 * k + j + 1]).then_inc(cx_in[1 - j], 16)
            over_pairs(sp, step)

        @block.tensor
        def _(pe):
            pe.wait_ge(weights_in, 64)
            for c in range(NCH):
                nc.tensor.matmul(psum[0:DK, c, 0:CH], wqT[:], xnT[:, c * CH:(c + 1) * CH],
                                 start=True, stop=True).then_inc(q_ready, 1)
            for c in range(NCH):
                pe.wait_ge(q_done, c + 1)
                nc.tensor.matmul(psum[:, 4 + c, 0:CH], wk[:], qT[:, c * CH:(c + 1) * CH],
                                 start=True, stop=True).then_inc(qk_ready, 1)
            for b in range(B):
                last = nc.tensor.matmul(psum[0:LQ, 0, b:b + 1], qT[:, b * LQ:(b + 1) * LQ], bk[:],
                                        start=True, stop=True)
            last.then_inc(qb_ready, 1)
            pe.wait_ge(qk_done, NCH)
            pe.wait_ge(qb_done, 1)

            def transposes(k, j):
                i = 1 - j
                reach(pe, sig_done, k, 2, j)
                reach(pe, alpha_done, k, 2, j - 1)
                for t in range(NT):
                    last = nc.tensor.transpose(psum[0:KT, T_BANKS.start + t // 4, t % 4 * D:(t % 4 + 1) * D],
                                               sig[i][:, t * KT:(t + 1) * KT], ident[:])
                last.then_inc(sigT_ready, 1)

            def scores(k, j):
                pe.wait_ge(ctxT_in[j], (k + 1) * 16)
                reach(pe, picked, k, 4, 2 * (j + 1))
                reach(pe, sig_done, k, 2, j)
                for m in range(3):
                    last = nc.tensor.matmul(psum[0:LQ, m, 0:500], qk[j][:], ctxT[j][:, m * 500:(m + 1) * 500],
                                            start=True, stop=True)
                last.then_inc(s_ready, 1)

            def turn(k, j):
                reach(pe, y_done, k, 2, j - 1)
                reach(pe, x_done, k, 2, j - 2)
                nc.tensor.transpose(psum[:, Y_BANK, 0:D], y[j][:], ident[:]).then_inc(yT_ready, 1)

            def output(k, j):
                i = 1 - j
                reach(pe, alpha_done, k, 2, j)
                pe.wait_ge(cx_in[i], (k + j) * 16)
                reach(pe, y_done, k, 2, j - 1)
                for t in range(NT):
                    last = nc.tensor.matmul(psum[0:LQ, O_BANK, 0:D], alpha[i][:, t, :], cx[i][:, t, :],
                                            start=t == 0, stop=t == NT - 1)
                last.then_inc(o_ready, 1)

            def step(k):
                for j, first, _ in samples(k):
                    if not first:
                        transposes(k, j)
                    scores(k, j)
                    if not (isinstance(k, int) and k == 0):
                        turn(k, j)
                    if not first:
                        output(k, j)
            over_pairs(pe, step)
            transposes(NPAIR, 0)
            turn(NPAIR, 0)
            output(NPAIR, 0)
            turn(NPAIR, 1)

        @block.scalar
        def _(act):
            for c in range(NCH):
                act.wait_ge(q_ready, c + 1)
                nc.scalar.activation(qT[:, c * CH:(c + 1) * CH], psum[0:DK, c, 0:CH], ACT.Identity,
                                     bias=bq[:]).then_inc(q_done, 1)

            act.wait_ge(cleared, 4)

            def leave(k, j):
                i = 1 - j
                reach(act, o_ready, k, 2, j)
                reach(act, yT_ready, k, 2, j - 2)
                nc.scalar.activation(y[i][0:LQ, :], psum[0:LQ, O_BANK, 0:D], ACT.Copy).then_inc(y_done, 1)

            def step(k):
                for j, first, _ in samples(k):
                    reach(act, s_ready, k, 2, j + 1)
                    reach(act, sigT_ready, k, 2, j - 1)
                    nc.scalar.activation(
                        sig[j][0:LQ, :].rearrange("q (a n) -> q a n", a=3), psum[0:LQ, S_BANKS, 0:500],
                        ACT.Sigmoid, bias=bias[j][:], scale=SCALE).then_inc(sig_done, 1)
                    if not first:
                        leave(k, j)
            over_pairs(act, step)
            leave(NPAIR, 0)

        @block.vector
        def _(dve):
            for i in range(2):
                nc.vector.memset(y[i][:], 0.0).then_inc(cleared, 1)
                nc.vector.memset(sig[i][:], 0.0).then_inc(cleared, 1)
            dve.wait_ge(mask_in, 16)
            nc.vector.tensor_scalar(keep[:], masked[:], 1.0, None, ALU.not_equal).then_inc(keep_done, 1)
            for c in range(NCH):
                dve.wait_ge(qk_ready, c + 1)
                nc.vector.tensor_copy(qkT[:, c * CH:(c + 1) * CH], psum[:, 4 + c, 0:CH]).then_inc(qk_done, 1)
            dve.wait_ge(qb_ready, 1)
            nc.vector.tensor_scalar(qb[:], psum[0:LQ, 0, 0:B], SCALE, None, ALU.mult).then_inc(qb_done, 1)
            dve.wait_ge(qk_done, NCH)
            dve.wait_ge(qb_done, 1)
            dve.wait_ge(keep_done, 1)

            def pick(k, j):
                b = 2 * k + j
                nc.vector.tensor_copy(qk[j][:], qkT[:, bass.ds(b * LQ, LQ)]).then_inc(picked, 1)
                nc.vector.tensor_copy(bias[j][:], qb[:, bass.ds(b, 1)]).then_inc(picked, 1)

            def mask(k, j):
                i = 1 - j
                b = 2 * k + j - 1
                reach(dve, sigT_ready, k, 2, j)
                reach(dve, o_ready, k, 2, j - 2)
                split = lambda x: x.rearrange("p (a t) q -> p a t q", a=3)
                nc.vector.tensor_tensor(
                    split(alpha[i][:]), psum[0:KT, T_BANKS, :].rearrange("p a (t q) -> p a t q", t=4)[:, :, :, 0:LQ],
                    split(keep[:, b, :].unsqueeze(2).broadcast_to([KT, NT, LQ])), ALU.mult).then_inc(alpha_done, 1)

            def add(k, j):
                reach(dve, yT_ready, k, 2, j - 1)
                x = xT[:, bass.ds((2 * k + j - 2) * LQ, LQ)]
                nc.vector.tensor_tensor(x, x, psum[:, Y_BANK, 0:LQ], ALU.add).then_inc(x_done, 1)

            pick(0, 0)

            def step(k):
                for j, first, last in samples(k):
                    if not first:
                        mask(k, j)
                    if not last:
                        reach(dve, s_ready, k, 2, j)
                        reach(dve, sig_done, k, 2, j)
                        pick(*((k, 1) if j == 0 else (k + 1, 0)))
                    if not (isinstance(k, int) and k == 0):
                        add(k, j)
            over_pairs(dve, step)
            mask(NPAIR, 0)
            add(NPAIR, 0)
            add(NPAIR, 1)


TERMS = 4
GH = H // TERMS
GQ = GH * LQ
DH = D // H


def head_queries(ph, name, xnT, wq_d, bq_d, own, qx_d, psum):
    nc = ph.nc
    with ExitStack() as ctx:
        sb = lambda n, s, dt=F32: ctx.enter_context(nc.sbuf_tensor(f"{name}_{n}", s, dt))
        sem = lambda n: ph.semaphore(f"{name}_{n}")
        wq, bq, qT = sb("wq", [D, D]), sb("bq", [D, 1]), sb("qT", [D, T])
        part = [sb("hi", [D, T], F16), sb("lo", [D, T], F16)]
        stack = sb("stack", [D, TERMS, T], F16)
        stage = [sb(f"stage{i}", [D, CB, TERMS, GH, LQ], F16) for i in range(2)]
        weights_in, q_ready, q_done, hi_done, lo_done, stacked, staged = map(
            sem, ("weights_in", "q_ready", "q_done", "hi_done", "lo_done", "stacked", "staged"))
        stored = [sem(f"stored{i}") for i in range(2)]
        block = ctx.enter_context(ph.block())

        @block.sync
        def _(sp):
            sp.dma_start(wq[:], wq_d).then_inc(weights_in, 16)
            sp.dma_start(bq[:], bq_d).then_inc(weights_in, 16)
            sp.wait_ge(hi_done, NCH)
            sp.wait_ge(lo_done, NCH)
            for term in range(TERMS):
                for g in range(TERMS):
                    sp.dma_start(stack[32 * term:32 * term + 32, g, :],
                                 part[term % 2][32 * g:32 * g + 32, :]).then_inc(stacked, 16)
            for c in range(NCH):
                sp.wait_ge(staged, GH * (c + 1))
                sp.dma_start(qx_d[c * CB:(c + 1) * CB].rearrange("b p n -> p b n"),
                             stage[c % 2][:].rearrange("p b g h q -> p b (g h q)")).then_inc(stored[c % 2], 16)
            for i in range(2):
                sp.wait_ge(stored[i], 16 * (NCH // 2))

        @block.tensor
        def _(pe):
            pe.wait_ge(weights_in, 32)
            for c in range(NCH):
                nc.tensor.matmul(psum[:, c, 0:CH], wq[:], xnT[:, c * CH:(c + 1) * CH],
                                 start=True, stop=True).then_inc(q_ready, 1)

        @block.scalar
        def _(act):
            for c in range(NCH):
                act.wait_ge(q_ready, c + 1)
                nc.scalar.activation(part[0][:, c * CH:(c + 1) * CH], psum[:, c, 0:CH], ACT.Identity,
                                     bias=bq[:]).then_inc(hi_done, 1)

        @block.vector
        def _(dve):
            for c in range(NCH):
                dve.wait_ge(hi_done, c + 1)
                nc.vector.scalar_tensor_tensor(part[1][:, c * CH:(c + 1) * CH], psum[:, c, 0:CH], bq[:],
                                               part[0][:, c * CH:(c + 1) * CH], ALU.add,
                                               ALU.subtract).then_inc(lo_done, 1)
            dve.wait_ge(stacked, 16 * TERMS * TERMS)
            for c in range(NCH):
                if c >= 2:
                    dve.wait_ge(stored[c % 2], 16 * (c // 2))
                for h in range(GH):
                    nc.vector.tensor_scalar(
                        stage[c % 2][:, :, :, h, :],
                        stack[:, :, c * CH:(c + 1) * CH].rearrange("p g (b q) -> p b g q", b=CB),
                        own[:, h:h + 1], None, ALU.mult).then_inc(staged, 1)


def folded_weights(ph, wqT_d, wkT_d, wvT_d, wo_d, gate_d, bo, w_in, w_out, psum):
    DH = 64
    nc = ph.nc
    with ExitStack() as ctx:
        sb = lambda n, s: ctx.enter_context(nc.sbuf_tensor(f"fw_{n}", s, F32))
        sem = lambda n: ph.semaphore(f"fw_{n}")
        wqT, wkT, wvT, wo = (sb(n, [DH, H, D]) for n in ("wqT", "wkT", "wvT", "wo"))
        gate, tanh = sb("gate", [D, 1]), sb("tanh", [D, 1])
        weights_in, gate_in, tanh_done, m_ready, m_done = map(
            sem, ("weights_in", "gate_in", "tanh_done", "m_ready", "m_done"))
        block = ctx.enter_context(ph.block())
        NG = 2 * H // 4

        @block.sync
        def _(sp):
            sp.dma_start(gate[:], gate_d.broadcast_to([D, 1])).then_inc(gate_in, 16)
            for dst, src in ((wqT, wqT_d), (wkT, wkT_d), (wvT, wvT_d), (wo, wo_d)):
                sp.dma_start(dst[:], src.rearrange("(h e) d -> e h d", h=H)).then_inc(weights_in, 16)

        @block.tensor
        def _(pe):
            pe.wait_ge(weights_in, 64)
            for g in range(NG):
                left, right = (wqT, wkT) if g < NG // 2 else (wvT, wo)
                for i in range(4):
                    h = (4 * g + i) % H
                    last = nc.tensor.matmul(psum[:, g, i * D:(i + 1) * D], left[:, h, :], right[:, h, :],
                                            start=True, stop=True)
                last.then_inc(m_ready, 1)

        @block.scalar
        def _(act):
            act.wait_ge(gate_in, 16)
            nc.scalar.activation(tanh[:], gate[:], ACT.Tanh).then_inc(tanh_done, 1)

        @block.vector
        def _(dve):
            for g in range(NG // 2):
                dve.wait_ge(m_ready, g + 1)
                nc.vector.tensor_copy(w_in[:, 4 * g:4 * g + 4, :],
                                      psum[:, g, :].rearrange("p (h d) -> p h d", h=4)).then_inc(m_done, 1)
            dve.wait_ge(tanh_done, 1)
            nc.vector.tensor_scalar(bo[:], bo[:], tanh[:], None, ALU.mult).then_inc(m_done, 1)
            for g in range(NG // 2):
                dve.wait_ge(m_ready, NG // 2 + g + 1)
                nc.vector.tensor_scalar(w_out[:, 4 * g:4 * g + 4, :],
                                        psum[:, NG // 2 + g, :].rearrange("p (h d) -> p h d", h=4),
                                        tanh[:], None, ALU.mult).then_inc(m_done, 1)


def folded_queries(ph, xnT, w_in, qx2_d, psum):
    nc = ph.nc
    with ExitStack() as ctx:
        stage = [ctx.enter_context(nc.sbuf_tensor(f"fq_stage{i}", [D, CB, 2, H, LQ], F16)) for i in range(2)]
        sem = lambda n: ph.semaphore(f"fq_{n}")
        ready, hi_done, lo_done = sem("ready"), sem("hi_done"), sem("lo_done")
        stored = [sem(f"stored{i}") for i in range(2)]
        block = ctx.enter_context(ph.block())

        def chunk(n):
            return psum[:, n % 8, 0:CH].rearrange("p (b q) -> p b q", b=CB)

        @block.sync
        def _(sp):
            for c in range(NCH):
                sp.wait_ge(lo_done, H * (c + 1))
                sp.dma_start(qx2_d[c * CB:(c + 1) * CB].rearrange("b p n -> p b n"),
                             stage[c % 2][:].rearrange("p b i h q -> p b (i h q)")).then_inc(stored[c % 2], 16)
            for i in range(2):
                sp.wait_ge(stored[i], 16 * (NCH // 2))

        @block.tensor
        def _(pe):
            for c in range(NCH):
                for h in range(H):
                    n = c * H + h
                    if n >= 8:
                        pe.wait_ge(lo_done, n - 7)
                    nc.tensor.matmul(psum[:, n % 8, 0:CH], w_in[:, h, :], xnT[:, c * CH:(c + 1) * CH],
                                     start=True, stop=True).then_inc(ready, 1)

        @block.scalar
        def _(act):
            for c in range(NCH):
                if c >= 2:
                    act.wait_ge(stored[c % 2], 16 * (c // 2))
                for h in range(H):
                    act.wait_ge(ready, c * H + h + 1)
                    nc.scalar.activation(stage[c % 2][:, :, 0, h, :], chunk(c * H + h), ACT.Copy).then_inc(hi_done, 1)

        @block.vector
        def _(dve):
            for c in range(NCH):
                for h in range(H):
                    dve.wait_ge(hi_done, c * H + h + 1)
                    nc.vector.tensor_tensor(stage[c % 2][:, :, 1, h, :], chunk(c * H + h),
                                            stage[c % 2][:, :, 0, h, :], ALU.subtract).then_inc(lo_done, 1)


class Front:

    ITEMS = 6

    def __init__(self, nc, sb, sem, weights, bank):
        self.nc, self.bank, self.weights = nc, bank, weights
        self.wk, self.wv, self.bk, self.bv = sb("wk", [D, D]), sb("wv", [D, D]), sb("bk", [D, 1]), sb("bv", [D, D])
        self.ctxT = [sb(f"ctxT{i}", [D, LK]) for i in range(2)]
        self.k = [[sb(f"k{n}{i}", [D, LK], F16) for n in ("hi", "lo")] for i in range(2)]
        self.ks = [sb(f"ks{i}", [D, TERMS, LK], F16) for i in range(2)]
        self.v = [sb(f"v{i}", [KT, NT, D]) for i in range(2)]
        self.weights_in = sem("weights_in")
        self.ctxT_in = [sem(f"ctxT_in{i}") for i in range(2)]
        self.ks_in = [sem(f"ks_in{i}") for i in range(2)]
        self.ready, self.hi_done, self.free = sem("side_ready"), sem("khi_done"), sem("side_free")

    def load_weights(self, sp):
        wk_d, bk_d, wv_d, bv_d = self.weights
        sp.dma_start(self.wk[:], wk_d).then_inc(self.weights_in, 16)
        sp.dma_start(self.wv[:], wv_d).then_inc(self.weights_in, 16)
        sp.dma_start(self.bk[:], bk_d).then_inc(self.weights_in, 16)
        sp.dma_start(self.bv[:], bv_d.broadcast_to([D, D])).then_inc(self.weights_in, 16)

    def stack(self, sp, k, j):
        reach(sp, self.free, k, 2 * self.ITEMS, self.ITEMS * j + 3)
        for term in range(TERMS):
            for g in range(TERMS):
                sp.dma_start(self.ks[j][32 * term:32 * term + 32, g, :],
                             self.k[j][term // 2][32 * g:32 * g + 32, :]).then_inc(self.ks_in[j], 16)

    def stacked(self, eng, k, j):
        eng.wait_ge(self.ks_in[j], (k + 1) * (16 * TERMS * TERMS))

    def product(self, pe, k, j, i):
        nc = self.nc
        if i == 0:
            pe.wait_ge(self.ctxT_in[j], (k + 1) * 16)
        reach(pe, self.free, k, 2 * self.ITEMS, self.ITEMS * j + i)
        if i < 3:
            nc.tensor.matmul(self.bank[:, 0:500], self.wk[:], self.ctxT[j][:, i * 500:(i + 1) * 500],
                             start=True, stop=True).then_inc(self.ready, 1)
        else:
            for n in range(4):
                t = 4 * (i - 3) + n
                last = nc.tensor.matmul(self.bank[0:KT, n * D:(n + 1) * D],
                                        self.ctxT[j][:, t * KT:(t + 1) * KT], self.wv[:], start=True, stop=True)
            last.then_inc(self.ready, 1)

    def key_hi(self, act, k, j, i):
        reach(act, self.ready, k, 2 * self.ITEMS, self.ITEMS * j + i + 1)
        if not (isinstance(k, int) and k == 0):
            self.stacked(act, k - 1, j)
        self.nc.scalar.activation(self.k[j][0][:, i * 500:(i + 1) * 500], self.bank[:, 0:500], ACT.Identity,
                                  bias=self.bk[:]).then_inc(self.hi_done, 1)

    def key_lo(self, dve, k, j, i):
        reach(dve, self.hi_done, k, 6, 3 * j + i + 1)
        s = slice(i * 500, (i + 1) * 500)
        self.nc.vector.scalar_tensor_tensor(self.k[j][1][:, s], self.bank[:, 0:500], self.bk[:], self.k[j][0][:, s],
                                            ALU.add, ALU.subtract).then_inc(self.free, 1)

    def value(self, dve, k, j, i):
        reach(dve, self.ready, k, 2 * self.ITEMS, self.ITEMS * j + i + 1)
        t = 4 * (i - 3)
        self.nc.vector.tensor_tensor(
            self.v[j][:, t:t + 4, :], self.bank[0:KT, :].rearrange("p (t n) -> p t n", t=4),
            self.bv[0:KT, :].unsqueeze(1).broadcast_to([KT, 4, D]), ALU.add).then_inc(self.free, 1)


def after(k, j):
    return (k, 1) if j == 0 else (k + 1, 0)


def query_softmax_attention(ph, name, ctxT_d, qx_d, ox_d, proj, scale, ident, psum):
    nc = ph.nc
    with ExitStack() as ctx:
        sb = lambda n, s, dt=F32: ctx.enter_context(nc.sbuf_tensor(f"{name}_{n}", s, dt))
        sem = lambda n: ph.semaphore(f"{name}_{n}")
        front = Front(nc, sb, sem, proj, psum[:, 6, :])
        identh = sb("ident", [KT, KT], BF16)
        qx = [sb(f"qx{i}", [D, TERMS, GQ], F16) for i in range(2)]
        ox = [sb(f"ox{i}", [D, HQ]) for i in range(2)]
        p = [sb(f"p{i}", [KT, H, LQ]) for i in range(4)]
        vz = [sb(f"vz{i}", [KT, H, DH]) for i in range(4)]
        ntop = [sb(f"ntop{i}", [KT, H], BF16) for i in range(2)]
        f28 = [sb(f"f28{i}", [KT, H, 28]) for i in range(2)]
        f14 = [sb(f"f14{i}", [KT, H, 14]) for i in range(2)]
        f7 = [sb(f"f7{i}", [KT, H, 7]) for i in range(2)]
        z = [sb(f"z{i}", [KT, H]) for i in range(2)]
        rz = [sb(f"rz{i}", [KT, H]) for i in range(2)]
        qx_in = [sem(f"qx_in{i}") for i in range(2)]
        ox_out = [sem(f"ox_out{i}") for i in range(2)]
        (ident_done, s_ready, top_done, sub_ready, exp_done, half_done, quarter_done, tree_done,
         z_done, rz_done, vz_done, o_ready, o_done) = map(sem, (
             "ident_done", "s_ready", "top_done", "sub_ready", "exp_done", "half_done",
             "quarter_done", "tree_done", "z_done", "rz_done", "vz_done", "o_ready", "o_done"))
        ITEM_AT = {1: 0, 2: 1, 4: 2, 6: 3, 8: 4, 10: 5}
        TOP_BANK, SUB_BANK = 0, 2
        LAG = 4
        block = ctx.enter_context(ph.block())

        @block.sync
        def _(sp):
            front.load_weights(sp)
            for j in range(2):
                sp.dma_start(front.ctxT[j][:], ctxT_d[j]).then_inc(front.ctxT_in[j], 16)
            sp.dma_start(qx[0][:].rearrange("p a n -> p (a n)"), qx_d[0]).then_inc(qx_in[0], 16)
            front.stack(sp, 0, 0)

            def store(k, j):
                reach(sp, o_done, k, 2, j + 1)
                sp.dma_start(ox_d[2 * k + j], ox[j][:]).then_inc(ox_out[j], 16)

            def step(k):
                end = isinstance(k, int) and k == NPAIR - 1
                for j, first, last in samples(k):
                    if not last:
                        kn, jn = after(k, j)
                        reach(sp, sub_ready, k, 2 * NT, NT * j)
                        sp.dma_start(qx[jn][:].rearrange("p a n -> p (a n)"),
                                     qx_d[2 * k + j + 1]).then_inc(qx_in[jn], 16)
                        front.stack(sp, kn, jn)
                    if not end:
                        reach(sp, front.ready, k, 12, 6 * j + 6)
                        sp.dma_start(front.ctxT[j][:], ctxT_d[2 * k + j + 2]).then_inc(front.ctxT_in[j], 16)
                    if not first:
                        store(*((k, 0) if j else (k - 1, 1)))
            over_pairs(sp, step)
            store(NPAIR - 1, 1)
            for i in range(2):
                sp.wait_ge(ox_out[i], 16 * NPAIR)

        @block.tensor
        def _(pe):
            pe.wait_ge(front.weights_in, 64)
            for i in range(6):
                front.product(pe, 0, 0, i)
            pe.wait_ge(ident_done, 1)

            def score(out, j, t, g, **flags):
                return nc.tensor.matmul(out[:, g % 2 * GQ:(g % 2 + 1) * GQ], front.ks[j][:, g, t * KT:(t + 1) * KT],
                                        qx[j][:, g, :], **flags)

            def subtract(k, s):
                s -= 1
                reach(pe, top_done, k, 2 * NT, s + 1)
                j, t = s // NT % 2, s % NT
                reach(pe, exp_done, k, 2 * NT, s)
                for a in range(2):
                    out = psum[0:KT, SUB_BANK + a, :]
                    nc.tensor.matmul(out[:, 0:HALF], identh[:],
                                     ntop[s % 2][:, 8 * a:8 * a + 8].unsqueeze(2).broadcast_to([KT, 8, LQ]),
                                     start=True, stop=False)
                    for g in range(2):
                        last = score(out, j, t, 2 * a + g, start=False, stop=g == 1)
                last.then_inc(sub_ready, 1)

            def output(k, s):
                s -= LAG
                j, t = s // NT % 2, s % NT
                reach(pe, vz_done, k, 2 * NT, s + 1)
                if t == 0:
                    reach(pe, o_done, k, 2, s // NT)
                for a in range(2):
                    last = nc.tensor.matmul(
                        psum[:, 4 + a, 0:HALF], vz[s % 4][:].rearrange("p h d -> p (h d)"),
                        p[s % 4][:, 8 * a:8 * a + 8, :].rearrange("p h q -> p (h q)"),
                        start=t == 0, stop=t == NT - 1)
                last.then_inc(o_ready, 1)

            def step(k):
                for j, first, last_sample in samples(k):
                    for t in range(NT):
                        s = NT * j + t
                        if t == 0:
                            front.stacked(pe, k, j)
                            pe.wait_ge(qx_in[j], (k + 1) * 16)
                        reach(pe, top_done, k, 2 * NT, s)
                        for g in range(TERMS):
                            last = score(psum[0:KT, TOP_BANK + g // 2, :], j, t, g, start=True, stop=True)
                        last.then_inc(s_ready, 1)
                        if not (first and t < 1):
                            subtract(k, s)
                        if not (first and t < LAG):
                            output(k, s)
                        if t in ITEM_AT and not last_sample:
                            front.product(pe, *after(k, j), ITEM_AT[t])
            over_pairs(pe, step)
            for s in range(LAG):
                if s == 0:
                    subtract(NPAIR, s)
                output(NPAIR, s)

        @block.scalar
        def _(act):
            act.wait_ge(front.weights_in, 64)
            for i in range(3):
                front.key_hi(act, 0, 0, i)

            def exponentials(k, s):
                s -= 1
                reach(act, sub_ready, k, 2 * NT, s + 1)
                reach(act, o_ready, k, 2 * NT, s - 3)
                nc.scalar.activation(p[s % 4][:].rearrange("p (a h) q -> p a (h q)", a=2),
                                     psum[0:KT, SUB_BANK:SUB_BANK + 2, 0:HALF], ACT.Exp,
                                     scale=scale).then_inc(exp_done, 1)

            def output(k, j):
                i = 1 - j
                reach(act, o_ready, k, 2 * NT, NT * j)
                reach(act, ox_out[i], k, 16, 16 * (j - 1))
                nc.scalar.activation(ox[i][:].rearrange("p (a n) -> p a n", a=2), psum[:, 4:6, 0:HALF],
                                     ACT.Copy).then_inc(o_done, 1)

            def step(k):
                for j, first, last_sample in samples(k):
                    for t in range(NT):
                        if not (first and t < 1):
                            exponentials(k, NT * j + t)
                        if t == LAG - 1 and not first:
                            output(k, j)
                        if t in ITEM_AT and ITEM_AT[t] < 3 and not last_sample:
                            front.key_hi(act, *after(k, j), ITEM_AT[t])
            over_pairs(act, step)
            exponentials(NPAIR, 0)
            output(NPAIR, 0)

        @block.gpsimd
        def _(pool):
            def step(k):
                for j, _, _ in samples(k):
                    for t in range(NT):
                        s = NT * j + t
                        reach(pool, exp_done, k, 2 * NT, s + 1)
                        pt = p[s % 4]
                        nc.gpsimd.tensor_tensor(f28[s % 2][:], pt[:, :, 0:28], pt[:, :, 28:56],
                                                ALU.add).then_inc(half_done, 1)
                        reach(pool, half_done, k, 2 * NT, s + 1)
                        nc.gpsimd.tensor_tensor(f14[s % 2][:], f28[s % 2][:, :, 0:14], f28[s % 2][:, :, 14:28],
                                                ALU.add).then_inc(quarter_done, 1)
                        reach(pool, quarter_done, k, 2 * NT, s + 1)
                        reach(pool, z_done, k, 2 * NT, s - 1)
                        nc.gpsimd.tensor_tensor(f7[s % 2][:], f14[s % 2][:, :, 0:7], f14[s % 2][:, :, 7:14],
                                                ALU.add).then_inc(tree_done, 1)
            over_pairs(pool, step)

        @block.vector
        def _(dve):
            nc.vector.tensor_copy(identh[:], ident[0:KT, 0:KT]).then_inc(ident_done, 1)
            dve.wait_ge(front.weights_in, 64)
            for i in range(3):
                front.key_lo(dve, 0, 0, i)
            for i in range(3, 6):
                front.value(dve, 0, 0, i)

            def normalise(k, s):
                s -= 3
                j, t = s // NT % 2, s % NT
                reach(dve, tree_done, k, 2 * NT, s + 1)
                nc.vector.tensor_reduce(z[s % 2][:], f7[s % 2][:], AX.X, ALU.add).then_inc(z_done, 1)
                reach(dve, z_done, k, 2 * NT, s + 1)
                nc.vector.reciprocal(rz[s % 2][:], z[s % 2][:]).then_inc(rz_done, 1)
                reach(dve, rz_done, k, 2 * NT, s + 1)
                reach(dve, o_ready, k, 2 * NT, s - 3)
                nc.vector.tensor_tensor(
                    vz[s % 4][:], front.v[j][:, t, :].rearrange("p (h d) -> p h d", h=H),
                    rz[s % 2][:].unsqueeze(2).broadcast_to([KT, H, DH]), ALU.mult).then_inc(vz_done, 1)

            def step(k):
                for j, first, last_sample in samples(k):
                    for t in range(NT):
                        s = NT * j + t
                        reach(dve, s_ready, k, 2 * NT, s + 1)
                        reach(dve, sub_ready, k, 2 * NT, s - 1)
                        nc.vector.tensor_reduce(
                            ntop[s % 2][:].rearrange("p (a h) -> p a h", a=2),
                            psum[0:KT, TOP_BANK:TOP_BANK + 2, 0:HALF].rearrange("p a (h q) -> p a h q", h=H // 2),
                            AX.X, ALU.max, negate=True).then_inc(top_done, 1)
                        if not (first and t < 3):
                            normalise(k, s)
                        if t in ITEM_AT and not last_sample:
                            item = ITEM_AT[t]
                            (front.key_lo if item < 3 else front.value)(dve, *after(k, j), item)
            over_pairs(dve, step)
            for s in range(3):
                normalise(NPAIR, s)


def row_pieces(r):
    pieces, at = [], 0
    while at < 128:
        row = 128 * r + at
        n = min(GQ - row % GQ, 128 - at)
        if at % 64 and n > 32:
            n = 32
        pieces.append((row // GQ, row % GQ, at, n))
        at += n
    return pieces


def key_softmax_attention(ph, name, ctxT_d, ctx_d, qx_d, ox_d, proj, scale, ident, ones, window, psum):
    nc = ph.nc
    LIFT = 12 * math.log(2.0)
    with ExitStack() as ctx:
        sb = lambda n, s, dt=F32: ctx.enter_context(nc.sbuf_tensor(f"{name}_{n}", s, dt))
        sem = lambda n: ph.semaphore(f"{name}_{n}")
        ox = [sb(f"ox{i}", [D, HQ]) for i in range(2)]
        p = [sb(f"p{i}", [D, LK]) for i in range(2)]
        pT = [[sb(f"pT{n}{i}", [KT, NT, D], F16) for n in ("hi", "lo")] for i in range(2)]
        vs = [[sb(f"v{n}{i}", [KT, NT, D], F16) for n in ("hi", "lo")] for i in range(2)]
        a = sb("a", [D, RT, D])
        top, shift, z, rz = (sb(n, [D, 2 * RT]) for n in ("top", "shift", "z", "rz"))
        qx_in = [sem(f"qx_in{i}") for i in range(2)]
        v_in = [sem(f"v_in{i}") for i in range(2)]
        ox_out = [sem(f"ox_out{i}") for i in range(2)]
        t_ready, hi_done, lo_done = ([sem(f"{n}{i}") for i in range(3)] for n in ("t_ready", "hi_done", "lo_done"))
        (cleared, s_ready, top_done, shift_done, exp_done, rz_done, o_ready, a_done, aT_ready, aT_done,
         vhi_done, vlo_done, ctx_hi_done, ctx_lo_done) = map(sem, (
             "cleared", "s_ready", "top_done", "shift_done", "exp_done", "rz_done", "o_ready", "a_done",
             "aT_ready", "aT_done", "vhi_done", "vlo_done", "ctx_hi_done", "ctx_lo_done"))
        S_BANKS, T_BANK, O_BANK, SIDE = slice(0, 3), 3, 6, 7
        if proj:
            front = Front(nc, sb, sem, proj, psum[:, SIDE, :])
            qx = [sb(f"qx{i}", [D, TERMS, GQ], F16) for i in range(2)]
        else:
            front = None
            qx = [sb(f"qx{i}", [D, 2, HQ], F16) for i in range(2)]
            ctxT, cx = [sb(f"ctxT{i}", [D, LK]) for i in range(2)], [sb(f"cx{i}", [KT, NT, D]) for i in range(2)]
            ctxT_in = [sem(f"ctxT_in{i}") for i in range(2)]
            cT = [[sb(f"cT{n}{i}", [D, LK], F16) for n in ("hi", "lo")] for i in range(2)]
        ITEM_AT = {(0, 0): 0, (0, 1): 1, (1, 0): 2, (2, 0): 3, (3, 0): 4, (4, 0): 5} if proj else {}
        block = ctx.enter_context(ph.block())

        def cols(r):
            return slice(128 * r // LQ * DH, min(128 * r // LQ * DH + 32, D)) if proj else slice(0, D)

        @block.sync
        def _(sp):
            sp.dma_start(qx[0][:].rearrange("p a n -> p (a n)"), qx_d[0]).then_inc(qx_in[0], 16)
            if proj:
                front.load_weights(sp)
                for j in range(2):
                    sp.dma_start(front.ctxT[j][:], ctxT_d[j]).then_inc(front.ctxT_in[j], 16)
                front.stack(sp, 0, 0)
            else:
                for j in range(2):
                    sp.dma_start(ctxT[j][:], ctxT_d[j]).then_inc(ctxT_in[j], 16)
                    sp.dma_start(cx[j][:], ctx_d[j]).then_inc(v_in[j], 16)

            def store(k, j):
                reach(sp, aT_done, k, 2 * RT, RT * (j + 1))
                sp.dma_start(ox_d[2 * k + j], ox[j][:]).then_inc(ox_out[j], 16)

            def step(k):
                end = isinstance(k, int) and k == NPAIR - 1
                for j, first, last in samples(k):
                    jn = 1 - j
                    if not last:
                        reach(sp, s_ready, k, 2 * RT, RT * j)
                        sp.dma_start(qx[jn][:].rearrange("p a n -> p (a n)"),
                                     qx_d[2 * k + j + 1]).then_inc(qx_in[jn], 16)
                        if proj:
                            front.stack(sp, *after(k, j))
                    if not end:
                        if proj:
                            reach(sp, front.ready, k, 12, 6 * j + 6)
                            sp.dma_start(front.ctxT[j][:], ctxT_d[2 * k + j + 2]).then_inc(front.ctxT_in[j], 16)
                        else:
                            reach(sp, ctx_lo_done, k, 2, j + 1)
                            sp.dma_start(ctxT[j][:], ctxT_d[2 * k + j + 2]).then_inc(ctxT_in[j], 16)
                            reach(sp, vlo_done, k, 2, j + 1)
                            sp.dma_start(cx[j][:], ctx_d[2 * k + j + 2]).then_inc(v_in[j], 16)
                    if not first:
                        store(*((k, 0) if j else (k - 1, 1)))
            over_pairs(sp, step)
            store(NPAIR - 1, 1)
            for i in range(2):
                sp.wait_ge(ox_out[i], 16 * NPAIR)

        @block.gpsimd
        def _(pool):
            def split_values(k, j, i):
                reach(pool, front.free, k, 12, 6 * j + 4 + i)
                reach(pool, o_ready, k, 2 * RT, RT * (j - 1))
                t = slice(4 * i, 4 * i + 4)
                nc.gpsimd.tensor_tensor(vs[j][0][:, t, :], front.v[j][:, t, :],
                                        ones[0:KT, :].unsqueeze(1).broadcast_to([KT, 4, D]), ALU.mult).then_inc(vhi_done, 1)
                reach(pool, vhi_done, k, 6, 3 * j + i + 1)
                nc.gpsimd.tensor_tensor(vs[j][1][:, t, :], front.v[j][:, t, :], vs[j][0][:, t, :],
                                        ALU.subtract).then_inc(vlo_done, 1)

            def split_context(k, j):
                pool.wait_ge(ctxT_in[j], (k + 1) * 16)
                reach(pool, s_ready, k, 2 * RT, RT * (j - 1))
                nc.gpsimd.tensor_tensor(cT[j][0][:], ctxT[j][:], ones[:, 0:1].broadcast_to([D, LK]),
                                        ALU.mult).then_inc(ctx_hi_done, 1)
                reach(pool, ctx_hi_done, k, 2, j + 1)
                nc.gpsimd.tensor_tensor(cT[j][1][:], ctxT[j][:], cT[j][0][:], ALU.subtract).then_inc(ctx_lo_done, 1)
                pool.wait_ge(v_in[j], (k + 1) * 16)
                reach(pool, o_ready, k, 2 * RT, RT * (j - 1))
                nc.gpsimd.tensor_tensor(vs[j][0][:], cx[j][:], ones[0:KT, :].unsqueeze(1).broadcast_to([KT, NT, D]),
                                        ALU.mult).then_inc(vhi_done, 1)
                reach(pool, vhi_done, k, 2, j + 1)
                nc.gpsimd.tensor_tensor(vs[j][1][:], cx[j][:], vs[j][0][:], ALU.subtract).then_inc(vlo_done, 1)

            def step(k):
                for j, _, _ in samples(k):
                    if proj:
                        for i in range(3):
                            split_values(k, j, i)
                    else:
                        split_context(k, j)
            over_pairs(pool, step)

        @block.tensor
        def _(pe):
            if proj:
                pe.wait_ge(front.weights_in, 64)
                for i in range(6):
                    front.product(pe, 0, 0, i)

            def scores(k, j, r, s):
                reach(pe, exp_done, k, 2 * RT, s)
                if proj:
                    for g, at, to, n in row_pieces(r):
                        for m in range(3):
                            last = nc.tensor.matmul(psum[to:to + n, m, 0:500], qx[j][:, g, at:at + n],
                                                    front.ks[j][:, g, m * 500:(m + 1) * 500], start=True, stop=True)
                else:
                    for n, (q, c) in enumerate(((0, 0), (0, 1), (1, 0))):
                        for m in range(3):
                            last = nc.tensor.matmul(psum[:, m, 0:500], qx[j][:, q, r * 128:(r + 1) * 128],
                                                    cT[j][c][:, m * 500:(m + 1) * 500], start=n == 0, stop=n == 2)
                last.then_inc(s_ready, 1)

            def transposes(k, s, i):
                s -= 1
                if i == 0:
                    reach(pe, exp_done, k, 2 * RT, s + 1)
                reach(pe, lo_done[i], k, 2 * RT, s)
                for m in range(4):
                    t = 4 * i + m
                    last = nc.tensor.transpose(psum[0:KT, T_BANK + i, m * D:(m + 1) * D],
                                               p[s % 2][:, t * KT:(t + 1) * KT], ident[:])
                last.then_inc(t_ready[i], 1)

            def output(k, s, i):
                s -= 2
                j, r = s // RT % 2, s % RT
                reach(pe, lo_done[i], k, 2 * RT, s + 1)
                if i == 0:
                    reach(pe, a_done, k, 2 * RT, s)
                    if r == 0:
                        n = 3 if proj else 1
                        reach(pe, vlo_done, k, 2 * n, n * (s // RT + 1))
                c = cols(r)
                for m in range(4):
                    t = 4 * i + m
                    for n, (x, y) in enumerate(((0, 0), (0, 1), (1, 0))):
                        last = nc.tensor.matmul(psum[:, O_BANK, 0:c.stop - c.start], pT[s % 2][x][:, t, :],
                                                vs[j][y][:, t, c], start=t == 0 and n == 0,
                                                stop=t == NT - 1 and n == 2)
                if i == 2:
                    last.then_inc(o_ready, 1)

            def turn(k, j, s, made):
                s -= 3
                reach(pe, a_done, k, 2 * RT, s + 1)
                if proj:
                    reach(pe, front.free, k, 12, 6 * (j + 1) + made)
                reach(pe, aT_done, k, 2 * RT, s)
                nc.tensor.transpose(psum[:, SIDE, 0:D], a[:, s % RT, :], ident[:]).then_inc(aT_ready, 1)

            def items(k, j, r, slot, s):
                if (r, slot) in ITEM_AT:
                    reach(pe, aT_done, k, 2 * RT, s - 3)
                    front.product(pe, *after(k, j), ITEM_AT[r, slot])

            def rest(k, j, r, s, t_on, o_on, a_on, more):
                if more:
                    items(k, j, r, 0, s)
                for what, i in ((transposes, 0), (transposes, 1), (output, 0), (output, 1), (transposes, 2),
                                (output, 2)):
                    if t_on if what is transposes else o_on:
                        what(k, s, i)
                if more:
                    items(k, j, r, 1, s)
                if a_on:
                    turn(k, j, s, sum(x <= r for x, _ in ITEM_AT) if more else 0)

            def step(k):
                for j, first, last_sample in samples(k):
                    for r in range(RT):
                        s = RT * j + r
                        if r == 0:
                            pe.wait_ge(qx_in[j], (k + 1) * 16)
                            if proj:
                                front.stacked(pe, k, j)
                            else:
                                reach(pe, ctx_lo_done, k, 2, j + 1)
                        scores(k, j, r, s)
                        rest(k, j, r, s, not (first and r < 1), not (first and r < 2), not (first and r < 3),
                             not last_sample)
            over_pairs(pe, step)
            for s in range(3):
                rest(NPAIR, -1, s, s, s < 1, s < 2, True, False)

        @block.scalar
        def _(act):
            if proj:
                act.wait_ge(front.weights_in, 64)
                for i in range(3):
                    front.key_hi(act, 0, 0, i)

            def leave(k, s):
                s -= 4
                j, r = s // RT % 2, s % RT
                reach(act, aT_ready, k, 2 * RT, s + 1)
                if r == 0:
                    reach(act, ox_out[j], k, 16, 0)
                nc.scalar.activation(ox[j][:, r * 128:(r + 1) * 128], psum[:, SIDE, 0:D],
                                     ACT.Copy).then_inc(aT_done, 1)

            def transposed(k, s, i):
                s -= 1
                reach(act, t_ready[i], k, 2 * RT, s + 1)
                reach(act, o_ready, k, 2 * RT, s - 1)
                nc.scalar.activation(pT[s % 2][0][:, 4 * i:4 * i + 4, :].rearrange("p t n -> p (t n)"),
                                     psum[0:KT, T_BANK + i, :], ACT.Copy).then_inc(hi_done[i], 1)

            def step(k):
                for j, first, last_sample in samples(k):
                    for r in range(RT):
                        s = RT * j + r
                        if not (first and r < 4):
                            leave(k, s)
                        behind = not (first and r < 1)
                        if behind:
                            transposed(k, s, 0)
                            transposed(k, s, 1)
                        reach(act, shift_done, k, 2 * RT, s + 1)
                        reach(act, t_ready[2], k, 2 * RT, s - 1)
                        nc.scalar.activation(
                            p[s % 2][:].rearrange("p (a n) -> p a n", a=3), psum[:, S_BANKS, 0:500], ACT.Exp,
                            bias=shift[:, s:s + 1], scale=scale, accum_out=z[:, s:s + 1]).then_inc(exp_done, 1)
                        if ITEM_AT.get((r, 0), 9) < 3 and not last_sample:
                            front.key_hi(act, *after(k, j), ITEM_AT[r, 0])
                        if behind:
                            transposed(k, s, 2)
                        if ITEM_AT.get((r, 1), 9) < 3 and not last_sample:
                            front.key_hi(act, *after(k, j), ITEM_AT[r, 1])
            over_pairs(act, step)
            for s in range(4):
                leave(NPAIR, s)
                if s == 0:
                    for i in range(3):
                        transposed(NPAIR, 0, i)

        @block.vector
        def _(dve):
            for n, x in enumerate((top, shift, z, rz, a)):
                nc.vector.memset(x[:], 0.0).then_inc(cleared, 1)
            dve.wait_ge(cleared, 5)
            if proj:
                dve.wait_ge(front.weights_in, 64)
                for i in range(3):
                    front.key_lo(dve, 0, 0, i)
                for i in range(3, 6):
                    front.value(dve, 0, 0, i)

            def transposed(k, s, i):
                s -= 2 if i == 2 else 1
                reach(dve, hi_done[i], k, 2 * RT, s + 1)
                reach(dve, o_ready, k, 2 * RT, s - 1)
                t = slice(4 * i, 4 * i + 4)
                nc.vector.tensor_tensor(
                    pT[s % 2][1][:, t, :], psum[0:KT, T_BANK + i, :].rearrange("p (t n) -> p t n", t=4),
                    pT[s % 2][0][:, t, :], ALU.subtract).then_inc(lo_done[i], 1)

            def items(k, j, r, slot):
                if (r, slot) in ITEM_AT:
                    item = ITEM_AT[r, slot]
                    (front.key_lo if item < 3 else front.value)(dve, *after(k, j), item)

            def attention(k, s):
                s -= 3
                r, c = s % RT, cols(s % RT)
                n = s % (2 * RT)
                reach(dve, o_ready, k, 2 * RT, s + 1)
                reach(dve, aT_ready, k, 2 * RT, s - RT + 1)
                got = psum[:, O_BANK, 0:c.stop - c.start]
                if proj:
                    nc.vector.scalar_tensor_tensor(a[:, r, c], got, rz[:, n:n + 1], window[:, r, 0:c.stop - c.start],
                                                   ALU.mult, ALU.mult).then_inc(a_done, 1)
                else:
                    nc.vector.tensor_scalar(a[:, r, :], got, rz[:, n:n + 1], None, ALU.mult).then_inc(a_done, 1)

            def step(k):
                for j, first, last_sample in samples(k):
                    for r in range(RT):
                        s = RT * j + r
                        c = slice(s, s + 1)
                        if not (first and r < 3):
                            attention(k, s)
                        reach(dve, s_ready, k, 2 * RT, s + 1)
                        nc.vector.tensor_reduce(top[:, c], psum[:, S_BANKS, 0:500], AX.XY,
                                                ALU.max).then_inc(top_done, 1)
                        reach(dve, top_done, k, 2 * RT, s + 1)
                        nc.vector.tensor_scalar(shift[:, c], top[:, c], -scale, LIFT,
                                                ALU.mult, ALU.add).then_inc(shift_done, 1)
                        if not (first and r < 2):
                            transposed(k, s, 2)
                        if not last_sample:
                            items(k, j, r, 0)
                        if not (first and r < 1):
                            transposed(k, s, 0)
                            transposed(k, s, 1)
                        if not last_sample:
                            items(k, j, r, 1)
                        reach(dve, exp_done, k, 2 * RT, s + 1)
                        nc.vector.reciprocal(rz[:, c], z[:, c]).then_inc(rz_done, 1)
            over_pairs(dve, step)
            for s in range(3):
                attention(NPAIR, s)
                if s < 2:
                    transposed(NPAIR, s, 2)
                if s == 0:
                    transposed(NPAIR, 0, 0)
                    transposed(NPAIR, 0, 1)


def output_projection(ph, name, xT, ox_d, w_out, bo, psum):
    nc = ph.nc
    with ExitStack() as ctx:
        ox = [ctx.enter_context(nc.sbuf_tensor(f"{name}_ox{i}", [D, CB, HQ], F32)) for i in range(2)]
        sem = lambda n: ph.semaphore(f"{name}_{n}")
        ox_in = [sem(f"ox_in{i}") for i in range(2)]
        y_ready, x_done = sem("y_ready"), sem("x_done")
        block = ctx.enter_context(ph.block())

        @block.sync
        def _(sp):
            for c in range(NCH):
                if c >= 2:
                    sp.wait_ge(y_ready, c - 1)
                sp.dma_start(ox[c % 2][:], ox_d[c * CB:(c + 1) * CB].rearrange("b p n -> p b n")).then_inc(ox_in[c % 2], 16)

        @block.tensor
        def _(pe):
            for c in range(NCH):
                pe.wait_ge(ox_in[c % 2], 16 * (c // 2 + 1))
                for h in range(H):
                    last = nc.tensor.matmul(psum[:, c, 0:CH], w_out[:, h, :], ox[c % 2][:, :, h * LQ:(h + 1) * LQ],
                                            start=h == 0, stop=h == H - 1)
                last.then_inc(y_ready, 1)

        @block.vector
        def _(dve):
            for c in range(NCH):
                dve.wait_ge(y_ready, c + 1)
                x = xT[:, c * CH:(c + 1) * CH]
                nc.vector.scalar_tensor_tensor(x, psum[:, c, 0:CH], bo[:], x, ALU.add, ALU.add).then_inc(x_done, 1)


def masked_output_weights(ph, name, wo_d, heads, w_out):
    nc = ph.nc
    with ExitStack() as ctx:
        wo = ctx.enter_context(nc.sbuf_tensor(f"{name}_wo", [D, D], F32))
        wo_in = ph.semaphore(f"{name}_wo_in")
        done = ph.semaphore(f"{name}_done")
        block = ctx.enter_context(ph.block())

        @block.sync
        def _(sp):
            sp.dma_start(wo[:], wo_d).then_inc(wo_in, 16)

        @block.vector
        def _(dve):
            dve.wait_ge(wo_in, 16)
            for h in range(H):
                nc.vector.tensor_scalar(w_out[:, h, :], wo[:], heads[:, h:h + 1], None, ALU.mult).then_inc(done, 1)


def router(ph, name, xnT, gate_d, gate_bias_d, select_bias_d, norm_eps, iota, comb, psum):
    nc = ph.nc
    with ExitStack() as ctx:
        sb = lambda n, s, dt=F32: ctx.enter_context(nc.sbuf_tensor(f"{name}_{n}", s, dt))
        sem = lambda n: ph.semaphore(f"{name}_{n}")
        gate, bias = sb("gate", [D, E]), sb("bias", [D, 1, E])
        logit, prob, sel = (sb(n, [RTOK, NR, E]) for n in ("logit", "prob", "sel"))
        best, index, indexf = sb("best", [RTOK, NR, 8]), sb("index", [RTOK, NR, 8], U32), sb("indexf", [RTOK, NR, 8])
        first, second = sb("first", [RTOK, NR, E]), sb("second", [RTOK, NR, E])
        one = sb("one", [RTOK, NR])
        weights_in, logit_ready, exp_ready, exp_done, step_done, best_done, index_done = map(
            sem, ("weights_in", "logit_ready", "exp_ready", "exp_done", "step_done", "best_done", "index_done"))
        block = ctx.enter_context(ph.block())
        bias_d = gate_bias_d if gate_bias_d is not None else select_bias_d

        def wide(a):
            return a.unsqueeze(2).broadcast_to([RTOK, NR, E])

        @block.sync
        def _(sp):
            sp.dma_start(gate[:], gate_d).then_inc(weights_in, 16)
            if bias_d is not None:
                sp.dma_start(bias[:, 0, :], bias_d.broadcast_to([D, E])).then_inc(weights_in, 16)

        @block.tensor
        def _(pe):
            pe.wait_ge(weights_in, 32 if bias_d is not None else 16)
            for i in range(NR):
                last = nc.tensor.matmul(psum[0:RTOK, 0, i * E:(i + 1) * E], xnT[:, i * RTOK:(i + 1) * RTOK],
                                        gate[:], start=True, stop=True)
            last.then_inc(logit_ready, 1)

        @block.scalar
        def _(act):
            act.wait_ge(exp_ready, 1)
            nc.scalar.activation(prob[:], logit[:], ACT.Exp).then_inc(exp_done, 1)

        @block.vector
        def _(dve):
            done = 0

            def then(ins):
                nonlocal done
                done += 1
                ins.then_inc(step_done, 1)
                dve.wait_ge(step_done, done)

            dve.wait_ge(logit_ready, 1)
            wide_bias = bias[0:RTOK, :, :].broadcast_to([RTOK, NR, E])
            raw = psum[0:RTOK, 0, 0:NR * E].rearrange("p (i e) -> p i e", i=NR)
            if gate_bias_d is not None:
                then(nc.vector.tensor_tensor(logit[:], raw, wide_bias, ALU.add))
            else:
                then(nc.vector.tensor_copy(logit[:], raw))
            then(nc.vector.tensor_reduce(one[:], logit[:], AX.X, ALU.max))
            nc.vector.tensor_tensor(logit[:], logit[:], wide(one[:]), ALU.subtract).then_inc(exp_ready, 1)
            dve.wait_ge(exp_done, 1)
            then(nc.vector.tensor_reduce(one[:], prob[:], AX.X, ALU.add))
            then(nc.vector.reciprocal(one[:], one[:]))
            then(nc.vector.tensor_tensor(prob[:], prob[:], wide(one[:]), ALU.mult))
            key = prob
            if select_bias_d is not None:
                then(nc.vector.tensor_tensor(sel[:], prob[:], wide_bias, ALU.add))
                key = sel
            for i in range(NR):
                nc.vector.max(best[:, i, :], key[:, i, :]).then_inc(best_done, 1)
            for i in range(NR):
                dve.wait_ge(best_done, i + 1)
                nc.vector.max_index(index[:, i, :], best[:, i, :], key[:, i, :]).then_inc(index_done, 1)
            dve.wait_ge(index_done, NR)
            then(nc.vector.tensor_copy(indexf[:], index[:]))
            wide_iota = iota[0:RTOK, :].unsqueeze(1).broadcast_to([RTOK, NR, E])
            then(nc.vector.tensor_tensor(first[:], wide_iota, wide(indexf[:, :, 0]), ALU.is_equal))
            then(nc.vector.tensor_tensor(second[:], wide_iota, wide(indexf[:, :, 1]), ALU.is_equal))
            then(nc.vector.tensor_tensor(first[:], first[:], second[:], ALU.add))
            then(nc.vector.tensor_tensor(comb[:], first[:], prob[:], ALU.mult))
            if norm_eps is not None:
                then(nc.vector.tensor_reduce(one[:], comb[:], AX.X, ALU.add))
                then(nc.vector.tensor_scalar(one[:], one[:], norm_eps, None, ALU.add))
                then(nc.vector.reciprocal(one[:], one[:]))
                then(nc.vector.tensor_tensor(comb[:], comb[:], wide(one[:]), ALU.mult))


def experts(ph, name, xT, xnT, comb, gate_d, up_d, down_d, biases, pieces, mode, n_exp, ident, ones, psum, int_scale=None):
    NF = len(pieces)
    F = sum(n for _, n in pieces)
    PMAX = max(n for _, n in pieces)
    weighted = mode != "plain"
    NS = 2 if n_exp > 1 else 1
    nc = ph.nc
    with ExitStack() as ctx:
        sb = lambda n, s, dt=F32: ctx.enter_context(nc.sbuf_tensor(f"{name}_{n}", s, dt))
        sem = lambda n: ph.semaphore(f"{name}_{n}")
        wg = [sb(f"wg{i}", [D, F]) for i in range(NS)]
        wu = [sb(f"wu{i}", [D, F]) for i in range(NS)]
        wd = [sb(f"wd{i}", [PMAX, NF, D]) for i in range(NS)]
        hid = [sb(f"hid{i}", [PMAX, NF, CH]) for i in range(2)]
        act_out = [sb(f"act_out{i}", [PMAX, CH]) for i in range(2)]
        prod = [sb(f"prod{i}", [PMAX, CH]) for i in range(2)]
        y = [sb(f"y{i}", [D, CH]) for i in range(2)]
        if weighted:
            diag = [sb(f"diag{i}", [RTOK, NR, RTOK]) for i in range(2)]
            wide = [sb(f"wide{i}", [D, T]) for i in range(2)]
        xs = [sb(f"xs{i}", [D, T]) for i in range(2)] if mode == "in" else None
        if mode == "bias":
            gb, ub = ([sb(f"{n}{i}", [PMAX, NF]) for i in range(2)] for n in ("gb", "ub"))
            db = [sb(f"db{i}", [D, 1]) for i in range(2)]
        if int_scale is not None:
            raw = [sb(f"raw{i}", [D, F], I32) for i in range(2)] + [sb("raw2", [PMAX, NF, D], I32)]
        loads = (2 + (1 if all(n == PMAX for _, n in pieces) else 2)) + (3 if mode == "bias" else 0)
        w_in = [sem(f"w_in{i}") for i in range(NS)]
        (w_cast, diag_done, wide_ready, wide_done, xs_done, g_ready, u_ready, act_done, mid_done, h_done,
         y_ready, y_done, x_done) = map(sem, (
             "w_cast", "diag_done", "wide_ready", "wide_done", "xs_done", "g_ready", "u_ready", "act_done",
             "mid_done", "h_done", "y_ready", "y_done", "x_done"))
        G_BANK, U_BANK, Y_BANK, W_BANK = 0, 2, 4, 6
        block = ctx.enter_context(ph.block())
        UNITS = NCH * NS

        def over(eng, step):
            step(0)
            if n_exp > 2:
                with eng.Fori(1, n_exp // 2) as k:
                    step(k)

        @block.sync
        def _(sp):
            def load(e, i):
                sp.dma_start(wg[i][:], gate_d[:, e, :]).then_inc(w_in[i], 16)
                sp.dma_start(wu[i][:], up_d[:, e, :]).then_inc(w_in[i], 16)
                full = [n for _, n in pieces if n == PMAX]
                sp.dma_start(wd[i][:, 0:len(full), :],
                             down_d[e, 0:PMAX * len(full), :].rearrange("(f p) d -> p f d", p=PMAX)).then_inc(w_in[i], 16)
                if len(full) < NF:
                    at, n = pieces[-1]
                    sp.dma_start(wd[i][0:n, NF - 1, :], down_d[e, at:at + n, :]).then_inc(w_in[i], 16)
                if mode == "bias":
                    gb_d, ub_d, db_d = biases
                    sp.dma_start(gb[i][:], gb_d[e]).then_inc(w_in[i], 16)
                    sp.dma_start(ub[i][:], ub_d[e]).then_inc(w_in[i], 16)
                    sp.dma_start(db[i][:], db_d[e]).then_inc(w_in[i], 16)

            if int_scale is not None:
                sp.dma_start(raw[0][:], gate_d[:, 0, :]).then_inc(w_in[0], 16)
                sp.dma_start(raw[1][:], up_d[:, 0, :]).then_inc(w_in[0], 16)
                sp.dma_start(raw[2][:], down_d[0].rearrange("(f p) d -> p f d", p=PMAX)).then_inc(w_in[0], 16)
            else:
                def step(k):
                    for i in range(NS):
                        reach(sp, x_done, k, UNITS, NCH * (i - 1))
                        load(NS * k + i, i)
                over(sp, step)

        @block.tensor
        def _(pe):
            def weights(k, i):
                reach(pe, diag_done, k, NS, i + 1)
                for c in range(NCH):
                    reach(pe, wide_done, k, UNITS, NCH * i + c)
                    nc.tensor.matmul(psum[:, W_BANK, 0:CH], ones[0:RTOK, :],
                                     diag[i][:, 4 * c:4 * c + 4, :].rearrange("p i n -> p (i n)"),
                                     start=True, stop=True).then_inc(wide_ready, 1)

            def down(k, u, f):
                u -= 1
                i = u // NCH % NS
                n = pieces[f][1]
                reach(pe, h_done if mode == "bias" else mid_done, k, UNITS * NF, NF * u + f + 1)
                if f == 0:
                    reach(pe, y_done, k, UNITS, u - 1)
                last = nc.tensor.matmul(psum[:, Y_BANK + u % 2, 0:CH], wd[i][0:n, f, :], hid[u % 2][0:n, f, :],
                                        start=f == 0, stop=f == NF - 1)
                if f == NF - 1:
                    last.then_inc(y_ready, 1)

            def step(k):
                if weighted:
                    weights(k, 0)
                for u in range(UNITS):
                    i, c = u // NCH, u % NCH
                    if c == 0:
                        if int_scale is not None:
                            pe.wait_ge(w_cast, 3)
                        else:
                            pe.wait_ge(w_in[i], (k + 1) * 16 * loads)
                        if mode == "in":
                            reach(pe, xs_done, k, NS, i + 1)
                    if weighted and NS == 2 and u == 2:
                        weights(k, 1)
                    src = xs[i] if mode == "in" else xnT
                    for f, (at, n) in enumerate(pieces):
                        m = NF * u + f
                        reach(pe, act_done, k, UNITS * NF, m - 1)
                        nc.tensor.matmul(psum[0:n, G_BANK + m % 2, 0:CH], wg[i][:, at:at + n],
                                         src[:, c * CH:(c + 1) * CH], start=True, stop=True).then_inc(g_ready, 1)
                        reach(pe, mid_done, k, UNITS * NF, m - 1)
                        nc.tensor.matmul(psum[0:n, U_BANK + m % 2, 0:CH], wu[i][:, at:at + n],
                                         src[:, c * CH:(c + 1) * CH], start=True, stop=True).then_inc(u_ready, 1)
                        if not (isinstance(k, int) and k == 0 and u == 0):
                            down(k, u, f)
            over(pe, step)
            for f in range(NF):
                down(max(n_exp // 2, 1), 0, f)

        @block.scalar
        def _(act):
            def weights(k, i):
                for c in range(NCH):
                    reach(act, wide_ready, k, UNITS, NCH * i + c + 1)
                    if mode == "in":
                        reach(act, xs_done, k, NS, i - 1)
                    else:
                        reach(act, y_done, k, UNITS, NCH * (i - 1))
                    nc.scalar.activation(wide[i][:, c * CH:(c + 1) * CH], psum[:, W_BANK, 0:CH],
                                         ACT.Copy).then_inc(wide_done, 1)

            def step(k):
                if weighted:
                    weights(k, 0)
                for u in range(UNITS):
                    i = u // NCH
                    if weighted and NS == 2 and u == 2:
                        weights(k, 1)
                    for f, (at, n) in enumerate(pieces):
                        m = NF * u + f
                        if mode == "bias":
                            reach(act, g_ready, k, UNITS * NF, m + 1)
                            if u % NCH == 0 and f == 0:
                                act.wait_ge(w_in[i], (k + 1) * 16 * loads)
                            reach(act, mid_done, k, UNITS * NF, m - 1)
                            nc.scalar.activation(act_out[m % 2][0:n, :], psum[0:n, G_BANK + m % 2, 0:CH],
                                                 ACT.Identity, bias=gb[i][0:n, f:f + 1]).then_inc(act_done, 1)
                            reach(act, mid_done, k, UNITS * NF, m + 1)
                            reach(act, y_ready, k, UNITS, u - 1)
                            nc.scalar.activation(hid[u % 2][0:n, f, :], prod[m % 2][0:n, :],
                                                 ACT.Silu).then_inc(h_done, 1)
                        else:
                            reach(act, g_ready, k, UNITS * NF, m + 1)
                            reach(act, mid_done, k, UNITS * NF, m - 1)
                            nc.scalar.activation(act_out[m % 2][0:n, :], psum[0:n, G_BANK + m % 2, 0:CH],
                                                 ACT.Silu).then_inc(act_done, 1)
            over(act, step)

        @block.gpsimd
        def _(pool):
            def step(k):
                for u in range(UNITS):
                    c = u % NCH
                    reach(pool, y_done, k, UNITS, u + 1)
                    reach(pool, x_done, k, UNITS, u)
                    x = xT[:, c * CH:(c + 1) * CH]
                    nc.gpsimd.tensor_tensor(x, x, y[u % 2][:], ALU.add).then_inc(x_done, 1)
            over(pool, step)

        @block.vector
        def _(dve):
            def diagonals(k, i):
                reach(dve, wide_ready, k, UNITS, NCH * (i - 1))
                e = NS * k + i
                c = comb[:, :, e:e + 1] if isinstance(k, int) else comb[:, :, bass.ds(e, 1)]
                nc.vector.tensor_tensor(diag[i][:], ident[0:RTOK, 0:RTOK].unsqueeze(1).broadcast_to([RTOK, NR, RTOK]),
                                        c.broadcast_to([RTOK, NR, RTOK]), ALU.mult).then_inc(diag_done, 1)

            def inputs(k, i):
                reach(dve, wide_done, k, UNITS, NCH * (i + 1))
                reach(dve, u_ready, k, UNITS * NF, NCH * NF * (i - 1))
                nc.vector.tensor_tensor(xs[i][:], xnT[:], wide[i][:], ALU.mult).then_inc(xs_done, 1)

            def outputs(k, u):
                u -= 1
                i, c = u // NCH % NS, u % NCH
                reach(dve, y_ready, k, UNITS, u + 1)
                reach(dve, x_done, k, UNITS, u - 1)
                out, got = y[u % 2][:], psum[:, Y_BANK + u % 2, 0:CH]
                if mode in ("in", "plain"):
                    nc.vector.tensor_copy(out, got).then_inc(y_done, 1)
                else:
                    if c == 0:
                        reach(dve, wide_done, k, UNITS, NCH * (u // NCH + 1))
                    w = wide[i][:, c * CH:(c + 1) * CH]
                    if mode == "bias":
                        nc.vector.scalar_tensor_tensor(out, got, db[i][:], w, ALU.add, ALU.mult).then_inc(y_done, 1)
                    else:
                        nc.vector.tensor_tensor(out, got, w, ALU.mult).then_inc(y_done, 1)

            if int_scale is not None:
                dve.wait_ge(w_in[0], 48)
                for dst, src in ((wg[0], raw[0]), (wu[0], raw[1]), (wd[0], raw[2])):
                    nc.vector.tensor_scalar(dst[:], src[:], int_scale, None, ALU.mult).then_inc(w_cast, 1)

            def step(k):
                if weighted:
                    diagonals(k, 0)
                    if mode == "in":
                        inputs(k, 0)
                for u in range(UNITS):
                    i = u // NCH
                    if weighted and NS == 2 and u == 1:
                        diagonals(k, 1)
                    if mode == "in" and u == 3:
                        inputs(k, 1)
                    for f, (at, n) in enumerate(pieces):
                        m = NF * u + f
                        reach(dve, act_done, k, UNITS * NF, m + 1)
                        reach(dve, u_ready, k, UNITS * NF, m + 1)
                        up = psum[0:n, U_BANK + m % 2, 0:CH]
                        if mode == "bias":
                            if u % NCH == 0 and f == 0:
                                dve.wait_ge(w_in[i], (k + 1) * 16 * loads)
                            reach(dve, h_done, k, UNITS * NF, m - 1)
                            nc.vector.scalar_tensor_tensor(prod[m % 2][0:n, :], up, ub[i][0:n, f:f + 1],
                                                           act_out[m % 2][0:n, :], ALU.add,
                                                           ALU.mult).then_inc(mid_done, 1)
                        else:
                            reach(dve, y_ready, k, UNITS, u - 1)
                            nc.vector.tensor_tensor(hid[u % 2][0:n, f, :], act_out[m % 2][0:n, :], up,
                                                    ALU.mult).then_inc(mid_done, 1)
                    if not (isinstance(k, int) and k == 0 and u == 0):
                        outputs(k, u)
            over(dve, step)
            outputs(max(n_exp // 2, 1), 0)


def build(nc, a, out):
    with ExitStack() as ctx:
        sb = lambda n, s, dt=F32: ctx.enter_context(nc.sbuf_tensor(n, s, dt))
        xT, xnT = sb("xT", [D, T]), sb("xnT", [D, T])
        ident, ones, ones_mean = sb("ident", [D, D]), sb("ones", [D, D]), sb("ones_mean", [D, D])
        heads, own, iota = sb("heads", [D, H]), sb("own", [D, GH]), sb("iota", [D, E])
        window = sb("window", [D, RT, 32])
        gamma, beta, bo = sb("gamma", [D, 1]), sb("beta", [D, 1]), [sb(f"bo{i}", [D, 1]) for i in range(3)]
        comb = sb("comb", [RTOK, NR, E])
        psum = ctx.enter_context(nc.psum_tensor("psum", [D, 8, 512], F32))
        qx_d = nc.dram_tensor("qx_scratch", (B, D, HQ), F16, kind="Internal").ap()
        qx2_d = nc.dram_tensor("qx2_scratch", (B, D, 2 * HQ), F16, kind="Internal").ap()
        ox_d = nc.dram_tensor("ox_scratch", (B, D, HQ), F32, kind="Internal").ap()
        ph = Phases(nc)
        start_in, const_done = ph.semaphore("start_in"), ph.semaphore("const_done")
        col = lambda n: a[n].rearrange("(d o) -> d o", o=1)
        row = lambda n: a[n].rearrange("(o d) -> o d", o=1)

        with ph.block() as block:
            @block.sync
            def _(sp):
                moves = [(xT[:], a["xT"]), (ident[:], a["ident"]), (heads[:], a["heads"]),
                         (own[:], a["own"]), (window[:], a["window"]), (iota[:], a["iota"]),
                         (gamma[:], col("L2_xattn_ln_gamma")), (beta[:], col("L2_xattn_ln_beta")),
                         (bo[0][:], col("L1_xattn_bo")), (bo[1][:], col("L2_xattn_b_out")), (bo[2][:], col("L3_xattn_bo"))]
                for dst, src in moves:
                    sp.dma_start(dst, src).then_inc(start_in, 16)
                sp.wait_ge(start_in, 16 * len(moves))

            @block.vector
            def _(dve):
                nc.vector.memset(ones[:], 1.0).then_inc(const_done, 1)
                nc.vector.memset(ones_mean[:], 1.0 / D).then_inc(const_done, 1)

        norm = lambda name: layer_norm(ph, name, xT, xnT, ones_mean, psum)

        norm("n0")
        sigmoid_attention(ph, xT, xnT, a["ctxT"], a["ctx"].rearrange("b (t p) d -> b p t d", p=KT),
                          a["mask"], a["L0_xattn_WqT"], col("L0_xattn_bq"), a["L0_xattn_Wk"], col("L0_xattn_bk"), ident,
                          psum)
        norm("n1")
        router(ph, "r0", xnT, a["L0_ffn_gate_wT"], None, row("L0_ffn_expert_bias"), None, iota, comb, psum)
        experts(ph, "e0", xT, xnT, comb, a["L0_ffn_w1"], a["L0_ffn_w3"], a["L0_ffn_w2"], None,
                [(0, 128), (128, 128), (256, 96)], "in", E, ident, ones, psum)

        norm("n2")
        with nc.sbuf_tensor("w_out1", [D, H, D], F32) as w_out:
            masked_output_weights(ph, "w1", a["L1_xattn_Wo"], heads, w_out)
            head_queries(ph, "q1", xnT, a["L1_xattn_Wq"], col("L1_xattn_bq"), own, qx_d, psum)
            query_softmax_attention(ph, "a1", a["ctxT"], qx_d, ox_d,
                                    (a["L1_xattn_Wk"], col("L1_xattn_bk"), a["L1_xattn_Wv"], row("L1_xattn_bv")),
                                    float(DH) ** -0.5, ident, psum)
            output_projection(ph, "o1", xT, ox_d, w_out, bo[0], psum)
        norm("n3")
        router(ph, "r1", xnT, a["L1_ffn_gate_wT"], row("L1_ffn_gate_b"), None, 1e-20, iota, comb, psum)
        experts(ph, "e1", xT, xnT, comb, a["L1_ffn_gp_wT"], a["L1_ffn_up_wT"], a["L1_ffn_down_wT"],
                (a["L1_ffn_gp_bT"], a["L1_ffn_up_bT"],
                 a["L1_ffn_down_b"].rearrange("e (d o) -> e d o", o=1)),
                [(102 * f, 102) for f in range(4)], "bias", E, ident, ones, psum)

        norm("n4")
        layer_norm(ph, "n4b", xnT, xnT, ones_mean, psum, (gamma[:], beta[:]))
        with nc.sbuf_tensor("w_out2", [D, H, D], F32) as w_out:
            with nc.sbuf_tensor("w_in2", [D, H, D], F32) as w_in:
                folded_weights(ph, a["L2_xattn_w_qT"], a["L2_xattn_w_kT"], a["L2_xattn_w_vT"], a["L2_xattn_w_out"],
                               a["L2_xattn_gate"].rearrange("(o d) -> o d", o=1), bo[1], w_in, w_out, psum)
                folded_queries(ph, xnT, w_in, qx2_d, psum)
            key_softmax_attention(ph, "a2", a["ctxT"], a["ctx"].rearrange("b (t p) d -> b p t d", p=KT), qx2_d, ox_d,
                                  None, 64.0 ** -0.5, ident, ones, window, psum)
            output_projection(ph, "o2", xT, ox_d, w_out, bo[1], psum)
        norm("n5")
        experts(ph, "e2", xT, xnT, None, a["L2_ffn_w_gateT"], a["L2_ffn_w_upT"], a["L2_ffn_w_downT"], None,
                [(128 * f, 128) for f in range(3)], "plain", 1, ident, ones, psum, int_scale=1.0 / 127.0)

        norm("n6")
        with nc.sbuf_tensor("w_out3", [D, H, D], F32) as w_out:
            masked_output_weights(ph, "w3", a["L3_xattn_Wo"], heads, w_out)
            head_queries(ph, "q3", xnT, a["L3_xattn_Wq"], col("L3_xattn_bq"), own, qx_d, psum)
            key_softmax_attention(ph, "a3", a["ctxT"], None, qx_d, ox_d,
                                  (a["L3_xattn_Wk"], col("L3_xattn_bk"), a["L3_xattn_Wv"], row("L3_xattn_bv")),
                                  float(DH) ** -0.5, ident, ones, window, psum)
            output_projection(ph, "o3", xT, ox_d, w_out, bo[2], psum)
        norm("n7")
        router(ph, "r3", xnT, a["L3_ffn_gate_wT"], None, None, 0.0, iota, comb, psum)
        experts(ph, "e3", xT, xnT, comb, a["L3_ffn_gateT"], a["L3_ffn_upT"], a["L3_ffn_down_projT"], None,
                [(128 * f, 128) for f in range(4)], "out", E, ident, ones, psum)

        out_done = ph.semaphore("out_done")
        with ph.block() as block:
            @block.sync
            def _(sp):
                sp.dma_start(out, xT[:]).then_inc(out_done, 16)
                sp.wait_ge(out_done, 16)


def kernel(**inputs):
    import numpy as np
    import concourse.bacc as bacc
    from concourse.bass_utils import run_bass_kernel_spmd

    i = {n: np.asarray(x) for n, x in inputs.items()}
    a = {
        "xT": i["x"].reshape(T, D).T, "ctx": i["ctx_1024"], "ctxT": i["ctx_1024"].transpose(0, 2, 1),
        "mask": i["mask_BxS2_ik1"].reshape(B, NT, KT).transpose(2, 0, 1),
        "ident": np.eye(D, dtype=np.float32),
        "heads": np.repeat(np.eye(H, dtype=np.float32), D // H, axis=0),
        "own": np.tile(np.repeat(np.eye(GH, dtype=np.float32), DH, axis=0), (TERMS, 1)),
        "window": np.stack([(np.arange(128 * r, 128 * r + 128)[:, None] // LQ - 128 * r // LQ
                             == np.arange(32) // DH).astype(np.float32) for r in range(RT)], axis=1),
        "iota": np.tile(np.arange(E, dtype=np.float32), (D, 1)),
        "L0_xattn_WqT": i["L0_xattn_Wq"].T, "L0_ffn_gate_wT": i["L0_ffn_gate_w"].T,
        "L0_ffn_w1": i["L0_ffn_w1"].transpose(1, 0, 2), "L0_ffn_w3": i["L0_ffn_w3"].transpose(1, 0, 2),
        "L0_ffn_w2": i["L0_ffn_w2"],
        "L1_ffn_gate_wT": i["L1_ffn_gate_w"].T,
        "L1_ffn_gp_wT": i["L1_ffn_gp_w"].transpose(2, 0, 1), "L1_ffn_up_wT": i["L1_ffn_up_w"].transpose(2, 0, 1),
        "L1_ffn_down_wT": i["L1_ffn_down_w"].transpose(0, 2, 1),
        "L1_ffn_gp_bT": i["L1_ffn_gp_b"].reshape(E, 4, 102).transpose(0, 2, 1),
        "L1_ffn_up_bT": i["L1_ffn_up_b"].reshape(E, 4, 102).transpose(0, 2, 1),
        "L2_xattn_w_qT": i["L2_xattn_w_q"].T, "L2_xattn_w_kT": i["L2_xattn_w_kv"][:, :1024].T,
        "L2_xattn_w_vT": i["L2_xattn_w_kv"][:, 1024:].T,
        "L2_ffn_w_gateT": i["L2_ffn_w_gate"].T[:, None], "L2_ffn_w_upT": i["L2_ffn_w_up"].T[:, None],
        "L2_ffn_w_downT": i["L2_ffn_w_down"].T[None],
        "L3_ffn_gate_wT": i["L3_ffn_gate_w"].T,
        "L3_ffn_gateT": i["L3_ffn_gate_up_proj"][:, :512].transpose(2, 0, 1),
        "L3_ffn_upT": i["L3_ffn_gate_up_proj"][:, 512:].transpose(2, 0, 1),
        "L3_ffn_down_projT": i["L3_ffn_down_proj"].transpose(0, 2, 1),
    }
    for n in ("L0_xattn_bq", "L0_xattn_Wk", "L0_xattn_bk", "L0_ffn_expert_bias", "L1_xattn_Wq", "L1_xattn_bq",
              "L1_xattn_Wk", "L1_xattn_bk", "L1_xattn_Wv", "L1_xattn_bv", "L1_xattn_Wo", "L1_xattn_bo",
              "L1_ffn_gate_b", "L1_ffn_down_b", "L2_xattn_ln_gamma",
              "L2_xattn_ln_beta", "L2_xattn_w_out", "L2_xattn_b_out", "L2_xattn_gate", "L3_xattn_Wq", "L3_xattn_bq",
              "L3_xattn_Wk", "L3_xattn_bk", "L3_xattn_Wv", "L3_xattn_bv", "L3_xattn_Wo", "L3_xattn_bo"):
        a[n] = i[n]
    nc = bacc.Bacc("TRN2", target_bir_lowering=False, num_devices=1)
    arrays, aps = {}, {}
    for n, x in a.items():
        arrays[f"in_{n}"] = np.ascontiguousarray(x)
        aps[n] = nc.dram_tensor(f"in_{n}", x.shape, mybir.dt.from_np(x.dtype), kind="ExternalInput").ap()
    out = nc.dram_tensor("out_xT", (D, T), F32, kind="ExternalOutput").ap()
    build(nc, aps, out)
    r = run_bass_kernel_spmd(nc, [arrays], core_ids=[0])
    return np.ascontiguousarray(r.results[0]["out_xT"].T).reshape(B, LQ, D)
```

```python
import math
from contextlib import ExitStack, contextmanager

import concourse.bass as bass
from concourse import mybir

F32 = mybir.dt.float32
F16 = mybir.dt.float16
BF16 = mybir.dt.bfloat16
I32 = mybir.dt.int32
U32 = mybir.dt.uint32
ALU = mybir.AluOpType
ACT = mybir.ActivationFunctionType
AX = mybir.AxisListType

D = 128
B, LQ, LK = 32, 56, 1500
T = B * LQ
CH = 448
NCH = T // CH
CB = CH // LQ
KT = 125
NT = LK // KT
H = 16
HQ = H * LQ
HALF = HQ // 2
RT = HQ // 128
NPAIR = B // 2
E = 8
RTOK = 112
NR = T // RTOK
EPS = 1e-5


def reach(eng, sem, k, per, off):
    if isinstance(k, int):
        if per * k + off > 0:
            eng.wait_ge(sem, per * k + off)
    else:
        assert per + off >= 0
        eng.wait_ge(sem, k * per + off)


def over_pairs(eng, step, peeled=1):
    for k in range(peeled):
        step(k)
    with eng.Fori(peeled, NPAIR - 1) as k:
        step(k)
    step(NPAIR - 1)


def samples(k):
    for j in range(2):
        yield j, isinstance(k, int) and k == 0 and j == 0, isinstance(k, int) and k == NPAIR - 1 and j == 1


class Phases:

    def __init__(self, nc):
        self.nc, self.own, self.before = nc, [], []
        self.own_held, self.before_held = ExitStack(), ExitStack()

    def semaphore(self, name):
        self.own.append(self.own_held.enter_context(self.nc.semaphore(name)))
        return self.own[-1]

    @contextmanager
    def block(self):
        with self.nc.Block() as block:
            @block.gpsimd
            def _(pool):
                for s in self.before:
                    pool.sem_clear(s)
            yield block
        self.before_held.close()
        self.before, self.before_held = self.own, self.own_held
        self.own, self.own_held = [], ExitStack()


def layer_norm(ph, name, src, dst, ones_mean, spread, psum, affine=None, ahead=()):
    nc = ph.nc
    with ExitStack() as ctx:
        cen = ctx.enter_context(nc.sbuf_tensor(f"{name}_cen", [D, NCH, CH], F32))
        sq = ctx.enter_context(nc.sbuf_tensor(f"{name}_sq", [D, NCH, CH], F32))
        rstd = ctx.enter_context(nc.sbuf_tensor(f"{name}_rstd", [D, CH], F32))
        sem = lambda n: ph.semaphore(f"{name}_{n}")
        mean_ready, centred, squared, var_ready, rooted, inverted, scaled, rstd_ready, done = map(
            sem, ("mean_ready", "centred", "squared", "var_ready", "rooted", "inverted", "scaled", "rstd_ready",
                  "done"))
        VAR_BANK = 4
        block = ctx.enter_context(ph.block())

        @block.sync
        def _(sp):
            for to, source, loaded in ahead:
                sp.dma_start(to, source).then_inc(loaded, 16)

        @block.tensor
        def _(pe):
            for c in range(NCH):
                nc.tensor.matmul(psum[:, c, 0:CH], ones_mean[:], src[:, c * CH:(c + 1) * CH],
                                 start=True, stop=True).then_inc(mean_ready, 1)
            for c in range(NCH):
                pe.wait_ge(squared, c + 1)
                nc.tensor.matmul(psum[32 * c:32 * c + 32, VAR_BANK, 0:CH], ones_mean[:, 0:32], sq[:, c, :],
                                 start=True, stop=True).then_inc(var_ready, 1)
            pe.wait_ge(rooted, 1)
            for c in range(NCH):
                nc.tensor.matmul(psum[:, c, 0:CH], spread[:, c, :], rstd[:], start=True, stop=True).then_inc(rstd_ready, 1)

        @block.scalar
        def _(act):
            for c in range(NCH):
                act.wait_ge(centred, c + 1)
                nc.scalar.activation(sq[:, c, :], cen[:, c, :], ACT.Square).then_inc(squared, 1)
            act.wait_ge(inverted, 1)
            nc.scalar.activation(rstd[:], rstd[:], ACT.Sqrt).then_inc(rooted, 1)

        @block.vector
        def _(dve):
            for c in range(NCH):
                dve.wait_ge(mean_ready, c + 1)
                nc.vector.tensor_tensor(cen[:, c, :], src[:, c * CH:(c + 1) * CH], psum[:, c, 0:CH],
                                        ALU.subtract).then_inc(centred, 1)
            dve.wait_ge(var_ready, NCH)
            nc.vector.tensor_scalar(rstd[:], psum[:, VAR_BANK, 0:CH], EPS, None, ALU.add).then_inc(scaled, 1)
            dve.wait_ge(scaled, 1)
            nc.vector.reciprocal(rstd[:], rstd[:]).then_inc(inverted, 1)
            for c in range(NCH):
                dve.wait_ge(rstd_ready, c + 1)
                nc.vector.tensor_tensor(dst[:, c * CH:(c + 1) * CH], cen[:, c, :], psum[:, c, 0:CH],
                                        ALU.mult).then_inc(done, 1)
            if affine is not None:
                gamma, beta = affine
                dve.wait_ge(done, NCH)
                nc.vector.tensor_scalar(dst[:], dst[:], gamma, beta, ALU.mult, ALU.add).then_inc(done, 1)


def sigmoid_attention(ph, xT, xnT, ctxT_d, ctx_d, mask_d, wqT_d, bq_d, wk_d, bk_d, ident, psum):
    SCALE = float(D) ** -0.5
    DK = 64
    nc = ph.nc
    with ExitStack() as ctx:
        sb = lambda n, s, dt=F32: ctx.enter_context(nc.sbuf_tensor(f"sa_{n}", s, dt))
        sem = lambda n: ph.semaphore(f"sa_{n}")
        wqT, wk, bq, bk = sb("wqT", [D, DK]), sb("wk", [DK, D]), sb("bq", [DK, 1]), sb("bk", [DK, 1])
        masked = sb("masked", [KT, B, NT], I32)
        keep = sb("keep", [KT, B, NT])
        qT, qkT, qb = sb("qT", [DK, T]), sb("qkT", [D, T]), sb("qb", [LQ, B])
        qk, bias = [sb(f"qk{i}", [D, LQ]) for i in range(2)], [sb(f"bias{i}", [LQ, 1]) for i in range(2)]
        ctxT = [sb(f"ctxT{i}", [D, LK]) for i in range(2)]
        cx = [sb(f"cx{i}", [KT, NT, D]) for i in range(2)]
        sig = [sb(f"sig{i}", [D, LK]) for i in range(2)]
        alpha = [sb(f"alpha{i}", [KT, NT, LQ]) for i in range(2)]
        y = [sb(f"y{i}", [D, D]) for i in range(2)]
        weights_in, mask_in, keep_done, cleared = sem("weights_in"), sem("mask_in"), sem("keep_done"), sem("cleared")
        q_ready, q_done, qk_ready, qk_done, qb_ready, qb_done = map(
            sem, ("q_ready", "q_done", "qk_ready", "qk_done", "qb_ready", "qb_done"))
        ctxT_in = [sem(f"ctxT_in{i}") for i in range(2)]
        cx_in = [sem(f"cx_in{i}") for i in range(2)]
        picked, s_ready, sig_done, sigT_ready, alpha_done, o_ready, y_done, yT_ready, x_done = map(
            sem, ("picked", "s_ready", "sig_done", "sigT_ready", "alpha_done", "o_ready", "y_done", "yT_ready",
                  "x_done"))
        PEELED = 2
        S_BANKS, T_BANKS, O_BANK, Y_BANK = slice(0, 3), slice(3, 6), 6, 7
        block = ctx.enter_context(ph.block())

        @block.sync
        def _(sp):
            sp.dma_start(wqT[:], wqT_d).then_inc(weights_in, 16)
            sp.dma_start(wk[:], wk_d).then_inc(weights_in, 16)
            sp.dma_start(bq[:], bq_d).then_inc(weights_in, 16)
            sp.dma_start(bk[:], bk_d).then_inc(weights_in, 16)
            sp.dma_start(ctxT[0][:], ctxT_d[0]).then_inc(ctxT_in[0], 16)
            sp.dma_start(masked[:], mask_d).then_inc(mask_in, 16)
            sp.dma_start(ctxT[1][:], ctxT_d[1]).then_inc(ctxT_in[1], 16)
            sp.dma_start(cx[0][:], ctx_d[0]).then_inc(cx_in[0], 16)

            def step(k):
                for j, _, last in samples(k):
                    if not (isinstance(k, int) and k == NPAIR - 1):
                        reach(sp, s_ready, k, 2, j + 1)
                        sp.dma_start(ctxT[j][:], ctxT_d[2 * k + j + 2]).then_inc(ctxT_in[j], 16)
                    if not last:
                        reach(sp, o_ready, k, 2, j)
                        sp.dma_start(cx[1 - j][:], ctx_d[2 * k + j + 1]).then_inc(cx_in[1 - j], 16)
            over_pairs(sp, step, PEELED)

        @block.tensor
        def _(pe):
            pe.wait_ge(weights_in, 64)
            for c in range(NCH):
                nc.tensor.matmul(psum[0:DK, c, 0:CH], wqT[:], xnT[:, c * CH:(c + 1) * CH],
                                 start=True, stop=True).then_inc(q_ready, 1)
            for c in range(NCH):
                pe.wait_ge(q_done, c + 1)
                nc.tensor.matmul(psum[:, 4 + c, 0:CH], wk[:], qT[:, c * CH:(c + 1) * CH],
                                 start=True, stop=True).then_inc(qk_ready, 1)
            for b in range(B):
                last = nc.tensor.matmul(psum[0:LQ, 0, b:b + 1], qT[:, b * LQ:(b + 1) * LQ], bk[:],
                                        start=True, stop=True)
            last.then_inc(qb_ready, 1)
            pe.wait_ge(qk_done, NCH)
            pe.wait_ge(qb_done, 1)

            def transposes(k, j):
                i = 1 - j
                reach(pe, sig_done, k, 2, j)
                reach(pe, alpha_done, k, 2, j - 1)
                for t in range(NT):
                    last = nc.tensor.transpose(psum[0:KT, T_BANKS.start + t // 4, t % 4 * D:(t % 4 + 1) * D],
                                               sig[i][:, t * KT:(t + 1) * KT], ident[:])
                last.then_inc(sigT_ready, 1)

            def scores(k, j):
                pe.wait_ge(ctxT_in[j], (k + 1) * 16)
                reach(pe, picked, k, 4, 2 * (j + 1))
                reach(pe, sig_done, k, 2, j)
                for m in range(3):
                    last = nc.tensor.matmul(psum[0:LQ, m, 0:500], qk[j][:], ctxT[j][:, m * 500:(m + 1) * 500],
                                            start=True, stop=True)
                last.then_inc(s_ready, 1)

            def turn(k, j):
                reach(pe, y_done, k, 2, j - 1)
                reach(pe, x_done, k, 2, j - 2)
                nc.tensor.transpose(psum[:, Y_BANK, 0:D], y[j][:], ident[:]).then_inc(yT_ready, 1)

            def output(k, j):
                i = 1 - j
                reach(pe, alpha_done, k, 2, j)
                pe.wait_ge(cx_in[i], (k + j) * 16)
                reach(pe, y_done, k, 2, j - 1)
                for t in range(NT):
                    last = nc.tensor.matmul(psum[0:LQ, O_BANK, 0:D], alpha[i][:, t, :], cx[i][:, t, :],
                                            start=t == 0, stop=t == NT - 1)
                last.then_inc(o_ready, 1)

            def step(k):
                for j, first, _ in samples(k):
                    if not first:
                        transposes(k, j)
                    scores(k, j)
                    if not (isinstance(k, int) and k == 0):
                        turn(k, j)
                    if not first:
                        output(k, j)
            over_pairs(pe, step, PEELED)
            transposes(NPAIR, 0)
            turn(NPAIR, 0)
            output(NPAIR, 0)
            turn(NPAIR, 1)

        @block.scalar
        def _(act):
            for c in range(NCH):
                act.wait_ge(q_ready, c + 1)
                nc.scalar.activation(qT[:, c * CH:(c + 1) * CH], psum[0:DK, c, 0:CH], ACT.Identity,
                                     bias=bq[:]).then_inc(q_done, 1)

            act.wait_ge(cleared, 4)

            def leave(k, j):
                i = 1 - j
                reach(act, o_ready, k, 2, j)
                reach(act, yT_ready, k, 2, j - 2)
                nc.scalar.activation(y[i][0:LQ, :], psum[0:LQ, O_BANK, 0:D], ACT.Copy).then_inc(y_done, 1)

            def step(k):
                for j, first, _ in samples(k):
                    reach(act, s_ready, k, 2, j + 1)
                    reach(act, sigT_ready, k, 2, j - 1)
                    nc.scalar.activation(
                        sig[j][0:LQ, :].rearrange("q (a n) -> q a n", a=3), psum[0:LQ, S_BANKS, 0:500],
                        ACT.Sigmoid, bias=bias[j][:], scale=SCALE).then_inc(sig_done, 1)
                    if not first:
                        leave(k, j)
            over_pairs(act, step, PEELED)
            leave(NPAIR, 0)

        @block.vector
        def _(dve):
            for i in range(2):
                nc.vector.memset(y[i][:], 0.0).then_inc(cleared, 1)
                nc.vector.memset(sig[i][:], 0.0).then_inc(cleared, 1)
            dve.wait_ge(mask_in, 16)
            nc.vector.tensor_scalar(keep[:], masked[:], 1.0, None, ALU.not_equal).then_inc(keep_done, 1)
            for c in range(NCH):
                dve.wait_ge(qk_ready, c + 1)
                nc.vector.tensor_copy(qkT[:, c * CH:(c + 1) * CH], psum[:, 4 + c, 0:CH]).then_inc(qk_done, 1)
            dve.wait_ge(qb_ready, 1)
            nc.vector.tensor_scalar(qb[:], psum[0:LQ, 0, 0:B], SCALE, None, ALU.mult).then_inc(qb_done, 1)
            dve.wait_ge(qk_done, NCH)
            dve.wait_ge(qb_done, 1)
            dve.wait_ge(keep_done, 1)

            def pick(k, j):
                b = 2 * k + j
                nc.vector.tensor_copy(qk[j][:], qkT[:, bass.ds(b * LQ, LQ)]).then_inc(picked, 1)
                nc.vector.tensor_copy(bias[j][:], qb[:, bass.ds(b, 1)]).then_inc(picked, 1)

            def mask(k, j):
                i = 1 - j
                b = 2 * k + j - 1
                reach(dve, sigT_ready, k, 2, j)
                reach(dve, o_ready, k, 2, j - 2)
                split = lambda x: x.rearrange("p (a t) q -> p a t q", a=3)
                nc.vector.tensor_tensor(
                    split(alpha[i][:]), psum[0:KT, T_BANKS, :].rearrange("p a (t q) -> p a t q", t=4)[:, :, :, 0:LQ],
                    split(keep[:, b, :].unsqueeze(2).broadcast_to([KT, NT, LQ])), ALU.mult).then_inc(alpha_done, 1)

            def add(k, j):
                reach(dve, yT_ready, k, 2, j - 1)
                x = xT[:, bass.ds((2 * k + j - 2) * LQ, LQ)]
                nc.vector.tensor_tensor(x, x, psum[:, Y_BANK, 0:LQ], ALU.add).then_inc(x_done, 1)

            pick(0, 0)

            def step(k):
                for j, first, last in samples(k):
                    if not first:
                        mask(k, j)
                    if not last:
                        reach(dve, s_ready, k, 2, j)
                        reach(dve, sig_done, k, 2, j)
                        pick(*((k, 1) if j == 0 else (k + 1, 0)))
                    if not (isinstance(k, int) and k == 0):
                        add(k, j)
            over_pairs(dve, step, PEELED)
            mask(NPAIR, 0)
            add(NPAIR, 0)
            add(NPAIR, 1)


TERMS = 4
GH = H // TERMS
GQ = GH * LQ
DH = D // H


class HeadQueries:

    def __init__(self, nc, sb, sem, weights, xnT, stack, psum):
        self.nc, self.weights, self.xnT, self.stacks, self.psum = nc, weights, xnT, stack, psum
        self.wq, self.bq = sb("wq", [D, D]), sb("bq", [D, 1])
        self.part = [sb("qhi", [D, T], F16), sb("qlo", [D, T], F16)]
        self.weights_in, self.ready, self.hi_done, self.lo_done, self.stacked = map(
            sem, ("q_weights_in", "q_ready", "q_hi_done", "q_lo_done", "q_stacked"))

    def load_weights(self, sp):
        sp.dma_start(self.wq[:], self.weights[0]).then_inc(self.weights_in, 16)
        sp.dma_start(self.bq[:], self.weights[1]).then_inc(self.weights_in, 16)

    def stack(self, sp):
        for n, done in enumerate((self.hi_done, self.lo_done)):
            sp.wait_ge(done, NCH)
            for term in range(n, TERMS, 2):
                for g in range(TERMS):
                    sp.dma_start(self.stacks[32 * term:32 * term + 32, g, :],
                                 self.part[n][32 * g:32 * g + 32, :]).then_inc(self.stacked, 16)

    def products(self, pe):
        pe.wait_ge(self.weights_in, 32)
        for c in range(NCH):
            self.nc.tensor.matmul(self.psum[:, c, 0:CH], self.wq[:], self.xnT[:, c * CH:(c + 1) * CH],
                                  start=True, stop=True).then_inc(self.ready, 1)

    def hi(self, act):
        for c in range(NCH):
            act.wait_ge(self.ready, c + 1)
            self.nc.scalar.activation(self.part[0][:, c * CH:(c + 1) * CH], self.psum[:, c, 0:CH], ACT.Identity,
                                      bias=self.bq[:]).then_inc(self.hi_done, 1)

    def lo(self, dve):
        for c in range(NCH):
            dve.wait_ge(self.hi_done, c + 1)
            self.nc.vector.scalar_tensor_tensor(
                self.part[1][:, c * CH:(c + 1) * CH], self.psum[:, c, 0:CH], self.bq[:],
                self.part[0][:, c * CH:(c + 1) * CH], ALU.add, ALU.subtract).then_inc(self.lo_done, 1)

    def wait_stacked(self, eng):
        eng.wait_ge(self.stacked, 16 * TERMS * TERMS)


def spread_queries(eng, dst, stack, own, b, done):
    eng.tensor_tensor(
        dst.rearrange("p g (h q) -> p g h q", h=GH),
        stack[:, :, bass.ds(b * LQ, LQ)].unsqueeze(2).broadcast_to([D, TERMS, GH, LQ]),
        own[:].unsqueeze(1).unsqueeze(3).broadcast_to([D, TERMS, GH, LQ]), ALU.mult).then_inc(done, 1)


def folded_weights(ph, weights, weights_in, gate_d, bo, w_in, w_out, psum):
    nc = ph.nc
    with ExitStack() as ctx:
        sb = lambda n, s: ctx.enter_context(nc.sbuf_tensor(f"fw_{n}", s, F32))
        sem = lambda n: ph.semaphore(f"fw_{n}")
        wqT, wkT, wvT, wo = weights
        gate, tanh = sb("gate", [D, 1]), sb("tanh", [D, 1])
        gate_in, tanh_done, m_ready, m_done = map(
            sem, ("gate_in", "tanh_done", "m_ready", "m_done"))
        block = ctx.enter_context(ph.block())
        NG = 2 * H // 4

        @block.sync
        def _(sp):
            sp.dma_start(gate[:], gate_d.broadcast_to([D, 1])).then_inc(gate_in, 16)

        @block.tensor
        def _(pe):
            pe.wait_ge(weights_in, 64)
            for g in range(NG):
                left, right = (wqT, wkT) if g < NG // 2 else (wvT, wo)
                for i in range(4):
                    h = (4 * g + i) % H
                    last = nc.tensor.matmul(psum[:, g, i * D:(i + 1) * D], left[:, h, :], right[:, h, :],
                                            start=True, stop=True)
                last.then_inc(m_ready, 1)

        @block.scalar
        def _(act):
            act.wait_ge(gate_in, 16)
            nc.scalar.activation(tanh[:], gate[:], ACT.Tanh).then_inc(tanh_done, 1)

        @block.vector
        def _(dve):
            for g in range(NG // 2):
                dve.wait_ge(m_ready, g + 1)
                nc.vector.tensor_copy(w_in[:, 4 * g:4 * g + 4, :],
                                      psum[:, g, :].rearrange("p (h d) -> p h d", h=4)).then_inc(m_done, 1)
            dve.wait_ge(tanh_done, 1)
            nc.vector.tensor_scalar(bo[:], bo[:], tanh[:], None, ALU.mult).then_inc(m_done, 1)
            for g in range(NG // 2):
                dve.wait_ge(m_ready, NG // 2 + g + 1)
                nc.vector.tensor_scalar(w_out[:, 4 * g:4 * g + 4, :],
                                        psum[:, NG // 2 + g, :].rearrange("p (h d) -> p h d", h=4),
                                        tanh[:], None, ALU.mult).then_inc(m_done, 1)


class FoldedQueries:

    def __init__(self, nc, sb, sem, xnT, w_in, qx_d, psum):
        self.nc, self.xnT, self.w_in, self.qx_d, self.psum = nc, xnT, w_in, qx_d, psum
        self.stage = [sb(f"stage{i}", [D, CB, 2, H, LQ], F16) for i in range(2)]
        self.ready, self.hi_done, self.lo_done = sem("q_ready"), sem("q_hi_done"), sem("q_lo_done")
        self.stored = [sem(f"q_stored{i}") for i in range(2)]

    def bank(self, n):
        return self.psum[:, n % 8, 0:CH].rearrange("p (b q) -> p b q", b=CB)

    def store(self, sp):
        for c in range(NCH):
            sp.wait_ge(self.lo_done, H * (c + 1))
            sp.dma_start(self.qx_d[c * CB:(c + 1) * CB].rearrange("b p n -> p b n"),
                         self.stage[c % 2][:].rearrange("p b i h q -> p b (i h q)")).then_inc(self.stored[c % 2], 16)
        for i in range(2):
            sp.wait_ge(self.stored[i], 16 * (NCH // 2))

    def products(self, pe):
        for c in range(NCH):
            for h in range(H):
                n = c * H + h
                if n >= 8:
                    pe.wait_ge(self.lo_done, n - 7)
                self.nc.tensor.matmul(self.psum[:, n % 8, 0:CH], self.w_in[:, h, :],
                                      self.xnT[:, c * CH:(c + 1) * CH], start=True, stop=True).then_inc(self.ready, 1)
        pe.wait_ge(self.lo_done, NCH * H)

    def hi(self, act):
        for c in range(NCH):
            if c >= 2:
                act.wait_ge(self.stored[c % 2], 16 * (c // 2))
            for h in range(H):
                act.wait_ge(self.ready, c * H + h + 1)
                self.nc.scalar.activation(self.stage[c % 2][:, :, 0, h, :], self.bank(c * H + h),
                                          ACT.Copy).then_inc(self.hi_done, 1)

    def lo(self, dve):
        for c in range(NCH):
            for h in range(H):
                dve.wait_ge(self.hi_done, c * H + h + 1)
                self.nc.vector.tensor_tensor(self.stage[c % 2][:, :, 1, h, :], self.bank(c * H + h),
                                             self.stage[c % 2][:, :, 0, h, :], ALU.subtract).then_inc(self.lo_done, 1)


class Front:

    ITEMS = 6

    def __init__(self, nc, sb, sem, weights, bank, bv_columns, keys_by_pool):
        self.nc, self.bank, self.weights = nc, bank, weights
        self.wk, self.wv, self.bk, self.bv = sb("wk", [D, D]), sb("wv", [D, D]), sb("bk", [D, 1]), sb("bv", [D, bv_columns])
        self.ctxT = [sb(f"ctxT{i}", [D, LK]) for i in range(2)]
        self.k = [[sb(f"k{n}{i}", [D, LK], F16) for n in ("hi", "lo")] for i in range(2)]
        self.ks = [sb(f"ks{i}", [D, TERMS, LK], F16) for i in range(2)]
        self.v = [sb(f"v{i}", [KT, NT, D]) for i in range(2)]
        self.weights_in = sem("weights_in")
        self.ctxT_in = [sem(f"ctxT_in{i}") for i in range(2)]
        self.ks_in = [sem(f"ks_in{i}") for i in range(2)]
        self.whole = [sb(f"k{i}", [D, LK]) for i in range(2)] if keys_by_pool else None
        self.paired = sem("k_paired")
        self.ready, self.hi_done, self.free = sem("side_ready"), sem("khi_done"), sem("side_free")

    def load_weights(self, sp):
        wk_d, bk_d, wv_d, bv_d = self.weights
        sp.dma_start(self.wk[:], wk_d).then_inc(self.weights_in, 16)
        sp.dma_start(self.wv[:], wv_d).then_inc(self.weights_in, 16)
        sp.dma_start(self.bk[:], bk_d).then_inc(self.weights_in, 16)
        sp.dma_start(self.bv[:], bv_d.broadcast_to([D, self.bv.shape[1]])).then_inc(self.weights_in, 16)

    def stack(self, sp, k, j):
        if self.whole:
            reach(sp, self.paired, k, 6, 3 * (j + 1))
        else:
            reach(sp, self.free, k, 2 * self.ITEMS, self.ITEMS * j + 3)
        for term in range(TERMS):
            for g in range(TERMS):
                sp.dma_start(self.ks[j][32 * term:32 * term + 32, g, :],
                             self.k[j][term // 2][32 * g:32 * g + 32, :]).then_inc(self.ks_in[j], 16)

    def stacked(self, eng, k, j):
        eng.wait_ge(self.ks_in[j], (k + 1) * (16 * TERMS * TERMS))

    def product(self, pe, k, j, i):
        nc = self.nc
        if i == 0:
            pe.wait_ge(self.ctxT_in[j], (k + 1) * 16)
        reach(pe, self.free, k, 2 * self.ITEMS, self.ITEMS * j + i)
        if i < 3:
            nc.tensor.matmul(self.bank[:, 0:500], self.wk[:], self.ctxT[j][:, i * 500:(i + 1) * 500],
                             start=True, stop=True).then_inc(self.ready, 1)
        else:
            for n in range(4):
                t = 4 * (i - 3) + n
                last = nc.tensor.matmul(self.bank[0:KT, n * D:(n + 1) * D],
                                        self.ctxT[j][:, t * KT:(t + 1) * KT], self.wv[:], start=True, stop=True)
            last.then_inc(self.ready, 1)

    def key_hi(self, act, k, j, i):
        reach(act, self.ready, k, 2 * self.ITEMS, self.ITEMS * j + i + 1)
        if not (isinstance(k, int) and k == 0):
            self.stacked(act, k - 1, j)
        self.nc.scalar.activation(self.k[j][0][:, i * 500:(i + 1) * 500], self.bank[:, 0:500], ACT.Identity,
                                  bias=self.bk[:]).then_inc(self.hi_done, 1)

    def key_lo(self, dve, k, j, i):
        reach(dve, self.hi_done, k, 6, 3 * j + i + 1)
        s = slice(i * 500, (i + 1) * 500)
        self.nc.vector.scalar_tensor_tensor(self.k[j][1][:, s], self.bank[:, 0:500], self.bk[:], self.k[j][0][:, s],
                                            ALU.add, ALU.subtract).then_inc(self.free, 1)

    def whole_key(self, act, k, j, i):
        reach(act, self.ready, k, 2 * self.ITEMS, self.ITEMS * j + i + 1)
        if not (isinstance(k, int) and k == 0):
            reach(act, self.paired, k - 1, 6, 3 * (j + 1))
        self.nc.scalar.activation(self.whole[j][:, i * 500:(i + 1) * 500], self.bank[:, 0:500], ACT.Identity,
                                  bias=self.bk[:]).then_inc(self.free, 1)

    def key_pair(self, pool, k, j, i, ones):
        reach(pool, self.free, k, 2 * self.ITEMS, self.ITEMS * j + i + 1)
        if not (isinstance(k, int) and k == 0):
            self.stacked(pool, k - 1, j)
        s = slice(i * 500, (i + 1) * 500)
        whole, hi, lo = self.whole[j][:, s], self.k[j][0][:, s], self.k[j][1][:, s]
        self.nc.gpsimd.tensor_tensor(hi, whole, ones[:, 0:1].broadcast_to([D, 500]), ALU.mult).then_inc(self.hi_done, 1)
        reach(pool, self.hi_done, k, 6, 3 * j + i + 1)
        self.nc.gpsimd.tensor_tensor(lo, whole, hi, ALU.subtract).then_inc(self.paired, 1)

    def plain_value(self, act, k, j, i):
        reach(act, self.ready, k, 2 * self.ITEMS, self.ITEMS * j + i + 1)
        t = 4 * (i - 3)
        self.nc.scalar.activation(self.v[j][:, t:t + 4, :].rearrange("p t n -> p (t n)"), self.bank[0:KT, :],
                                  ACT.Copy).then_inc(self.free, 1)

    def value(self, dve, k, j, i):
        reach(dve, self.ready, k, 2 * self.ITEMS, self.ITEMS * j + i + 1)
        t = 4 * (i - 3)
        self.nc.vector.tensor_tensor(
            self.v[j][:, t:t + 4, :], self.bank[0:KT, :].rearrange("p (t n) -> p t n", t=4),
            self.bv[0:KT, :].unsqueeze(1).broadcast_to([KT, 4, D]), ALU.add).then_inc(self.free, 1)


def after(k, j):
    return (k, 1) if j == 0 else (k + 1, 0)


def query_softmax_attention(ph, name, xnT, ctxT_d, stack, attnT, query_weights, proj, scale, ident, own, heads, psum):
    nc = ph.nc
    with ExitStack() as ctx:
        sb = lambda n, s, dt=F32: ctx.enter_context(nc.sbuf_tensor(f"{name}_{n}", s, dt))
        sem = lambda n: ph.semaphore(f"{name}_{n}")
        front = Front(nc, sb, sem, proj, psum[:, 6, :], D, False)
        q = HeadQueries(nc, sb, sem, query_weights, xnT, stack, psum)
        identh = sb("ident", [KT, KT], BF16)
        qx = [sb(f"qx{i}", [D, TERMS, GQ], F16) for i in range(2)]
        ox, own_ox, attn = sb("ox", [D, H, LQ]), sb("own_ox", [D, H, LQ]), sb("attn", [D, LQ])
        p = [sb(f"p{i}", [KT, H, LQ]) for i in range(6)]
        vz = [sb(f"vz{i}", [KT, H, DH]) for i in range(4)]
        ntop = [sb(f"ntop{i}", [KT, H], BF16) for i in range(2)]
        f28 = [sb(f"f28{i}", [KT, H, 28]) for i in range(2)]
        f14 = [sb(f"f14{i}", [KT, H, 14]) for i in range(2)]
        f7 = [sb(f"f7{i}", [KT, H, 7]) for i in range(2)]
        z = [sb(f"z{i}", [KT, H]) for i in range(2)]
        rz = [sb(f"rz{i}", [KT, H]) for i in range(2)]
        (ident_done, s_ready, top_done, sub_ready, sub_done, exp_done, half_done, quarter_done, tree_done,
         z_done, rz_done, vz_done, o_ready, o_done, qx_done, own_done, picked,
         attn_done) = map(sem, (
             "ident_done", "s_ready", "top_done", "sub_ready", "sub_done", "exp_done", "half_done",
             "quarter_done", "tree_done", "z_done", "rz_done", "vz_done", "o_ready", "o_done", "qx_done",
             "own_done", "picked", "attn_done"))
        ITEM_AT = {1: 0, 3: 1, 5: 2, 7: 3, 9: 4, 11: 5}
        TOP_BANK, SUB_BANK = 0, 2
        LAG = 5
        block = ctx.enter_context(ph.block())

        @block.sync
        def _(sp):
            q.load_weights(sp)
            front.load_weights(sp)
            for j in range(2):
                sp.dma_start(front.ctxT[j][:], ctxT_d[j]).then_inc(front.ctxT_in[j], 16)
            q.stack(sp)
            front.stack(sp, 0, 0)

            def step(k):
                end = isinstance(k, int) and k == NPAIR - 1
                for j, first, last in samples(k):
                    if not last:
                        reach(sp, exp_done, k, 2 * NT, NT * j)
                        front.stack(sp, *after(k, j))
                    if not end:
                        reach(sp, front.ready, k, 12, 6 * j + 6)
                        sp.dma_start(front.ctxT[j][:], ctxT_d[2 * k + j + 2]).then_inc(front.ctxT_in[j], 16)
            over_pairs(sp, step)

        @block.tensor
        def _(pe):
            q.products(pe)
            pe.wait_ge(front.weights_in, 64)
            for i in range(6):
                front.product(pe, 0, 0, i)
            pe.wait_ge(ident_done, 1)

            def score(out, j, t, g, **flags):
                return nc.tensor.matmul(out[:, g % 2 * GQ:(g % 2 + 1) * GQ], front.ks[j][:, g, t * KT:(t + 1) * KT],
                                        qx[j][:, g, :], **flags)

            def subtract(k, s):
                s -= 1
                j, t = s // NT % 2, s % NT
                reach(pe, exp_done, k, 2 * NT, s - 1)
                for a in range(2):
                    out = psum[0:KT, SUB_BANK + a, :]
                    nc.tensor.matmul(out[:, 0:HALF], identh[:],
                                     ntop[s % 2][:, 8 * a:8 * a + 8].unsqueeze(2).broadcast_to([KT, 8, LQ]),
                                     start=True, stop=False)
                    for g in range(2):
                        last = score(out, j, t, 2 * a + g, start=False, stop=g == 1)
                last.then_inc(sub_ready, 1)

            def output(k, s):
                s -= LAG
                j, t = s // NT % 2, s % NT
                reach(pe, vz_done, k, 2 * NT, s + 1)
                if t == 0:
                    reach(pe, o_done, k, 2, s // NT)
                for a in range(2):
                    last = nc.tensor.matmul(
                        psum[:, 4 + a, 0:HALF], vz[s % 4][:].rearrange("p h d -> p (h d)"),
                        p[s % 6][:, 8 * a:8 * a + 8, :].rearrange("p h q -> p (h q)"),
                        start=t == 0, stop=t == NT - 1)
                last.then_inc(o_ready, 1)

            def step(k):
                for j, first, last_sample in samples(k):
                    for t in range(NT):
                        s = NT * j + t
                        if t == 0:
                            front.stacked(pe, k, j)
                            reach(pe, qx_done, k, 2, j + 1)
                        if t % 2:
                            reach(pe, top_done, k, 2 * NT, s)
                        else:
                            reach(pe, sub_done, k, NT, s // 2)
                        for g in range(TERMS):
                            last = score(psum[0:KT, TOP_BANK + g // 2, :], j, t, g, start=True, stop=True)
                        last.then_inc(s_ready, 1)
                        if t % 2:
                            subtract(k, s)
                        if t in ITEM_AT and not last_sample:
                            front.product(pe, *after(k, j), ITEM_AT[t])
                        if not (first and t < LAG):
                            output(k, s)
            over_pairs(pe, step)
            for s in range(LAG):
                output(NPAIR, s)

        @block.scalar
        def _(act):
            q.hi(act)
            act.wait_ge(front.weights_in, 64)
            for i in range(3):
                front.key_hi(act, 0, 0, i)

            def exponentials(k, s):
                s -= 1
                if s % 2:
                    reach(act, sub_done, k, NT, (s + 1) // 2)
                    nc.scalar.activation(p[s % 6][:], p[s % 6][:], ACT.Exp, scale=scale).then_inc(exp_done, 1)
                else:
                    reach(act, sub_ready, k, NT, s // 2 + 1)
                    reach(act, o_ready, k, 2 * NT, s - 5)
                    nc.scalar.activation(p[s % 6][:].rearrange("p (a h) q -> p a (h q)", a=2),
                                         psum[0:KT, SUB_BANK:SUB_BANK + 2, 0:HALF], ACT.Exp,
                                         scale=scale).then_inc(exp_done, 1)

            def leave(k, j):
                reach(act, o_ready, k, 2 * NT, NT * j)
                reach(act, own_done, k, 2, j - 1)
                nc.scalar.activation(ox[:].rearrange("p (a h) q -> p a (h q)", a=2), psum[:, 4:6, 0:HALF],
                                     ACT.Copy).then_inc(o_done, 1)

            def step(k):
                for j, first, last_sample in samples(k):
                    for t in range(NT):
                        if not (first and t < 1):
                            exponentials(k, NT * j + t)
                        if t == LAG - 1 and not first:
                            leave(k, j)
                        if t in ITEM_AT and ITEM_AT[t] < 3 and not last_sample:
                            front.key_hi(act, *after(k, j), ITEM_AT[t])
            over_pairs(act, step)
            exponentials(NPAIR, 0)
            leave(NPAIR, 0)

        @block.gpsimd
        def _(pool):
            def queries(k, j):
                reach(pool, sub_ready, k, NT, NT // 2 * (j - 1))
                spread_queries(nc.gpsimd, qx[j][:], stack, own, 2 * k + j, qx_done)

            def mask(k, j):
                reach(pool, o_done, k, 2, j)
                reach(pool, picked, k, 2, j - 1)
                nc.gpsimd.tensor_tensor(own_ox[:], ox[:], heads[:].unsqueeze(2).broadcast_to([D, H, LQ]),
                                        ALU.mult).then_inc(own_done, 1)

            q.wait_stacked(pool)
            queries(0, 0)

            def step(k):
                for j, first, last_sample in samples(k):
                    for t in range(NT):
                        if t == LAG and not first:
                            mask(k, j)
                        if t == 1 and not last_sample:
                            queries(*after(k, j))
                        s = NT * j + t
                        reach(pool, exp_done, k, 2 * NT, s + 1)
                        pt = p[s % 6]
                        nc.gpsimd.tensor_tensor(f28[s % 2][:], pt[:, :, 0:28], pt[:, :, 28:56],
                                                ALU.add).then_inc(half_done, 1)
                        reach(pool, half_done, k, 2 * NT, s + 1)
                        nc.gpsimd.tensor_tensor(f14[s % 2][:], f28[s % 2][:, :, 0:14], f28[s % 2][:, :, 14:28],
                                                ALU.add).then_inc(quarter_done, 1)
                        reach(pool, quarter_done, k, 2 * NT, s + 1)
                        reach(pool, z_done, k, 2 * NT, s - 1)
                        nc.gpsimd.tensor_tensor(f7[s % 2][:], f14[s % 2][:, :, 0:7], f14[s % 2][:, :, 7:14],
                                                ALU.add).then_inc(tree_done, 1)
            over_pairs(pool, step)
            mask(NPAIR, 0)

        @block.vector
        def _(dve):
            nc.vector.tensor_copy(identh[:], ident[0:KT, 0:KT]).then_inc(ident_done, 1)
            q.lo(dve)
            dve.wait_ge(front.weights_in, 64)
            for i in range(3):
                front.key_lo(dve, 0, 0, i)
            for i in range(3, 6):
                front.value(dve, 0, 0, i)

            def normalise(k, s):
                s -= 3
                j, t = s // NT % 2, s % NT
                reach(dve, tree_done, k, 2 * NT, s + 1)
                nc.vector.tensor_reduce(z[s % 2][:], f7[s % 2][:], AX.X, ALU.add).then_inc(z_done, 1)
                reach(dve, z_done, k, 2 * NT, s + 1)
                nc.vector.reciprocal(rz[s % 2][:], z[s % 2][:]).then_inc(rz_done, 1)
                reach(dve, rz_done, k, 2 * NT, s + 1)
                reach(dve, o_ready, k, 2 * NT, s - 3)
                nc.vector.tensor_tensor(
                    vz[s % 4][:], front.v[j][:, t, :].rearrange("p (h d) -> p h d", h=H),
                    rz[s % 2][:].unsqueeze(2).broadcast_to([KT, H, DH]), ALU.mult).then_inc(vz_done, 1)

            def attention(k, j):
                reach(dve, own_done, k, 2, j)
                reach(dve, attn_done, k, 2, j - 1)
                nc.vector.tensor_reduce(attn[:], own_ox[:].rearrange("p h q -> p q h"), AX.X,
                                        ALU.add).then_inc(picked, 1)
                reach(dve, picked, k, 2, j)
                nc.vector.tensor_copy(attnT[:, bass.ds((2 * k + j - 1) * LQ, LQ)], attn[:]).then_inc(attn_done, 1)

            def step(k):
                for j, first, last_sample in samples(k):
                    for t in range(NT):
                        s = NT * j + t
                        reach(dve, s_ready, k, 2 * NT, s + 1)
                        if t % 2 == 0:
                            reach(dve, sub_ready, k, NT, s // 2)
                        nc.vector.tensor_reduce(
                            ntop[s % 2][:].rearrange("p (a h) -> p a h", a=2),
                            psum[0:KT, TOP_BANK:TOP_BANK + 2, 0:HALF].rearrange("p a (h q) -> p a h q", h=H // 2),
                            AX.X, ALU.max, negate=True).then_inc(top_done, 1)
                        if t % 2:
                            reach(dve, top_done, k, 2 * NT, s + 1)
                            reach(dve, o_ready, k, 2 * NT, s - 5)
                            split = lambda x: x.rearrange("p (a h) q -> p a h q", a=2)
                            nc.vector.tensor_tensor(
                                split(p[s % 6][:]),
                                psum[0:KT, TOP_BANK:TOP_BANK + 2, 0:HALF].rearrange("p a (h q) -> p a h q", h=H // 2),
                                split(ntop[s % 2][:].unsqueeze(2).broadcast_to([KT, H, LQ])),
                                ALU.add).then_inc(sub_done, 1)
                        if not (first and t < 3):
                            normalise(k, s)
                        if t == LAG + 2 and not first:
                            attention(k, j)
                        if t in ITEM_AT and not last_sample:
                            item = ITEM_AT[t]
                            (front.key_lo if item < 3 else front.value)(dve, *after(k, j), item)
            over_pairs(dve, step)
            for s in range(3):
                normalise(NPAIR, s)
            attention(NPAIR, 0)


def row_pieces(r):
    pieces, at = [], 0
    while at < 128:
        row = 128 * r + at
        n = min(GQ - row % GQ, 128 - at)
        if at % 64 and n > 32:
            n = 32
        pieces.append((row // GQ, row % GQ, at, n))
        at += n
    return pieces


def key_softmax_attention(ph, name, xnT, ctxT_d, ctx_d, source, dest, query_weights, proj, scale, ident, ones, masks, psum):
    nc = ph.nc
    PARTS = ((0, 2), (2, 3))
    LIFT = 12 * math.log(2.0)
    with ExitStack() as ctx:
        sb = lambda n, s, dt=F32: ctx.enter_context(nc.sbuf_tensor(f"{name}_{n}", s, dt))
        sem = lambda n: ph.semaphore(f"{name}_{n}")
        p = [sb(f"p{i}", [D, LK]) for i in range(2)]
        pT = [[sb(f"pT{n}{i}", [KT, NT, D], F16) for n in ("hi", "lo")] for i in range(2)]
        vs = [[sb(f"v{n}{i}", [KT, NT, D], F16) for n in ("hi", "lo")] for i in range(2)]
        a = [sb(f"a{i}", [D, RT, D]) for i in range(2)]
        tops, zs = sb("tops", [D, 2 * RT, 3]), sb("zs", [D, 2 * RT, len(PARTS)])
        top, shift, z, rz = (sb(n, [D, 2 * RT]) for n in ("top", "shift", "z", "rz"))
        v_in = [sem(f"v_in{i}") for i in range(2)]
        t_ready, hi_done, lo_done = ([sem(f"{n}{i}") for i in range(3)] for n in ("t_ready", "hi_done", "lo_done"))
        s_ready = [sem(f"s_ready{i}") for i in range(3)]
        exp_done = [sem(f"exp_done{i}") for i in range(len(PARTS))]
        (cleared, tops_done, top_done, shift_done, z_done, rz_done, o_ready, a_done, aT_ready, aT_done,
         vhi_done, vlo_done, ctx_hi_done, ctx_lo_done) = map(sem, (
             "cleared", "tops_done", "top_done", "shift_done", "z_done", "rz_done", "o_ready", "a_done",
             "aT_ready", "aT_done", "vhi_done", "vlo_done", "ctx_hi_done", "ctx_lo_done"))
        T_BANK, O_BANK, SIDE = 3, 6, 7
        if proj:
            front = Front(nc, sb, sem, proj, psum[:, SIDE, :], 1, True)
            qx = [sb(f"qx{i}", [D, TERMS, GQ], F16) for i in range(2)]
            own, window, same_query = masks
            q = HeadQueries(nc, sb, sem, query_weights, xnT, source, psum)
            qx_done = sem("qx_done")
        else:
            front = None
            qx = [sb(f"qx{i}", [D, 2, HQ], F16) for i in range(2)]
            q = FoldedQueries(nc, sb, sem, xnT, query_weights, source, psum)
            ox = [sb(f"ox{i}", [D, HQ]) for i in range(2)]
            qx_in = [sem(f"qx_in{i}") for i in range(2)]
            ox_out = [sem(f"ox_out{i}") for i in range(2)]
            ctxT, cx = [sb(f"ctxT{i}", [D, LK]) for i in range(2)], [sb(f"cx{i}", [KT, NT, D]) for i in range(2)]
            ctxT_in = [sem(f"ctxT_in{i}") for i in range(2)]
            cT = [[sb(f"cT{n}{i}", [D, LK], F16) for n in ("hi", "lo")] for i in range(2)]
        TURN_AT = 3
        ITEM_AT = {0: 0, 1: 1, 2: 2, 4: 3, 5: 4, 6: 5} if proj else {}
        block = ctx.enter_context(ph.block())

        def cols(r):
            return slice(128 * r // LQ * DH, min(128 * r // LQ * DH + 32, D)) if proj else slice(0, D)

        @block.sync
        def _(sp):
            if proj:
                q.load_weights(sp)
                front.load_weights(sp)
                for j in range(2):
                    sp.dma_start(front.ctxT[j][:], ctxT_d[j]).then_inc(front.ctxT_in[j], 16)
                q.stack(sp)
                front.stack(sp, 0, 0)
            else:
                for j in range(2):
                    sp.dma_start(ctxT[j][:], ctxT_d[j]).then_inc(ctxT_in[j], 16)
                    sp.dma_start(cx[j][:], ctx_d[j]).then_inc(v_in[j], 16)
                q.store(sp)
                sp.dma_start(qx[0][:].rearrange("p a n -> p (a n)"), source[0]).then_inc(qx_in[0], 16)

            def store(k, j):
                reach(sp, aT_done, k, 2 * RT, RT * (j + 1))
                sp.dma_start(dest[2 * k + j], ox[j][:]).then_inc(ox_out[j], 16)

            def step(k):
                end = isinstance(k, int) and k == NPAIR - 1
                for j, first, last in samples(k):
                    jn = 1 - j
                    if not last:
                        reach(sp, s_ready[2], k, 2 * RT, RT * j)
                        if proj:
                            front.stack(sp, *after(k, j))
                        else:
                            sp.dma_start(qx[jn][:].rearrange("p a n -> p (a n)"),
                                         source[2 * k + j + 1]).then_inc(qx_in[jn], 16)
                    if not end:
                        if proj:
                            reach(sp, front.ready, k, 12, 6 * j + 6)
                            sp.dma_start(front.ctxT[j][:], ctxT_d[2 * k + j + 2]).then_inc(front.ctxT_in[j], 16)
                        else:
                            reach(sp, ctx_lo_done, k, 2, j + 1)
                            sp.dma_start(ctxT[j][:], ctxT_d[2 * k + j + 2]).then_inc(ctxT_in[j], 16)
                            reach(sp, vlo_done, k, 2, j + 1)
                            sp.dma_start(cx[j][:], ctx_d[2 * k + j + 2]).then_inc(v_in[j], 16)
                    if not proj and not first:
                        store(*((k, 0) if j else (k - 1, 1)))
            over_pairs(sp, step)
            if not proj:
                store(NPAIR - 1, 1)
                for i in range(2):
                    sp.wait_ge(ox_out[i], 16 * NPAIR)

        @block.gpsimd
        def _(pool):
            def split_values(k, j, i):
                reach(pool, front.free, k, 12, 6 * j + 4 + i)
                reach(pool, o_ready, k, 2 * RT, RT * (j - 1))
                t = slice(4 * i, 4 * i + 4)
                nc.gpsimd.tensor_tensor(vs[j][0][:, t, :], front.v[j][:, t, :],
                                        ones[0:KT, :].unsqueeze(1).broadcast_to([KT, 4, D]), ALU.mult).then_inc(vhi_done, 1)
                reach(pool, vhi_done, k, 6, 3 * j + i + 1)
                nc.gpsimd.tensor_tensor(vs[j][1][:, t, :], front.v[j][:, t, :], vs[j][0][:, t, :],
                                        ALU.subtract).then_inc(vlo_done, 1)

            def split_context(k, j):
                pool.wait_ge(ctxT_in[j], (k + 1) * 16)
                reach(pool, s_ready[2], k, 2 * RT, RT * (j - 1))
                nc.gpsimd.tensor_tensor(cT[j][0][:], ctxT[j][:], ones[:, 0:1].broadcast_to([D, LK]),
                                        ALU.mult).then_inc(ctx_hi_done, 1)
                reach(pool, ctx_hi_done, k, 2, j + 1)
                nc.gpsimd.tensor_tensor(cT[j][1][:], ctxT[j][:], cT[j][0][:], ALU.subtract).then_inc(ctx_lo_done, 1)
                pool.wait_ge(v_in[j], (k + 1) * 16)
                reach(pool, o_ready, k, 2 * RT, RT * (j - 1))
                nc.gpsimd.tensor_tensor(vs[j][0][:], cx[j][:], ones[0:KT, :].unsqueeze(1).broadcast_to([KT, NT, D]),
                                        ALU.mult).then_inc(vhi_done, 1)
                reach(pool, vhi_done, k, 2, j + 1)
                nc.gpsimd.tensor_tensor(vs[j][1][:], cx[j][:], vs[j][0][:], ALU.subtract).then_inc(vlo_done, 1)

            def queries(k, j):
                reach(pool, s_ready[2], k, 2 * RT, RT * (j - 1))
                spread_queries(nc.gpsimd, qx[j][:], source, own, 2 * k + j, qx_done)

            def step(k):
                for j, _, _ in samples(k):
                    if proj:
                        for i in range(3):
                            front.key_pair(pool, k, j, i, ones)
                        queries(k, j)
                        for i in range(3):
                            split_values(k, j, i)
                    else:
                        split_context(k, j)
            if proj:
                q.wait_stacked(pool)
            over_pairs(pool, step)

        @block.tensor
        def _(pe):
            if proj:
                q.products(pe)
                pe.wait_ge(front.weights_in, 64)
                for i in range(6):
                    front.product(pe, 0, 0, i)
            else:
                q.products(pe)

            def scores(k, j, r, s):
                for m in range(3):
                    for part, (at, to) in enumerate(PARTS):
                        if m == at:
                            reach(pe, exp_done[part], k, 2 * RT, s)
                    keys = slice(m * 500, (m + 1) * 500)
                    if proj:
                        for g, at, to, n in row_pieces(r):
                            last = nc.tensor.matmul(psum[to:to + n, m, 0:500], qx[j][:, g, at:at + n],
                                                    front.ks[j][:, g, keys], start=True, stop=True)
                    else:
                        for n, (q, c) in enumerate(((0, 0), (0, 1), (1, 0))):
                            last = nc.tensor.matmul(psum[:, m, 0:500], qx[j][:, q, r * 128:(r + 1) * 128],
                                                    cT[j][c][:, keys], start=n == 0, stop=n == 2)
                    last.then_inc(s_ready[m], 1)

            def transposes(k, s, i):
                s -= 1
                if i == 0:
                    for done in exp_done:
                        reach(pe, done, k, 2 * RT, s + 1)
                reach(pe, lo_done[i], k, 2 * RT, s)
                for m in range(4):
                    t = 4 * i + m
                    last = nc.tensor.transpose(psum[0:KT, T_BANK + i, m * D:(m + 1) * D],
                                               p[s % 2][:, t * KT:(t + 1) * KT], ident[:])
                last.then_inc(t_ready[i], 1)

            def output(k, s, i):
                s -= 2
                j, r = s // RT % 2, s % RT
                reach(pe, lo_done[i], k, 2 * RT, s + 1)
                if i == 0:
                    reach(pe, a_done, k, 2 * RT, s)
                    if r == 0:
                        n = 3 if proj else 1
                        reach(pe, vlo_done, k, 2 * n, n * (s // RT + 1))
                c = cols(r)
                for m in range(4):
                    t = 4 * i + m
                    for n, (x, y) in enumerate(((0, 0), (0, 1), (1, 0))):
                        last = nc.tensor.matmul(psum[:, O_BANK, 0:c.stop - c.start], pT[s % 2][x][:, t, :],
                                                vs[j][y][:, t, c], start=t == 0 and n == 0,
                                                stop=t == NT - 1 and n == 2)
                if i == 2:
                    last.then_inc(o_ready, 1)

            def turn_tile(k, s):
                s -= 3
                reach(pe, a_done, k, 2 * RT, s + 1)
                reach(pe, aT_done, k, 2 * RT, s)
                nc.tensor.transpose(psum[:, SIDE, 0:D], a[s // RT % 2][:, s % RT, :], ident[:]).then_inc(aT_ready, 1)

            def turn_sample(k, j, more, tiles):
                i = 1 - j
                if tiles[0] == 0:
                    reach(pe, a_done, k, 2 * RT, RT * j)
                    made = 6 + sum(r < TURN_AT for r in ITEM_AT) if more else 6 if j else 0
                    reach(pe, front.free, k, 12, 6 * j + made)
                    reach(pe, aT_done, k, 2, j - 1)
                for r in tiles:
                    last = nc.tensor.matmul(psum[:, SIDE, 0:LQ], a[i][:, r, :], same_query[:, r, :],
                                            start=r == 0, stop=r == RT - 1)
                if tiles[-1] == RT - 1:
                    last.then_inc(aT_ready, 1)

            def item(k, j, r):
                if r == TURN_AT + 1:
                    reach(pe, aT_done, k, 2, j)
                front.product(pe, *after(k, j), ITEM_AT[r])

            def rest(k, j, r, s, t_on, o_on, a_on, more, turn):
                for i in range(2):
                    if t_on:
                        transposes(k, s, i)
                if more and r in ITEM_AT:
                    item(k, j, r)
                if turn and r == TURN_AT:
                    turn_sample(k, j, more, range(4))
                for i in range(2):
                    if o_on:
                        output(k, s, i)
                if t_on:
                    transposes(k, s, 2)
                if o_on:
                    output(k, s, 2)
                if turn and r == TURN_AT:
                    turn_sample(k, j, more, range(4, RT))
                if a_on and not proj:
                    turn_tile(k, s)

            def step(k):
                for j, first, last_sample in samples(k):
                    for r in range(RT):
                        s = RT * j + r
                        if r == 0:
                            if proj:
                                reach(pe, qx_done, k, 2, j + 1)
                                front.stacked(pe, k, j)
                            else:
                                pe.wait_ge(qx_in[j], (k + 1) * 16)
                                reach(pe, ctx_lo_done, k, 2, j + 1)
                        scores(k, j, r, s)
                        rest(k, j, r, s, not (first and r < 1), not (first and r < 2), not (first and r < 3),
                             not last_sample, proj and not first)
            over_pairs(pe, step)
            for s in range(3):
                rest(NPAIR, -1, s, s, s < 1, s < 2, True, False, False)
            if proj:
                turn_sample(NPAIR, 0, False, range(RT))

        @block.scalar
        def _(act):
            if proj:
                q.hi(act)
                act.wait_ge(front.weights_in, 64)
                for i in range(3):
                    front.whole_key(act, 0, 0, i)
                for i in range(3, 6):
                    front.plain_value(act, 0, 0, i)
            else:
                q.hi(act)

            def leave(k, s):
                s -= 4
                j, r = s // RT % 2, s % RT
                reach(act, aT_ready, k, 2 * RT, s + 1)
                if r == 0:
                    reach(act, ox_out[j], k, 16, 0)
                nc.scalar.activation(ox[j][:, r * 128:(r + 1) * 128], psum[:, SIDE, 0:D],
                                     ACT.Copy).then_inc(aT_done, 1)

            def transposed(k, s, i):
                s -= 1
                reach(act, t_ready[i], k, 2 * RT, s + 1)
                reach(act, o_ready, k, 2 * RT, s - 1)
                nc.scalar.activation(pT[s % 2][0][:, 4 * i:4 * i + 4, :].rearrange("p t n -> p (t n)"),
                                     psum[0:KT, T_BANK + i, :], ACT.Copy).then_inc(hi_done[i], 1)

            def step(k):
                for j, first, last_sample in samples(k):
                    for r in range(RT):
                        s = RT * j + r
                        if not proj and not (first and r < 4):
                            leave(k, s)
                        behind = not (first and r < 1)
                        if behind:
                            transposed(k, s, 0)
                            transposed(k, s, 1)
                        reach(act, shift_done, k, 2 * RT, s + 1)
                        reach(act, t_ready[2], k, 2 * RT, s - 1)
                        for part, (at, to) in enumerate(PARTS):
                            nc.scalar.activation(
                                p[s % 2][:].rearrange("p (a n) -> p a n", a=3)[:, at:to, :], psum[:, at:to, 0:500],
                                ACT.Exp, bias=shift[:, s:s + 1], scale=scale,
                                accum_out=zs[:, s, part:part + 1]).then_inc(exp_done[part], 1)
                        if r in ITEM_AT and not last_sample:
                            item = ITEM_AT[r]
                            (front.whole_key if item < 3 else front.plain_value)(act, *after(k, j), item)
                        if behind:
                            transposed(k, s, 2)
            over_pairs(act, step)
            for s in range(4):
                if not proj:
                    leave(NPAIR, s)
                if s == 0:
                    for i in range(3):
                        transposed(NPAIR, 0, i)

        @block.vector
        def _(dve):
            for x in (tops, zs, top, shift, z, rz, *a):
                nc.vector.memset(x[:], 0.0).then_inc(cleared, 1)
            dve.wait_ge(cleared, 8)
            if proj:
                q.lo(dve)
                dve.wait_ge(front.weights_in, 64)
            else:
                q.lo(dve)

            def leave_lo(k, s, i):
                s -= 2 if i == 2 else 1
                reach(dve, hi_done[i], k, 2 * RT, s + 1)
                reach(dve, o_ready, k, 2 * RT, s - 1)
                t = slice(4 * i, 4 * i + 4)
                nc.vector.tensor_tensor(
                    pT[s % 2][1][:, t, :], psum[0:KT, T_BANK + i, :].rearrange("p (t n) -> p t n", t=4),
                    pT[s % 2][0][:, t, :], ALU.subtract).then_inc(lo_done[i], 1)

            def sums(k, s):
                c = (s - 1) % (2 * RT)
                for done in exp_done:
                    reach(dve, done, k, 2 * RT, s)
                nc.vector.tensor_reduce(z[:, c:c + 1], zs[:, c, :], AX.X, ALU.add).then_inc(z_done, 1)

            def invert(k, s):
                c = (s - 1) % (2 * RT)
                reach(dve, z_done, k, 2 * RT, s)
                nc.vector.reciprocal(rz[:, c:c + 1], z[:, c:c + 1]).then_inc(rz_done, 1)

            def attention(k, s):
                s -= 3
                r, c = s % RT, cols(s % RT)
                n = s % (2 * RT)
                reach(dve, o_ready, k, 2 * RT, s + 1)
                reach(dve, rz_done, k, 2 * RT, s + 1)
                if not proj:
                    reach(dve, aT_ready, k, 2 * RT, s - RT + 1)
                elif r == 0:
                    reach(dve, aT_ready, k, 2, s // RT - 1)
                got = psum[:, O_BANK, 0:c.stop - c.start]
                if proj:
                    nc.vector.scalar_tensor_tensor(a[s // RT % 2][:, r, c], got, rz[:, n:n + 1], window[:, r, 0:c.stop - c.start],
                                                   ALU.mult, ALU.mult).then_inc(a_done, 1)
                else:
                    nc.vector.tensor_scalar(a[s // RT % 2][:, r, :], got, rz[:, n:n + 1], None, ALU.mult).then_inc(a_done, 1)

            def turned(k, j):
                reach(dve, aT_ready, k, 2, j)
                nc.vector.tensor_scalar(dest[:, bass.ds((2 * k + j - 1) * LQ, LQ)], psum[:, SIDE, 0:LQ],
                                        front.bv[:], None, ALU.add).then_inc(aT_done, 1)

            def step(k):
                for j, first, last_sample in samples(k):
                    for r in range(RT):
                        s = RT * j + r
                        c = slice(s, s + 1)
                        if proj and r == TURN_AT + 1 and not first:
                            turned(k, j)
                        if not (first and r < 3):
                            attention(k, s)
                        for m in range(3):
                            reach(dve, s_ready[m], k, 2 * RT, s + 1)
                            nc.vector.tensor_reduce(tops[:, s, m:m + 1], psum[:, m, 0:500], AX.X,
                                                    ALU.max).then_inc(tops_done, 1)
                        behind = not (first and r < 1)
                        if behind:
                            sums(k, s)
                        reach(dve, tops_done, k, 6 * RT, 3 * (s + 1))
                        nc.vector.tensor_reduce(top[:, c], tops[:, s, :], AX.X, ALU.max).then_inc(top_done, 1)
                        if behind:
                            invert(k, s)
                        reach(dve, top_done, k, 2 * RT, s + 1)
                        nc.vector.tensor_scalar(shift[:, c], top[:, c], -scale, LIFT,
                                                ALU.mult, ALU.add).then_inc(shift_done, 1)
                        if not (first and r < 2):
                            leave_lo(k, s, 2)
                        if behind:
                            leave_lo(k, s, 0)
                            leave_lo(k, s, 1)
            over_pairs(dve, step)
            sums(NPAIR, 0)
            invert(NPAIR, 0)
            for s in range(3):
                attention(NPAIR, s)
                if s < 2:
                    leave_lo(NPAIR, s, 2)
                if s == 0:
                    leave_lo(NPAIR, 0, 0)
                    leave_lo(NPAIR, 0, 1)
            if proj:
                turned(NPAIR, 0)


def output_projection(ph, name, xT, ox_d, w_out, bo, psum):
    nc = ph.nc
    with ExitStack() as ctx:
        ox = [ctx.enter_context(nc.sbuf_tensor(f"{name}_ox{i}", [D, CB, HQ], F32)) for i in range(2)]
        sem = lambda n: ph.semaphore(f"{name}_{n}")
        ox_in = [sem(f"ox_in{i}") for i in range(2)]
        y_ready, x_done = sem("y_ready"), sem("x_done")
        block = ctx.enter_context(ph.block())

        @block.sync
        def _(sp):
            for c in range(NCH):
                if c >= 2:
                    sp.wait_ge(y_ready, c - 1)
                sp.dma_start(ox[c % 2][:], ox_d[c * CB:(c + 1) * CB].rearrange("b p n -> p b n")).then_inc(ox_in[c % 2], 16)

        @block.tensor
        def _(pe):
            for c in range(NCH):
                pe.wait_ge(ox_in[c % 2], 16 * (c // 2 + 1))
                for h in range(H):
                    last = nc.tensor.matmul(psum[:, c, 0:CH], w_out[:, h, :], ox[c % 2][:, :, h * LQ:(h + 1) * LQ],
                                            start=h == 0, stop=h == H - 1)
                last.then_inc(y_ready, 1)

        @block.vector
        def _(dve):
            for c in range(NCH):
                dve.wait_ge(y_ready, c + 1)
                x = xT[:, c * CH:(c + 1) * CH]
                nc.vector.scalar_tensor_tensor(x, psum[:, c, 0:CH], bo[:], x, ALU.add, ALU.add).then_inc(x_done, 1)


def head_projection(ph, name, xT, attnT, wo_d, bo, psum):
    nc = ph.nc
    with ExitStack() as ctx:
        wo = ctx.enter_context(nc.sbuf_tensor(f"{name}_wo", [D, D], F32))
        wo_in, y_ready, x_done = (ph.semaphore(f"{name}_{n}") for n in ("wo_in", "y_ready", "x_done"))
        block = ctx.enter_context(ph.block())

        @block.sync
        def _(sp):
            sp.dma_start(wo[:], wo_d).then_inc(wo_in, 16)

        @block.tensor
        def _(pe):
            pe.wait_ge(wo_in, 16)
            for c in range(NCH):
                nc.tensor.matmul(psum[:, c, 0:CH], wo[:], attnT[:, c * CH:(c + 1) * CH],
                                 start=True, stop=True).then_inc(y_ready, 1)

        @block.vector
        def _(dve):
            for c in range(NCH):
                dve.wait_ge(y_ready, c + 1)
                x = xT[:, c * CH:(c + 1) * CH]
                nc.vector.scalar_tensor_tensor(x, psum[:, c, 0:CH], bo[:], x, ALU.add, ALU.add).then_inc(x_done, 1)


def router(ph, name, xnT, gate_d, gate_bias_d, select_bias_d, norm_eps, iota, comb, psum):
    nc = ph.nc
    with ExitStack() as ctx:
        sb = lambda n, s, dt=F32: ctx.enter_context(nc.sbuf_tensor(f"{name}_{n}", s, dt))
        sem = lambda n: ph.semaphore(f"{name}_{n}")
        gate, bias = sb("gate", [D, E]), sb("bias", [D, 1, E])
        logit, prob, sel = (sb(n, [RTOK, NR, E]) for n in ("logit", "prob", "sel"))
        best, index, indexf = sb("best", [RTOK, NR, 8]), sb("index", [RTOK, NR, 8], U32), sb("indexf", [RTOK, NR, 8])
        first, second = sb("first", [RTOK, NR, E]), sb("second", [RTOK, NR, E])
        one = sb("one", [RTOK, NR])
        weights_in, logit_ready, exp_ready, exp_done, step_done, best_done, index_done = map(
            sem, ("weights_in", "logit_ready", "exp_ready", "exp_done", "step_done", "best_done", "index_done"))
        block = ctx.enter_context(ph.block())
        bias_d = gate_bias_d if gate_bias_d is not None else select_bias_d

        def wide(a):
            return a.unsqueeze(2).broadcast_to([RTOK, NR, E])

        @block.sync
        def _(sp):
            sp.dma_start(gate[:], gate_d).then_inc(weights_in, 16)
            if bias_d is not None:
                sp.dma_start(bias[:, 0, :], bias_d.broadcast_to([D, E])).then_inc(weights_in, 16)

        @block.tensor
        def _(pe):
            pe.wait_ge(weights_in, 32 if bias_d is not None else 16)
            for i in range(NR):
                last = nc.tensor.matmul(psum[0:RTOK, 0, i * E:(i + 1) * E], xnT[:, i * RTOK:(i + 1) * RTOK],
                                        gate[:], start=True, stop=True)
            last.then_inc(logit_ready, 1)

        @block.scalar
        def _(act):
            act.wait_ge(exp_ready, 1)
            nc.scalar.activation(prob[:], logit[:], ACT.Exp).then_inc(exp_done, 1)

        @block.vector
        def _(dve):
            done = 0

            def then(ins):
                nonlocal done
                done += 1
                ins.then_inc(step_done, 1)
                dve.wait_ge(step_done, done)

            dve.wait_ge(logit_ready, 1)
            wide_bias = bias[0:RTOK, :, :].broadcast_to([RTOK, NR, E])
            raw = psum[0:RTOK, 0, 0:NR * E].rearrange("p (i e) -> p i e", i=NR)
            if gate_bias_d is not None:
                then(nc.vector.tensor_tensor(logit[:], raw, wide_bias, ALU.add))
            else:
                then(nc.vector.tensor_copy(logit[:], raw))
            then(nc.vector.tensor_reduce(one[:], logit[:], AX.X, ALU.max))
            nc.vector.tensor_tensor(logit[:], logit[:], wide(one[:]), ALU.subtract).then_inc(exp_ready, 1)
            dve.wait_ge(exp_done, 1)
            then(nc.vector.tensor_reduce(one[:], prob[:], AX.X, ALU.add))
            then(nc.vector.reciprocal(one[:], one[:]))
            then(nc.vector.tensor_tensor(prob[:], prob[:], wide(one[:]), ALU.mult))
            key = prob
            if select_bias_d is not None:
                then(nc.vector.tensor_tensor(sel[:], prob[:], wide_bias, ALU.add))
                key = sel
            for i in range(NR):
                nc.vector.max(best[:, i, :], key[:, i, :]).then_inc(best_done, 1)
            for i in range(NR):
                dve.wait_ge(best_done, i + 1)
                nc.vector.max_index(index[:, i, :], best[:, i, :], key[:, i, :]).then_inc(index_done, 1)
            dve.wait_ge(index_done, NR)
            then(nc.vector.tensor_copy(indexf[:], index[:]))
            wide_iota = iota[0:RTOK, :].unsqueeze(1).broadcast_to([RTOK, NR, E])
            then(nc.vector.tensor_tensor(first[:], wide_iota, wide(indexf[:, :, 0]), ALU.is_equal))
            then(nc.vector.tensor_tensor(second[:], wide_iota, wide(indexf[:, :, 1]), ALU.is_equal))
            then(nc.vector.tensor_tensor(first[:], first[:], second[:], ALU.add))
            then(nc.vector.tensor_tensor(comb[:], first[:], prob[:], ALU.mult))
            if norm_eps is not None:
                then(nc.vector.tensor_reduce(one[:], comb[:], AX.X, ALU.add))
                then(nc.vector.tensor_scalar(one[:], one[:], norm_eps, None, ALU.add))
                then(nc.vector.reciprocal(one[:], one[:]))
                then(nc.vector.tensor_tensor(comb[:], comb[:], wide(one[:]), ALU.mult))


def experts(ph, name, xT, xnT, comb, gate_d, up_d, down_d, biases, pieces, mode, n_exp, ident, ones, psum, int_scale=None):
    NF = len(pieces)
    F = sum(n for _, n in pieces)
    PMAX = max(n for _, n in pieces)
    weighted = mode != "plain"
    NS = 2 if n_exp > 1 else 1
    nc = ph.nc
    with ExitStack() as ctx:
        sb = lambda n, s, dt=F32: ctx.enter_context(nc.sbuf_tensor(f"{name}_{n}", s, dt))
        sem = lambda n: ph.semaphore(f"{name}_{n}")
        wg = [sb(f"wg{i}", [D, F]) for i in range(NS)]
        wu = [sb(f"wu{i}", [D, F]) for i in range(NS)]
        wd = [sb(f"wd{i}", [PMAX, NF, D]) for i in range(NS)]
        wgs, wus = ([[sb(f"{n}{i}{x}", [D, F], F16) for x in ("hi", "lo")] for i in range(NS)] for n in ("wg", "wu"))
        wds = [[sb(f"wd{i}{x}", [PMAX, NF, D], F16) for x in ("hi", "lo")] for i in range(NS)]
        splits = [(wg, wgs), (wu, wus), (wd, wds)]
        hid = [sb(f"hid{i}", [PMAX, CH]) for i in range(4)]
        hids = [[sb(f"hid{i}{x}", [PMAX, NF, CH], F16) for x in ("hi", "lo")] for i in range(2)]
        NSP = 2 * len(splits)
        BEHIND = 2 if mode == "bias" else 1
        PAIRS = ((0, 0), (0, 1), (1, 0))
        act_out = [sb(f"act_out{i}", [PMAX, CH]) for i in range(2)]
        prod = [sb(f"prod{i}", [PMAX, CH]) for i in range(2)]
        y = [sb(f"y{i}", [D, CH]) for i in range(2)]
        if weighted:
            diag = [sb(f"diag{i}", [RTOK, NR, RTOK]) for i in range(2)]
            wide = [sb(f"wide{i}", [D, T]) for i in range(2)]
        NX = NS if mode == "in" else 1
        xs = sb("xs", [D, T]) if mode == "in" else xnT
        xss = [[sb(f"xs{i}{x}", [D, T], F16) for x in ("hi", "lo")] for i in range(NX)]
        if mode == "bias":
            gb, ub = ([sb(f"{n}{i}", [PMAX, NF]) for i in range(2)] for n in ("gb", "ub"))
            db = [sb(f"db{i}", [D, 1]) for i in range(2)]
        if int_scale is not None:
            raw = [sb(f"raw{i}", [D, F], I32) for i in range(2)] + [sb("raw2", [PMAX, NF, D], I32)]
        loads = (2 + (1 if all(n == PMAX for _, n in pieces) else 2)) + (3 if mode == "bias" else 0)
        w_in = [sem(f"w_in{i}") for i in range(NS)]
        (w_cast, w_clear, w_split, hi_done, lo_done, diag_done, wide_ready, wide_done, xs_done, g_ready, u_ready, act_done, mid_done, h_done,
         y_ready, y_done, x_done) = map(sem, (
             "w_cast", "w_clear", "w_split", "hi_done", "lo_done", "diag_done", "wide_ready", "wide_done", "xs_done", "g_ready", "u_ready", "act_done",
             "mid_done", "h_done", "y_ready", "y_done", "x_done"))
        G_BANK, U_BANK, Y_BANK, W_BANK = 0, 2, 4, 6
        block = ctx.enter_context(ph.block())
        UNITS = NCH * NS

        def over(eng, step):
            step(0)
            if n_exp > 2:
                with eng.Fori(1, n_exp // 2 - 1) as k:
                    step(k)
                step(n_exp // 2 - 1)

        def following(k, i):
            if isinstance(k, int) and NS * k + i == n_exp - 1:
                return None
            return (k, 1) if i == 0 else (k + 1, 0)

        @block.sync
        def _(sp):
            def load(e, i):
                sp.dma_start(wg[i][:], gate_d[:, e, :]).then_inc(w_in[i], 16)
                sp.dma_start(wu[i][:], up_d[:, e, :]).then_inc(w_in[i], 16)
                full = [n for _, n in pieces if n == PMAX]
                sp.dma_start(wd[i][:, 0:len(full), :],
                             down_d[e, 0:PMAX * len(full), :].rearrange("(f p) d -> p f d", p=PMAX)).then_inc(w_in[i], 16)
                if len(full) < NF:
                    at, n = pieces[-1]
                    sp.dma_start(wd[i][0:n, NF - 1, :], down_d[e, at:at + n, :]).then_inc(w_in[i], 16)
                if mode == "bias":
                    gb_d, ub_d, db_d = biases
                    sp.dma_start(gb[i][:], gb_d[e]).then_inc(w_in[i], 16)
                    sp.dma_start(ub[i][:], ub_d[e]).then_inc(w_in[i], 16)
                    sp.dma_start(db[i][:], db_d[e]).then_inc(w_in[i], 16)

            if int_scale is not None:
                sp.dma_start(raw[0][:], gate_d[:, 0, :]).then_inc(w_in[0], 16)
                sp.dma_start(raw[1][:], up_d[:, 0, :]).then_inc(w_in[0], 16)
                sp.dma_start(raw[2][:], down_d[0].rearrange("(f p) d -> p f d", p=PMAX)).then_inc(w_in[0], 16)
            else:
                sp.wait_ge(w_clear, NS)

                def step(k):
                    for i in range(NS):
                        if mode == "bias":
                            reach(sp, x_done, k, UNITS, NCH * (i - 1))
                        reach(sp, w_split, k, NS * NSP, NSP * (i - 1))
                        load(NS * k + i, i)
                over(sp, step)

        @block.tensor
        def _(pe):
            def weights(k, i):
                reach(pe, diag_done, k, NS, i + 1)
                for c in range(NCH):
                    reach(pe, wide_done, k, UNITS, NCH * i + c - 1)
                    nc.tensor.matmul(psum[:, W_BANK + c % 2, 0:CH], ones[0:RTOK, :],
                                     diag[i][:, 4 * c:4 * c + 4, :].rearrange("p i n -> p (i n)"),
                                     start=True, stop=True).then_inc(wide_ready, 1)

            def down(k, u, f):
                u -= 1
                i = u // NCH % NS
                n = pieces[f][1]
                reach(pe, lo_done, k, UNITS * NF, NF * u + f + 1)
                if f == 0:
                    reach(pe, y_done, k, UNITS, u - 1)
                out = psum[:, Y_BANK + u % 2, 0:CH]
                if f == 0 and u % NCH == 0:
                    reach(pe, w_split, k, NS * NSP, NSP * i + 6)
                for x, (a, b) in enumerate(PAIRS):
                    last = nc.tensor.matmul(out, wds[i][a][0:n, f, :], hids[u % 2][b][0:n, f, :],
                                            start=f == 0 and x == 0, stop=f == NF - 1 and x == 2)
                if f == NF - 1:
                    last.then_inc(y_ready, 1)

            if weighted:
                weights(0, 0)

            def step(k):
                for u in range(UNITS):
                    i, c = u // NCH, u % NCH
                    if c == 0:
                        reach(pe, w_split, k, NS * NSP, NSP * i + 4)
                        if mode == "in":
                            reach(pe, xs_done, k, 3 * NS, 3 * (i + 1))
                        elif isinstance(k, int) and k == 0:
                            pe.wait_ge(xs_done, 2)
                    if weighted and c == 2 and following(k, i):
                        weights(*following(k, i))
                    src = xss[i % NX]

                    def product(bank, w):
                        for x, (a, b) in enumerate(PAIRS):
                            last = nc.tensor.matmul(psum[0:n, bank + m % 2, 0:CH], w[i][a][:, at:at + n],
                                                    src[b][:, c * CH:(c + 1) * CH], start=x == 0, stop=x == 2)
                        return last

                    for f, (at, n) in enumerate(pieces):
                        m = NF * u + f
                        reach(pe, act_done, k, UNITS * NF, m - 1)
                        product(G_BANK, wgs).then_inc(g_ready, 1)
                        reach(pe, mid_done, k, UNITS * NF, m - 1)
                        product(U_BANK, wus).then_inc(u_ready, 1)
                        if not (isinstance(k, int) and k == 0 and u == 0):
                            down(k, u, f)
            over(pe, step)
            for f in range(NF):
                down(max(n_exp // 2, 1), 0, f)

        @block.scalar
        def _(act):
            def weights(k, i):
                for c in range(NCH):
                    reach(act, wide_ready, k, UNITS, NCH * i + c + 1)
                    if mode == "in":
                        reach(act, xs_done, k, 3 * NS, 3 * (i - 1))
                    else:
                        reach(act, y_done, k, UNITS, NCH * (i - 1))
                    nc.scalar.activation(wide[i][:, c * CH:(c + 1) * CH], psum[:, W_BANK + c % 2, 0:CH],
                                         ACT.Copy).then_inc(wide_done, 1)

            def hidden(k, m):
                m -= 1
                n = pieces[m % NF][1]
                reach(act, mid_done, k, UNITS * NF, m + 1)
                reach(act, lo_done, k, UNITS * NF, m - 3)
                nc.scalar.activation(hid[m % 4][0:n, :], prod[m % 2][0:n, :], ACT.Silu).then_inc(h_done, 1)

            def hidden_hi(k, m):
                m -= BEHIND
                u, f, n = m // NF, m % NF, pieces[m % NF][1]
                reach(act, h_done if mode == "bias" else mid_done, k, UNITS * NF, m + 1)
                reach(act, y_ready, k, UNITS, u - 1)
                nc.scalar.activation(hids[u % 2][0][0:n, f, :], hid[m % 4][0:n, :], ACT.Copy).then_inc(hi_done, 1)

            if weighted:
                weights(0, 0)

            def step(k):
                for u in range(UNITS):
                    i, c = u // NCH, u % NCH
                    if weighted and c == 2 and following(k, i):
                        weights(*following(k, i))
                    for f, (at, n) in enumerate(pieces):
                        m = NF * u + f
                        if mode == "bias":
                            reach(act, g_ready, k, UNITS * NF, m + 1)
                            if u % NCH == 0 and f == 0:
                                act.wait_ge(w_in[i], (k + 1) * 16 * loads)
                            reach(act, mid_done, k, UNITS * NF, m - 1)
                            nc.scalar.activation(act_out[m % 2][0:n, :], psum[0:n, G_BANK + m % 2, 0:CH],
                                                 ACT.Identity, bias=gb[i][0:n, f:f + 1]).then_inc(act_done, 1)
                            if not (isinstance(k, int) and k == 0 and m == 0):
                                hidden(k, m)
                        else:
                            reach(act, g_ready, k, UNITS * NF, m + 1)
                            reach(act, mid_done, k, UNITS * NF, m - 1)
                            nc.scalar.activation(act_out[m % 2][0:n, :], psum[0:n, G_BANK + m % 2, 0:CH],
                                                 ACT.Silu).then_inc(act_done, 1)
                        if not (isinstance(k, int) and k == 0 and m < BEHIND):
                            hidden_hi(k, m)
            over(act, step)
            if mode == "bias":
                hidden(n_exp // 2, 0)
            for m in range(BEHIND):
                hidden_hi(max(n_exp // 2, 1), m)

        @block.gpsimd
        def _(pool):
            def split(k, i, n):
                if n == 0:
                    if int_scale is not None:
                        pool.wait_ge(w_cast, 3)
                    else:
                        pool.wait_ge(w_in[i], (k + 1) * 16 * loads)
                    reach(pool, y_ready, k, UNITS, NCH * (i - 1))
                whole, pair = splits[n][0][i][:], splits[n][1][i]
                if n == 2:
                    whole = whole.rearrange("p f d -> p (f d)")
                    pair = [x[:].rearrange("p f d -> p (f d)") for x in pair]
                else:
                    pair = [x[:] for x in pair]
                nc.gpsimd.tensor_tensor(pair[0], whole, ones[0:whole.shape[0], 0:1].broadcast_to(whole.shape),
                                        ALU.mult).then_inc(w_split, 1)
                reach(pool, w_split, k, NS * NSP, NSP * i + 2 * n + 1)
                nc.gpsimd.tensor_tensor(pair[1], whole, pair[0], ALU.subtract).then_inc(w_split, 1)

            for n in range(len(splits)):
                split(0, 0, n)

            def step(k):
                last = isinstance(k, int) and k == max(n_exp // 2, 1) - 1
                for u in range(UNITS):
                    c = u % NCH
                    reach(pool, y_done, k, UNITS, u + 1)
                    reach(pool, x_done, k, UNITS, u)
                    x = xT[:, c * CH:(c + 1) * CH]
                    nc.gpsimd.tensor_tensor(x, x, y[u % 2][:], ALU.add).then_inc(x_done, 1)
                    if NS == 2 and c < len(splits) and not (last and u >= NCH):
                        split(k if u < NCH else k + 1, 1 - u // NCH, c)
            over(pool, step)

        @block.vector
        def _(dve):
            if int_scale is None:
                for i in range(NS):
                    nc.vector.memset(wd[i][:, NF - 1, :], 0.0).then_inc(w_clear, 1)

            def diagonals(k, i):
                reach(dve, wide_ready, k, UNITS, NCH * (i - 1))
                e = NS * k + i
                c = comb[:, :, e:e + 1] if isinstance(k, int) else comb[:, :, bass.ds(e, 1)]
                nc.vector.tensor_tensor(diag[i][:], ident[0:RTOK, 0:RTOK].unsqueeze(1).broadcast_to([RTOK, NR, RTOK]),
                                        c.broadcast_to([RTOK, NR, RTOK]), ALU.mult).then_inc(diag_done, 1)

            def inputs(k, i):
                reach(dve, wide_done, k, UNITS, NCH * (i + 1))
                reach(dve, u_ready, k, UNITS * NF, NCH * NF * (i - 1))
                nc.vector.tensor_tensor(xs[:], xnT[:], wide[i][:], ALU.mult).then_inc(xs_done, 1)
                pair(k, i, 3 * NS, 3 * i + 1)

            def pair(k, i, per, at):
                reach(dve, xs_done, k, per, at)
                nc.vector.tensor_copy(xss[i][0][:], xs[:]).then_inc(xs_done, 1)
                reach(dve, xs_done, k, per, at + 1)
                nc.vector.tensor_tensor(xss[i][1][:], xs[:], xss[i][0][:], ALU.subtract).then_inc(xs_done, 1)

            def outputs(k, u):
                u -= 1
                i, c = u // NCH % NS, u % NCH
                reach(dve, y_ready, k, UNITS, u + 1)
                reach(dve, x_done, k, UNITS, u - 1)
                out, got = y[u % 2][:], psum[:, Y_BANK + u % 2, 0:CH]
                if mode in ("in", "plain"):
                    nc.vector.tensor_copy(out, got).then_inc(y_done, 1)
                else:
                    if c == 0:
                        reach(dve, wide_done, k, UNITS, NCH * (u // NCH + 1))
                    w = wide[i][:, c * CH:(c + 1) * CH]
                    if mode == "bias":
                        nc.vector.scalar_tensor_tensor(out, got, db[i][:], w, ALU.add, ALU.mult).then_inc(y_done, 1)
                    else:
                        nc.vector.tensor_tensor(out, got, w, ALU.mult).then_inc(y_done, 1)

            def hidden_lo(k, m):
                m -= BEHIND
                u, f, n = m // NF, m % NF, pieces[m % NF][1]
                reach(dve, hi_done, k, UNITS * NF, m + 1)
                nc.vector.tensor_tensor(hids[u % 2][1][0:n, f, :], hid[m % 4][0:n, :], hids[u % 2][0][0:n, f, :],
                                        ALU.subtract).then_inc(lo_done, 1)

            if mode != "in":
                pair(0, 0, 0, 0)
            if int_scale is not None:
                dve.wait_ge(w_in[0], 48)
                for dst, src in ((wg[0], raw[0]), (wu[0], raw[1]), (wd[0], raw[2])):
                    nc.vector.tensor_scalar(dst[:], src[:], int_scale, None, ALU.mult).then_inc(w_cast, 1)

            if weighted:
                diagonals(0, 0)
            if mode == "in":
                inputs(0, 0)

            def step(k):
                for u in range(UNITS):
                    i = u // NCH
                    if weighted and u % NCH == 1 and following(k, i):
                        diagonals(*following(k, i))
                    if mode == "in" and u % NCH == 3 and following(k, i):
                        inputs(*following(k, i))
                    for f, (at, n) in enumerate(pieces):
                        m = NF * u + f
                        reach(dve, act_done, k, UNITS * NF, m + 1)
                        reach(dve, u_ready, k, UNITS * NF, m + 1)
                        up = psum[0:n, U_BANK + m % 2, 0:CH]
                        if mode == "bias":
                            if u % NCH == 0 and f == 0:
                                dve.wait_ge(w_in[i], (k + 1) * 16 * loads)
                            reach(dve, h_done, k, UNITS * NF, m - 1)
                            nc.vector.scalar_tensor_tensor(prod[m % 2][0:n, :], up, ub[i][0:n, f:f + 1],
                                                           act_out[m % 2][0:n, :], ALU.add,
                                                           ALU.mult).then_inc(mid_done, 1)
                        else:
                            reach(dve, hi_done, k, UNITS * NF, m - 3)
                            reach(dve, lo_done, k, UNITS * NF, m - 3)
                            nc.vector.tensor_tensor(hid[m % 4][0:n, :], act_out[m % 2][0:n, :], up,
                                                    ALU.mult).then_inc(mid_done, 1)
                        if not (isinstance(k, int) and k == 0 and m < BEHIND):
                            hidden_lo(k, m)
                    if not (isinstance(k, int) and k == 0 and u == 0):
                        outputs(k, u)
            over(dve, step)
            for m in range(BEHIND):
                hidden_lo(max(n_exp // 2, 1), m)
            outputs(max(n_exp // 2, 1), 0)


def build(nc, a, out):
    with ExitStack() as ctx:
        sb = lambda n, s, dt=F32: ctx.enter_context(nc.sbuf_tensor(n, s, dt))
        xT, xnT = sb("xT", [D, T]), sb("xnT", [D, T])
        ident, ones, ones_mean = sb("ident", [D, D]), sb("ones", [D, D]), sb("ones_mean", [D, D])
        heads, own, iota = sb("heads", [D, H]), sb("own", [D, GH]), sb("iota", [D, E])
        window, same_query = sb("window", [D, RT, 32]), sb("same_query", [D, RT, LQ])
        spread = sb("spread", [D, NCH, D])
        gamma, beta, bo = sb("gamma", [D, 1]), sb("beta", [D, 1]), [sb(f"bo{i}", [D, 1]) for i in range(3)]
        comb = sb("comb", [RTOK, NR, E])
        psum = ctx.enter_context(nc.psum_tensor("psum", [D, 8, 512], F32))
        qx2_d = nc.dram_tensor("qx2_scratch", (B, D, 2 * HQ), F16, kind="Internal").ap()
        ox_d = nc.dram_tensor("ox_scratch", (B, D, HQ), F32, kind="Internal").ap()
        weights_in = ctx.enter_context(nc.semaphore("fw_weights_in"))
        ph = Phases(nc)
        start_in, const_done = ph.semaphore("start_in"), ph.semaphore("const_done")
        col = lambda n: a[n].rearrange("(d o) -> d o", o=1)
        row = lambda n: a[n].rearrange("(o d) -> o d", o=1)

        with ph.block() as block:
            @block.sync
            def _(sp):
                moves = [(xT[:], a["xT"]), (ident[:], a["ident"]), (heads[:], a["heads"]),
                         (own[:], a["own"]), (window[:], a["window"]), (same_query[:], a["same_query"]), (iota[:], a["iota"]), (spread[:], a["spread"]),
                         (gamma[:], col("L2_xattn_ln_gamma")), (beta[:], col("L2_xattn_ln_beta")),
                         (bo[0][:], col("L1_xattn_bo")), (bo[1][:], col("L2_xattn_b_out")), (bo[2][:], col("L3_xattn_bo"))]
                for dst, src in moves:
                    sp.dma_start(dst, src).then_inc(start_in, 16)
                sp.wait_ge(start_in, 16 * len(moves))

            @block.vector
            def _(dve):
                nc.vector.memset(ones[:], 1.0).then_inc(const_done, 1)
                nc.vector.memset(ones_mean[:], 1.0 / D).then_inc(const_done, 1)

        norm = lambda name: layer_norm(ph, name, xT, xnT, ones_mean, spread, psum)

        norm("n0")
        sigmoid_attention(ph, xT, xnT, a["ctxT"], a["ctx"].rearrange("b (t p) d -> b p t d", p=KT),
                          a["mask"], a["L0_xattn_WqT"], col("L0_xattn_bq"), a["L0_xattn_Wk"], col("L0_xattn_bk"), ident,
                          psum)
        norm("n1")
        router(ph, "r0", xnT, a["L0_ffn_gate_wT"], None, row("L0_ffn_expert_bias"), None, iota, comb, psum)
        experts(ph, "e0", xT, xnT, comb, a["L0_ffn_w1"], a["L0_ffn_w3"], a["L0_ffn_w2"], None,
                [(0, 128), (128, 128), (256, 96)], "in", E, ident, ones, psum)

        norm("n2")
        with nc.sbuf_tensor("attnT1", [D, T], F32) as attnT:
            with nc.sbuf_tensor("stack1", [D, TERMS, T], F16) as stack:
                query_softmax_attention(ph, "a1", xnT, a["ctxT"], stack, attnT,
                                        (a["L1_xattn_Wq"], col("L1_xattn_bq")),
                                        (a["L1_xattn_Wk"], col("L1_xattn_bk"), a["L1_xattn_Wv"], row("L1_xattn_bv")),
                                        float(DH) ** -0.5, ident, own, heads, psum)
            head_projection(ph, "o1", xT, attnT, a["L1_xattn_Wo"], bo[0], psum)
        norm("n3")
        router(ph, "r1", xnT, a["L1_ffn_gate_wT"], row("L1_ffn_gate_b"), None, 1e-20, iota, comb, psum)
        experts(ph, "e1", xT, xnT, comb, a["L1_ffn_gp_wT"], a["L1_ffn_up_wT"], a["L1_ffn_down_wT"],
                (a["L1_ffn_gp_bT"], a["L1_ffn_up_bT"],
                 a["L1_ffn_down_b"].rearrange("e (d o) -> e d o", o=1)),
                [(102 * f, 102) for f in range(4)], "bias", E, ident, ones, psum)

        norm("n4")
        with nc.sbuf_tensor("w_out2", [D, H, D], F32) as w_out:
            with nc.sbuf_tensor("w_in2", [D, H, D], F32) as w_in:
                with ExitStack() as held:
                    names = ("w_qT", "w_kT", "w_vT", "w_out")
                    weights = [held.enter_context(nc.sbuf_tensor(f"fw_{n}", [64, H, D], F32)) for n in names]
                    layer_norm(ph, "n4b", xnT, xnT, ones_mean, spread, psum, (gamma[:], beta[:]),
                               [(to[:], a[f"L2_xattn_{n}"].rearrange("(h e) d -> e h d", h=H), weights_in)
                                for n, to in zip(names, weights)])
                    folded_weights(ph, weights, weights_in, a["L2_xattn_gate"].rearrange("(o d) -> o d", o=1), bo[1],
                                   w_in, w_out, psum)
                key_softmax_attention(ph, "a2", xnT, a["ctxT"], a["ctx"].rearrange("b (t p) d -> b p t d", p=KT),
                                      qx2_d, ox_d, w_in, None, 64.0 ** -0.5, ident, ones, None, psum)
            output_projection(ph, "o2", xT, ox_d, w_out, bo[1], psum)
        norm("n5")
        experts(ph, "e2", xT, xnT, None, a["L2_ffn_w_gateT"], a["L2_ffn_w_upT"], a["L2_ffn_w_downT"], None,
                [(128 * f, 128) for f in range(3)], "plain", 1, ident, ones, psum, int_scale=1.0 / 127.0)

        norm("n6")
        with nc.sbuf_tensor("attnT3", [D, T], F32) as attnT:
            with nc.sbuf_tensor("stack3", [D, TERMS, T], F16) as stack:
                key_softmax_attention(ph, "a3", xnT, a["ctxT"], None, stack, attnT,
                                      (a["L3_xattn_Wq"], col("L3_xattn_bq")),
                                      (a["L3_xattn_Wk"], col("L3_xattn_bk"), a["L3_xattn_Wv"], col("L3_xattn_bv")),
                                      float(DH) ** -0.5, ident, ones, (own, window, same_query), psum)
            head_projection(ph, "o3", xT, attnT, a["L3_xattn_Wo"], bo[2], psum)
        norm("n7")
        router(ph, "r3", xnT, a["L3_ffn_gate_wT"], None, None, 0.0, iota, comb, psum)
        experts(ph, "e3", xT, xnT, comb, a["L3_ffn_gateT"], a["L3_ffn_upT"], a["L3_ffn_down_projT"], None,
                [(128 * f, 128) for f in range(4)], "out", E, ident, ones, psum)

        out_done = ph.semaphore("out_done")
        with ph.block() as block:
            @block.sync
            def _(sp):
                sp.dma_start(out, xT[:]).then_inc(out_done, 16)
                sp.wait_ge(out_done, 16)


def kernel(**inputs):
    import numpy as np
    import concourse.bacc as bacc
    from concourse.bass_utils import run_bass_kernel_spmd

    i = {n: np.asarray(x) for n, x in inputs.items()}
    a = {
        "xT": i["x"].reshape(T, D).T, "ctx": i["ctx_1024"], "ctxT": i["ctx_1024"].transpose(0, 2, 1),
        "mask": i["mask_BxS2_ik1"].reshape(B, NT, KT).transpose(2, 0, 1),
        "ident": np.eye(D, dtype=np.float32),
        "heads": np.repeat(np.eye(H, dtype=np.float32), D // H, axis=0),
        "own": np.tile(np.repeat(np.eye(GH, dtype=np.float32), DH, axis=0), (TERMS, 1)),
        "window": np.stack([(np.arange(128 * r, 128 * r + 128)[:, None] // LQ - 128 * r // LQ
                             == np.arange(32) // DH).astype(np.float32) for r in range(RT)], axis=1),
        "same_query": np.stack([(np.arange(128 * r, 128 * r + 128)[:, None] % LQ == np.arange(LQ)).astype(np.float32)
                                for r in range(RT)], axis=1),
        "spread": np.tile((np.arange(D)[:, None] == 32 * np.arange(NCH)).astype(np.float32)[:, :, None], (1, 1, D)),
        "iota": np.tile(np.arange(E, dtype=np.float32), (D, 1)),
        "L0_xattn_WqT": i["L0_xattn_Wq"].T, "L0_ffn_gate_wT": i["L0_ffn_gate_w"].T,
        "L0_ffn_w1": i["L0_ffn_w1"].transpose(1, 0, 2), "L0_ffn_w3": i["L0_ffn_w3"].transpose(1, 0, 2),
        "L0_ffn_w2": i["L0_ffn_w2"],
        "L1_ffn_gate_wT": i["L1_ffn_gate_w"].T,
        "L1_ffn_gp_wT": i["L1_ffn_gp_w"].transpose(2, 0, 1), "L1_ffn_up_wT": i["L1_ffn_up_w"].transpose(2, 0, 1),
        "L1_ffn_down_wT": i["L1_ffn_down_w"].transpose(0, 2, 1),
        "L1_ffn_gp_bT": i["L1_ffn_gp_b"].reshape(E, 4, 102).transpose(0, 2, 1),
        "L1_ffn_up_bT": i["L1_ffn_up_b"].reshape(E, 4, 102).transpose(0, 2, 1),
        "L2_xattn_w_qT": i["L2_xattn_w_q"].T, "L2_xattn_w_kT": i["L2_xattn_w_kv"][:, :1024].T,
        "L2_xattn_w_vT": i["L2_xattn_w_kv"][:, 1024:].T,
        "L2_ffn_w_gateT": i["L2_ffn_w_gate"].T[:, None], "L2_ffn_w_upT": i["L2_ffn_w_up"].T[:, None],
        "L2_ffn_w_downT": i["L2_ffn_w_down"].T[None],
        "L3_ffn_gate_wT": i["L3_ffn_gate_w"].T,
        "L3_ffn_gateT": i["L3_ffn_gate_up_proj"][:, :512].transpose(2, 0, 1),
        "L3_ffn_upT": i["L3_ffn_gate_up_proj"][:, 512:].transpose(2, 0, 1),
        "L3_ffn_down_projT": i["L3_ffn_down_proj"].transpose(0, 2, 1),
    }
    for n in ("L0_xattn_bq", "L0_xattn_Wk", "L0_xattn_bk", "L0_ffn_expert_bias", "L1_xattn_Wq", "L1_xattn_bq",
              "L1_xattn_Wk", "L1_xattn_bk", "L1_xattn_Wv", "L1_xattn_bv", "L1_xattn_Wo", "L1_xattn_bo",
              "L1_ffn_gate_b", "L1_ffn_down_b", "L2_xattn_ln_gamma",
              "L2_xattn_ln_beta", "L2_xattn_w_out", "L2_xattn_b_out", "L2_xattn_gate", "L3_xattn_Wq", "L3_xattn_bq",
              "L3_xattn_Wk", "L3_xattn_bk", "L3_xattn_Wv", "L3_xattn_bv", "L3_xattn_Wo", "L3_xattn_bo"):
        a[n] = i[n]
    nc = bacc.Bacc("TRN2", target_bir_lowering=False, num_devices=1)
    arrays, aps = {}, {}
    for n, x in a.items():
        arrays[f"in_{n}"] = np.ascontiguousarray(x)
        aps[n] = nc.dram_tensor(f"in_{n}", x.shape, mybir.dt.from_np(x.dtype), kind="ExternalInput").ap()
    out = nc.dram_tensor("out_xT", (D, T), F32, kind="ExternalOutput").ap()
    build(nc, aps, out)
    r = run_bass_kernel_spmd(nc, [arrays], core_ids=[0])
    return np.ascontiguousarray(r.results[0]["out_xT"].T).reshape(B, LQ, D)
```
